# Optimizing a Trainium2 kernel written in Bass

```python
import numpy as np
import jax
import jax.numpy as jnp

def _softmax(x, axis=-1):
    return jax.nn.softmax(x, axis=axis)

def _gelu(x):
    return jax.nn.gelu(x, approximate=True)

def _silu(x):
    return jax.nn.silu(x)

def _sigmoid(x):
    return jax.nn.sigmoid(x)

def _layernorm(x, axis=-1, eps=1e-05):
    m = jnp.mean(x, axis=axis, keepdims=True)
    v = jnp.var(x, axis=axis, keepdims=True)
    return (x - m) / jnp.sqrt(v + eps)

def _scatter_add(tgt, idx, src, axis=0):
    return tgt.at[idx].add(src)

def _segment_sum(src, seg, n):
    return jax.ops.segment_sum(src, seg, n)
kernel_name = 'mk_seq_postln_d2_jaxref_r8_dca8ab'

def setup_inputs(seed: int=0):
    np.random.seed(seed)
    _w = jnp.asarray

    def _L0_attn_setup():
        import jax, jax.numpy as jnp
        import numpy as np
        D_MODEL = 128
        D_INNER = 256
        DT_RANK = 64
        D_STATE = 16
        D_CONV = 4
        B, L = (2, 128)

        def _causal_depthwise_conv(xc, conv_w, conv_b):
            b, d, l = xc.shape
            K = conv_w.shape[-1]
            xp = jnp.pad(xc, ((0, 0), (0, 0), (K - 1, 0)))
            out = jnp.zeros_like(xc)
            for k in range(K):
                out = out + conv_w[:, 0, k][None, :, None] * xp[:, :, k:k + l]
            return out + conv_b[None, :, None]

        def _selective_scan(u, delta, A, Bm, Cm, Dv):
            deltaA = jnp.exp(jnp.einsum('bld,dn->bldn', delta, A))
            deltaB_u = jnp.einsum('bld,bln,bld->bldn', delta, Bm, u)
            b, l, d, n = deltaA.shape

            def step(h, inputs):
                dA_t, dBu_t, C_t = inputs
                h = dA_t * h + dBu_t
                y = jnp.einsum('bdn,bn->bd', h, C_t)
                return (h, y)
            h0 = jnp.zeros((b, d, n), dtype=u.dtype)
            xs = (jnp.swapaxes(deltaA, 0, 1), jnp.swapaxes(deltaB_u, 0, 1), jnp.swapaxes(Cm, 0, 1))
            _, ys = jax.lax.scan(step, h0, xs)
            y = jnp.swapaxes(ys, 0, 1)
            return y + u * Dv[None, None, :]
        key = jax.random.key(seed)
        ks = jax.random.split(key, 10)
        s = lambda fan_in: 1.0 / np.sqrt(fan_in)
        inp = {'x': jax.random.normal(ks[0], (B, L, D_MODEL), dtype=jnp.float32), 'in_proj_w': jax.random.uniform(ks[1], (2 * D_INNER, D_MODEL), jnp.float32, -s(D_MODEL), s(D_MODEL)), 'conv_w': jax.random.uniform(ks[2], (D_INNER, 1, D_CONV), jnp.float32, -s(D_CONV), s(D_CONV)), 'conv_b': jax.random.uniform(ks[3], (D_INNER,), jnp.float32, -s(D_CONV), s(D_CONV)), 'x_proj_w': jax.random.uniform(ks[4], (DT_RANK + 2 * D_STATE, D_INNER), jnp.float32, -s(D_INNER), s(D_INNER)), 'dt_proj_w': jax.random.uniform(ks[5], (D_INNER, DT_RANK), jnp.float32, -s(DT_RANK), s(DT_RANK)), 'dt_proj_b': jax.random.uniform(ks[6], (D_INNER,), jnp.float32, -s(DT_RANK), s(DT_RANK)), 'A_log': jnp.log(jnp.broadcast_to(jnp.arange(1, D_STATE + 1, dtype=jnp.float32), (D_INNER, D_STATE))), 'Dp': jnp.ones((D_INNER,), dtype=jnp.float32), 'out_proj_w': jax.random.uniform(ks[7], (D_MODEL, D_INNER), jnp.float32, -s(D_INNER), s(D_INNER))}
        return inp
    _L0_attn_in = _L0_attn_setup()

    def _L0_ffn_setup():
        import jax, jax.numpy as jnp
        import numpy as np
        FP8_MAX = 448.0
        SCALE = 1.0
        _FP8_DTYPE = getattr(jnp, 'float8_e4m3fn', jnp.float16)

        def quantize_e4m3(t, scale):
            return jnp.clip(t / scale, -FP8_MAX, FP8_MAX).astype(_FP8_DTYPE)
        key = jax.random.key(seed)
        kx, kw = jax.random.split(key)
        B, N, C, F = (8, 512, 128, 128)
        x = jax.random.normal(kx, (B, N, C), dtype=jnp.float32)
        weight = jax.random.normal(kw, (F, C), dtype=jnp.float32) * 0.02
        bias = jnp.zeros((F,), dtype=jnp.float32)
        return {'x': x, 'weight': weight, 'bias': bias}
    _L0_ffn_in = _L0_ffn_setup()

    def _L1_attn_setup():
        import jax, jax.numpy as jnp
        import numpy as np
        D_MODEL = 128
        STATE = 16
        key = jax.random.key(seed)
        ks = jax.random.split(key, 7)
        x = jax.random.normal(ks[0], (4, 512, D_MODEL), dtype=jnp.float32)
        A_log = jax.random.normal(ks[1], (STATE,), dtype=jnp.float32)
        B = jax.random.normal(ks[2], (STATE, D_MODEL), dtype=jnp.float32) * 0.05
        C = jax.random.normal(ks[3], (D_MODEL, STATE), dtype=jnp.float32) * 0.05
        D = jax.random.normal(ks[4], (D_MODEL,), dtype=jnp.float32)
        W_delta = jax.random.normal(ks[5], (D_MODEL, D_MODEL), dtype=jnp.float32) * 0.02
        b_delta = jax.random.normal(ks[6], (D_MODEL,), dtype=jnp.float32) * 0.02
        return {'x': x, 'A_log': A_log, 'B': B, 'C': C, 'D': D, 'W_delta': W_delta, 'b_delta': b_delta}
    _L1_attn_in = _L1_attn_setup()

    def _L1_ffn_setup():
        import jax, jax.numpy as jnp
        import numpy as np
        TOP_K = 2
        CAPACITY = 512
        EPS = 1e-06
        W_SCALE = 0.02

        def _rms(x, w):
            return x * jax.lax.rsqrt(jnp.mean(x * x, axis=-1, keepdims=True) + EPS) * w
        key = jax.random.key(seed)
        ks = jax.random.split(key, 8)
        B, S, H, F, E = (8, 512, 128, 256, 8)
        F4 = F // 4
        return {'hidden_states': jax.random.normal(ks[0], (B, S, H), jnp.float32), 'Wr': jax.random.normal(ks[1], (H, E), jnp.float32) * W_SCALE, 'norm_w': jnp.ones((E, H), jnp.float32), 'Wg': jax.random.normal(ks[2], (E, H, F), jnp.float32) * W_SCALE, 'Wu': jax.random.normal(ks[3], (E, H, F), jnp.float32) * W_SCALE, 'Wd': jax.random.normal(ks[4], (E, F, H), jnp.float32) * W_SCALE, 'f_norm': jnp.ones((H,), jnp.float32), 'fWg': jax.random.normal(ks[5], (H, F4), jnp.float32) * W_SCALE, 'fWu': jax.random.normal(ks[6], (H, F4), jnp.float32) * W_SCALE, 'fWd': jax.random.normal(ks[7], (F4, H), jnp.float32) * W_SCALE}
    _L1_ffn_in = _L1_ffn_setup()
    _d = {'L0_attn_x': _L0_attn_in['x'], 'L0_attn_in_proj_w': _L0_attn_in['in_proj_w'], 'L0_attn_conv_w': _L0_attn_in['conv_w'], 'L0_attn_conv_b': _L0_attn_in['conv_b'], 'L0_attn_x_proj_w': _L0_attn_in['x_proj_w'], 'L0_attn_dt_proj_w': _L0_attn_in['dt_proj_w'], 'L0_attn_dt_proj_b': _L0_attn_in['dt_proj_b'], 'L0_attn_A_log': _L0_attn_in['A_log'], 'L0_attn_Dp': _L0_attn_in['Dp'], 'L0_attn_out_proj_w': _L0_attn_in['out_proj_w'], 'L0_ffn_weight': _L0_ffn_in['weight'], 'L0_ffn_bias': _L0_ffn_in['bias'], 'L1_attn_A_log': _L1_attn_in['A_log'], 'L1_attn_B': _L1_attn_in['B'], 'L1_attn_C': _L1_attn_in['C'], 'L1_attn_D': _L1_attn_in['D'], 'L1_attn_W_delta': _L1_attn_in['W_delta'], 'L1_attn_b_delta': _L1_attn_in['b_delta'], 'L1_ffn_Wr': _L1_ffn_in['Wr'], 'L1_ffn_norm_w': _L1_ffn_in['norm_w'], 'L1_ffn_Wg': _L1_ffn_in['Wg'], 'L1_ffn_Wu': _L1_ffn_in['Wu'], 'L1_ffn_Wd': _L1_ffn_in['Wd'], 'L1_ffn_f_norm': _L1_ffn_in['f_norm'], 'L1_ffn_fWg': _L1_ffn_in['fWg'], 'L1_ffn_fWu': _L1_ffn_in['fWu'], 'L1_ffn_fWd': _L1_ffn_in['fWd']}
    _x0 = _d['L0_attn_x']
    _d['L0_attn_x'] = jax.random.normal(jax.random.fold_in(jax.random.key(seed), 1), (2, 1024, 128), dtype=_x0.dtype)
    del _x0
    return _d

def reference(L0_attn_x, L0_attn_in_proj_w, L0_attn_conv_w, L0_attn_conv_b, L0_attn_x_proj_w, L0_attn_dt_proj_w, L0_attn_dt_proj_b, L0_attn_A_log, L0_attn_Dp, L0_attn_out_proj_w, L0_ffn_weight, L0_ffn_bias, L1_attn_A_log, L1_attn_B, L1_attn_C, L1_attn_D, L1_attn_W_delta, L1_attn_b_delta, L1_ffn_Wr, L1_ffn_norm_w, L1_ffn_Wg, L1_ffn_Wu, L1_ffn_Wd, L1_ffn_f_norm, L1_ffn_fWg, L1_ffn_fWu, L1_ffn_fWd):

    def _L0_attn_ref(x, in_proj_w, conv_w, conv_b, x_proj_w, dt_proj_w, dt_proj_b, A_log, Dp, out_proj_w):
        import jax, jax.numpy as jnp
        import numpy as np
        D_MODEL = 128
        D_INNER = 256
        DT_RANK = 64
        D_STATE = 16
        D_CONV = 4
        B, L = (2, 128)

        def _causal_depthwise_conv(xc, conv_w, conv_b):
            b, d, l = xc.shape
            K = conv_w.shape[-1]
            xp = jnp.pad(xc, ((0, 0), (0, 0), (K - 1, 0)))
            out = jnp.zeros_like(xc)
            for k in range(K):
                out = out + conv_w[:, 0, k][None, :, None] * xp[:, :, k:k + l]
            return out + conv_b[None, :, None]

        def _selective_scan(u, delta, A, Bm, Cm, Dv):
            deltaA = jnp.exp(jnp.einsum('bld,dn->bldn', delta, A))
            deltaB_u = jnp.einsum('bld,bln,bld->bldn', delta, Bm, u)
            b, l, d, n = deltaA.shape

            def step(h, inputs):
                dA_t, dBu_t, C_t = inputs
                h = dA_t * h + dBu_t
                y = jnp.einsum('bdn,bn->bd', h, C_t)
                return (h, y)
            h0 = jnp.zeros((b, d, n), dtype=u.dtype)
            xs = (jnp.swapaxes(deltaA, 0, 1), jnp.swapaxes(deltaB_u, 0, 1), jnp.swapaxes(Cm, 0, 1))
            _, ys = jax.lax.scan(step, h0, xs)
            y = jnp.swapaxes(ys, 0, 1)
            return y + u * Dv[None, None, :]
        b, l, _ = x.shape
        x_and_res = x @ in_proj_w.T
        xi, res = jnp.split(x_and_res, [D_INNER], axis=-1)
        xc = jnp.swapaxes(xi, 1, 2)
        xc = _causal_depthwise_conv(xc, conv_w, conv_b)
        xi = jax.nn.silu(jnp.swapaxes(xc, 1, 2))
        A = -jnp.exp(A_log)
        x_dbl = xi @ x_proj_w.T
        dt, Bm, Cm = jnp.split(x_dbl, [DT_RANK, DT_RANK + D_STATE], axis=-1)
        delta = jax.nn.softplus(dt @ dt_proj_w.T + dt_proj_b)
        y = _selective_scan(xi, delta, A, Bm, Cm, Dp)
        y = y * jax.nn.silu(res)
        return y @ out_proj_w.T

    def _L0_ffn_ref(x, weight, bias):
        import jax, jax.numpy as jnp
        import numpy as np
        FP8_MAX = 448.0
        SCALE = 1.0
        _FP8_DTYPE = getattr(jnp, 'float8_e4m3fn', jnp.float16)

        def quantize_e4m3(t, scale):
            return jnp.clip(t / scale, -FP8_MAX, FP8_MAX).astype(_FP8_DTYPE)
        B, N, C = x.shape
        x2d = x.reshape(B * N, C)
        x_mat = quantize_e4m3(x2d, SCALE).astype(jnp.float16)
        w_mat = quantize_e4m3(weight, SCALE).astype(jnp.float16)
        out2d = (x_mat @ w_mat.T).astype(jnp.float32) * (SCALE * SCALE)
        out2d = out2d + bias
        return out2d.reshape(B, N, -1)

    def _L1_attn_ref(x, A_log, B, C, D, W_delta, b_delta):
        import jax, jax.numpy as jnp
        import numpy as np
        D_MODEL = 128
        STATE = 16
        delta = jax.nn.softplus(jnp.einsum('bld,ed->ble', x, W_delta) + b_delta).mean(-1)
        A = -jnp.exp(A_log)
        Bx = jnp.einsum('bld,nd->bln', x, B)
        dA = jnp.exp(delta[..., None] * A)
        dBx = delta[..., None] * Bx

        def step(h, inp):
            dA_t, dBx_t = inp
            h = dA_t * h + dBx_t
            return (h, h)
        h0 = jnp.zeros((x.shape[0], A_log.shape[0]), dtype=x.dtype)
        _, hs = jax.lax.scan(step, h0, (jnp.swapaxes(dA, 0, 1), jnp.swapaxes(dBx, 0, 1)))
        hs = jnp.swapaxes(hs, 0, 1)
        y = jnp.einsum('bln,dn->bld', hs, C) + D * x
        return y

    def _L1_ffn_ref(hidden_states, Wr, norm_w, Wg, Wu, Wd, f_norm, fWg, fWu, fWd):
        import jax, jax.numpy as jnp
        import numpy as np
        TOP_K = 2
        CAPACITY = 512
        EPS = 1e-06
        W_SCALE = 0.02

        def _rms(x, w):
            return x * jax.lax.rsqrt(jnp.mean(x * x, axis=-1, keepdims=True) + EPS) * w
        B, S, H = hidden_states.shape
        E = Wr.shape[1]
        N = B * S
        x = hidden_states.reshape(N, H)
        probs = jax.nn.softmax(x @ Wr, axis=-1)
        w_topk, e_topk = jax.lax.top_k(probs, TOP_K)
        e_flat = e_topk.reshape(-1)
        oh = jax.nn.one_hot(e_flat, E, dtype=jnp.int32)
        pos = jnp.take_along_axis(jnp.cumsum(oh, axis=0) - 1, e_flat[:, None], axis=1)[:, 0]
        keep = pos < CAPACITY
        x_rep = jnp.repeat(x, TOP_K, axis=0)
        buf = jnp.zeros((E, CAPACITY, H), x.dtype).at[e_flat, pos].set(x_rep, mode='drop')
        h = _rms(buf, norm_w[:, None, :])
        gate = jax.nn.gelu(jnp.einsum('ech,ehf->ecf', h, Wg), approximate=False)
        up = jnp.einsum('ech,ehf->ecf', h, Wu)
        buf_out = jnp.einsum('ecf,efh->ech', gate * up, Wd) + buf
        exp_out = buf_out[e_flat, jnp.minimum(pos, CAPACITY - 1)]
        contrib = w_topk.reshape(-1)[:, None] * exp_out * keep[:, None].astype(x.dtype)
        combined = x + contrib.reshape(N, TOP_K, H).sum(axis=1)
        overflow = (~keep).reshape(N, TOP_K).any(axis=1)
        fh = _rms(x, f_norm)
        fout = jax.nn.gelu(fh @ fWg, approximate=False) * (fh @ fWu) @ fWd + x
        out = jnp.where(overflow[:, None], fout, combined)
        return out.reshape(B, S, H)
    x = L0_attn_x
    x = _layernorm(x + _L0_attn_ref(x, L0_attn_in_proj_w, L0_attn_conv_w, L0_attn_conv_b, L0_attn_x_proj_w, L0_attn_dt_proj_w, L0_attn_dt_proj_b, L0_attn_A_log, L0_attn_Dp, L0_attn_out_proj_w), axis=-1)
    x = _layernorm(x + _L0_ffn_ref(x, L0_ffn_weight, L0_ffn_bias), axis=-1)
    x = _layernorm(x + _L1_attn_ref(x, L1_attn_A_log, L1_attn_B, L1_attn_C, L1_attn_D, L1_attn_W_delta, L1_attn_b_delta), axis=-1)
    x = _layernorm(x + _L1_ffn_ref(x, L1_ffn_Wr, L1_ffn_norm_w, L1_ffn_Wg, L1_ffn_Wu, L1_ffn_Wd, L1_ffn_f_norm, L1_ffn_fWg, L1_ffn_fWu, L1_ffn_fWd), axis=-1)
    return x

_drawn_inputs = setup_inputs


def setup_inputs(seed=0):
    import zlib

    import numpy as np

    out = dict(_drawn_inputs(seed))
    spreads = {'L0_attn_Dp': (1.0, 0.6),
     'L0_ffn_bias': (0.0, 0.1),
     'L1_ffn_norm_w': (1.0, 0.6),
     'L1_ffn_f_norm': (1.0, 0.6)}
    factors = {'L0_attn_x_proj_w': 8.0,
     'L0_attn_dt_proj_w': 8.0,
     'L0_attn_dt_proj_b': 8.0,
     'L0_attn_A_log': 8.0,
     'L1_attn_W_delta': 8.0,
     'L1_attn_b_delta': 64.0,
     'L1_ffn_Wr': 8.0,
     'L1_ffn_Wg': 8.0,
     'L1_ffn_Wu': 8.0,
     'L1_ffn_Wd': 8.0,
     'L1_ffn_fWg': 8.0,
     'L1_ffn_fWu': 8.0,
     'L1_ffn_fWd': 8.0}
    for name, (base, spread) in spreads.items():
        noise = np.random.default_rng([zlib.crc32(name.encode()), seed]).standard_normal(out[name].shape)
        drawn = base * np.exp(spread * noise) if base else spread * noise
        out[name] = jnp.asarray(drawn.astype(out[name].dtype))
    for name, factor in factors.items():
        out[name] = (out[name] * factor).astype(out[name].dtype)
    return out
```

```python
from contextlib import ExitStack

import concourse.bass as bass
from concourse import mybir

F32 = mybir.dt.float32
F16 = mybir.dt.float16
BF16 = mybir.dt.bfloat16
F8 = mybir.dt.float8e4
U32 = mybir.dt.uint32
ALU = mybir.AluOpType
ACT = mybir.ActivationFunctionType
AX = mybir.AxisListType

P = 128
BATCH, LENGTH = 2, 1024
TOKENS = BATCH * LENGTH
CHUNK = 512
BLOCKS = CHUNK // P
CHUNKS = TOKENS // CHUNK
PER_BATCH = LENGTH // CHUNK
HALVES = 2
INNER = HALVES * P
STATE = 16
RANK = 64
TAPS = 4
EXPERTS = 8
HIDDEN = 256
SIDE = 64
CAPACITY = 512
LN_EPS = 1e-5
RMS_EPS = 1e-6
RING = 3
STEPS = CHUNKS * STATE

PARAMS = {
    "ident": P, "conv_w": HALVES * TAPS, "conv_b": HALVES, "dt_b": HALVES, "a_log": HALVES * STATE,
    "skip": HALVES, "in_x": HALVES * P, "in_res": INNER, "x_proj": HALVES * 96, "dt_proj": INNER,
    "out_proj": HALVES * P, "ffn_w": P, "ffn_b": P, "l1_b": STATE, "l1_c": P, "l1_d": 1, "l1_delta": P,
    "l1_delta_b": 1, "l1_a_log": 1, "router": EXPERTS, "norm_w": EXPERTS, "f_norm": 1,
    "side_g": SIDE, "side_u": SIDE, "side_d": P, "before": P, "index": EXPERTS,
}
AT, _n = {}, 0
for _k, _w in PARAMS.items():
    AT[_k] = (_n, _w)
    _n += _w
PARAM_COLS = _n
FIRST_COLS = AT["out_proj"][0]


class Marks:

    def __init__(self, sem, names):
        self.sem, self.names = sem, names.split()
        assert len(set(self.names)) == len(self.names)

    def done(self, c, name):
        return c * len(self.names) + self.names.index(name) + 1


def build(nc, x_t, params, w_gate, w_up, w_down, out):
    with ExitStack() as ctx:
        def sb(name, shape, dt=F32):
            return ctx.enter_context(nc.sbuf_tensor(name, shape, dt))

        def bank(name):
            return ctx.enter_context(nc.psum_tensor(name, [P, 512], F32))

        def sem(name):
            return ctx.enter_context(nc.semaphore(name))

        par = sb("par", [P, PARAM_COLS])

        def par_of(name):
            a, w = AT[name]
            return par[:, a:a + w]

        ident = par_of("ident")
        conv_w, conv_b, dt_b = par_of("conv_w"), par_of("conv_b"), par_of("dt_b")
        skip = par_of("skip")
        in_x = par_of("in_x").rearrange("p (h m) -> p h m", h=HALVES)
        in_res = par_of("in_res")
        x_proj = par_of("x_proj").rearrange("p (h m) -> p h m", h=HALVES)
        dt_proj = par_of("dt_proj")
        out_proj = par_of("out_proj").rearrange("p (h m) -> p h m", h=HALVES)
        x_in = sb("x_in", [P, BATCH, TAPS - 1 + LENGTH])
        wg = sb("wg", [P, EXPERTS, HIDDEN])
        wu = sb("wu", [P, EXPERTS, HIDDEN])
        wd = sb("wd", [P, EXPERTS, 2, P])
        conv_proj = sb("conv_proj", [P, HALVES, TAPS, P])
        skip_diag = sb("skip_diag", [P, HALVES, P])
        b_stack = sb("b_stack", [P, HALVES, 96])
        parts_of = sb("parts_of", [96, STATE])
        select = sb("select", [96, STATE, P], BF16)
        decay_rate = sb("decay_rate", [P, HALVES, STATE])
        l1_rate = sb("l1_rate", [STATE, 1])
        l1_diag = sb("l1_diag", [P, P])
        mean_w = sb("mean_w", [P, STATE])
        ffn_small = sb("ffn_small", [P, P], F8)
        ffn_half = sb("ffn_half", [P, P], F8)
        ffn_t = sb("ffn_t", [P, P])
        ffn_t2 = sb("ffn_t2", [P, P])
        ffn_t3 = sb("ffn_t3", [P, P])
        ffn_big = sb("ffn_big", [P, P])
        ffn_q = sb("ffn_q", [P, P], F16)
        before = sb("before", [P, P], BF16)
        ones = sb("ones", [P, P], BF16)
        minus_half = sb("minus_half", [P, BLOCKS])
        side_g = sb("side_g", [P, SIDE])
        side_u = sb("side_u", [P, SIDE])

        u = sb("u", [P, HALVES, CHUNK])
        res_gate = sb("res_gate", [P, 2, BLOCKS, INNER])
        dt_low = sb("dt_low", [RANK, CHUNK])
        b_all = sb("b_all", [96, CHUNK])
        b_left = sb("b_left", [96, CHUNK])
        b_cut = sb("b_cut", [96, CHUNK], BF16)
        b_cut2 = sb("b_cut2", [96, CHUNK], BF16)
        b_parts = sb("b_parts", [96, 2, CHUNK], BF16)
        c_rows = sb("c_rows", [P, 2, BLOCKS, STATE])
        sp_abs = sb("sp_abs", [P, HALVES, CHUNK])
        sp_exp = sb("sp_exp", [P, HALVES, CHUNK])
        sp_ln = sp_abs
        sp_relu = sb("sp_relu", [P, HALVES, CHUNK])
        delta = sb("delta", [P, 2, HALVES, CHUNK])
        du = sb("du", [P, 2, HALVES, CHUNK])
        y = sb("y", [P, 2, BLOCKS, INNER])
        b_row = sb("b_row", [P, RING, CHUNK])
        decay = sb("decay", [P, RING, HALVES, CHUNK])
        drive = sb("drive", [P, RING, HALVES, CHUNK])
        state = sb("state", [P, 2, HALVES, CHUNK])
        carry = sb("carry", [P, HALVES, STATE])
        yg_t = sb("yg_t", [P, HALVES, CHUNK])
        stats = sb("stats", [P, BLOCKS, 6])
        moments = sb("moments", [P, BLOCKS, 2])
        var_eps = sb("var_eps", [P, BLOCKS])
        rstd = sb("rstd", [P, BLOCKS])
        shift = sb("shift", [P, BLOCKS])
        x1 = sb("x1", [P, BLOCKS, P])
        x1_bias = sb("x1_bias", [P, BLOCKS, P])
        x1_q = sb("x1_q", [P, CHUNK], F8)
        ffn_out = sb("ffn_out", [P, BLOCKS, P], F16)
        r2 = x2 = x1_bias
        x2_t = sb("x2_t", [P, CHUNK])
        l1_abs = sb("l1_abs", [P, CHUNK])
        l1_exp = sb("l1_exp", [P, CHUNK])
        l1_ln = l1_abs
        l1_relu = sb("l1_relu", [P, CHUNK])
        l1_sp = l1_t = sb("l1_sp", [P, CHUNK])
        l1_step = sb("l1_step", [STATE, CHUNK])
        l1_decay = sb("l1_decay", [STATE, CHUNK])
        l1_drive = sb("l1_drive", [STATE, CHUNK])
        l1_state = sb("l1_state", [STATE, 2, CHUNK])
        mean_sq = sb("mean_sq", [P, BLOCKS])
        rms = sb("rms", [P, BLOCKS])
        rms_inv = sb("rms_inv", [P, BLOCKS])
        scale3 = sb("scale3", [P, BLOCKS])
        shift3 = sb("shift3", [P, BLOCKS])
        x3 = sb("x3", [P, BLOCKS, P])
        hn = sb("hn", [P, BLOCKS, P])
        hn_t = sb("hn_t", [P, CHUNK])
        logits = sb("logits", [P, BLOCKS, EXPERTS])
        top = sb("top", [P, BLOCKS])
        centred = sb("centred", [P, BLOCKS, EXPERTS])
        exps = sb("exps", [P, BLOCKS, EXPERTS])
        total = sb("total", [P, BLOCKS])
        total_inv = sb("total_inv", [P, BLOCKS])
        probs = sb("probs", [P, BLOCKS, EXPERTS])
        sorted8 = sb("sorted8", [P, BLOCKS, 8])
        where8 = sb("where8", [P, BLOCKS, 8], U32)
        where_f = sb("where_f", [P, BLOCKS, 8])
        pick1 = sb("pick1", [P, BLOCKS, EXPERTS])
        pick2 = sb("pick2", [P, BLOCKS, EXPERTS])
        picked = sb("picked", [P, BLOCKS, EXPERTS], BF16)
        picked_new = sb("picked_new", [P, EXPERTS])
        picked_sum = sb("picked_sum", [P, EXPERTS])
        picked_before = sb("picked_before", [P, EXPERTS], BF16)
        late = sb("late", [P, BLOCKS, EXPERTS])
        overflow = sb("overflow", [P, BLOCKS])
        kept = sb("kept", [P, BLOCKS])
        weight0 = sb("weight0", [P, BLOCKS, EXPERTS])
        weight = sb("weight", [P, BLOCKS, EXPERTS])
        weight_sum = sb("weight_sum", [P, BLOCKS])
        x_weight = sb("x_weight", [P, BLOCKS])
        acc = sb("acc", [P, BLOCKS, P])
        gelu = sb("gelu", [P, 2, CHUNK])
        hidden = sb("hidden", [P, 2, 2, CHUNK])
        conv_diag = hidden[:, 0, :, :].rearrange("p h (k d) -> p h k d", k=TAPS)
        result = sb("result", [P, 2, BLOCKS, P])

        ps_pre = bank("ps_pre")
        ps_b = bank("ps_b")
        ps_h = [bank("ps_h0"), bank("ps_h1")]
        ps_g = bank("ps_g")
        ps_u = [bank("ps_u0"), bank("ps_u1")]
        ps_d = bank("ps_d")

        loaded_first = sem("loaded_first")
        loaded_x = sem("loaded_x")
        loaded_rest = sem("loaded_rest")
        loaded_experts = sem("loaded_experts")
        stored = [sem(f"stored{i}") for i in range(2)]
        pool_const = sem("pool_const")
        setup_dve = Marks(sem("setup_dve"), "diag skip_diag b_stack b_parts two three select rate ones clip small_a clip_half half_a "
                          "big small mask diff mix cast before l1_diag gate up side_g side_u zero")
        setup_act = Marks(sem("setup_act"), "a_exp l1_exp conv0 conv1")
        setup_pe = Marks(sem("setup_pe"), "conv0 conv1")
        pre_pe = Marks(sem("pre_pe"), "conv0 conv1 res0 res1 low bstack crows dt0 dt1 skip0 skip1")
        pre_act = Marks(sem("pre_act"), "u0 u1 gate0 gate1 low ball crows abs0 relu0 abs1 relu1 exp0 exp1 ln0 ln1 y0 y1")
        pre_dve = Marks(sem("pre_dve"), "cut1 left1 cut2 left2 part3 t0 a0 b0 t1 a1 b1 delta0 delta1 du0 du1")
        row_pe = sem("row_pe")
        row_act = sem("row_act")
        decay_act = sem("decay_act")
        drive_pool = sem("drive_pool")
        state_dve = sem("state_dve")
        carry_dve = sem("carry_dve")
        turned_pe = sem("turned_pe")
        y_dve = sem("y_dve")
        tail_pe = Marks(sem("tail_pe"), "yg0 yg1 r1 x1t ffn x2t dlt bx mean r3 hnt logits counts")
        tail_act = Marks(sem("tail_act"), "yg0 yg1 x1 x1q ffn x2 x2t abs relu exp ln step decay x3 hn hnt exps acc")
        tail_dve = Marks(sem("tail_dve"), "yg st1 mo1 sh1 r2 st2 mo2 sh2 t a b sp drive scan st3 mo3 vr msq sh3 inv s3 "
                         "f3 lg top cen tot tinv probs sort where wf p1 p2 picked late over kept w0 w wsum wone red psum pbef")
        tail_pool = Marks(sem("tail_pool"), "v1 rstd1 bias v2 rstd2 v3 rstd3 v4 rms")
        moe_pe = Marks(sem("moe_pe"), " ".join(f"g{e}a u{e}a g{e}b u{e}b d{e}" for e in range(EXPERTS)) + " gs us ds")
        moe_act = Marks(sem("moe_act"), " ".join(f"g{e}a g{e}b" for e in range(EXPERTS)) + " gs")
        moe_dve = Marks(sem("moe_dve"), " ".join(f"h{e}a h{e}b acc{e}" for e in range(EXPERTS)) + " hs accs st mo sh")
        moe_pool = Marks(sem("moe_pool"), "v rstd")
        result_act = sem("result_act")

        def after(eng, marks, c, name):
            eng.wait_ge(marks.sem, marks.done(c, name))

        def tokens(c):
            return c // PER_BATCH, c % PER_BATCH * CHUNK

        def block_of(ap, j):
            return ap[:, j * P:(j + 1) * P]

        def blocks_of(ap):
            return ap.rearrange("p (j d) -> p j d", j=BLOCKS)

        def order():
            parts = [("pre", 0, k) for k in range(PRE_PARTS)]
            for c in range(CHUNKS):
                for n in range(STATE):
                    parts.append(("step", c, n))
                    if c:
                        parts += [("tail", c - 1, k) for k in TAIL_SLOT.get(n, ())]
                        parts += [("expert", c - 1, e) for e in EXPERT_SLOT.get(n, ())]
                    if c + 1 < CHUNKS:
                        parts += [("pre", c + 1, k) for k in PRE_SLOT.get(n, ())]
            parts += [("flush", CHUNKS - 1, 0)]
            c = CHUNKS - 1
            parts += [("tail", c, k) for k in range(TAIL_PARTS)]
            parts += [("expert", c, e) for e in range(EXPERTS + 2)]
            return parts

        PRE_PARTS, TAIL_PARTS = 7, 9
        TAIL_SLOT = {1: [0], 2: [1], 3: [2], 4: [3], 5: [4], 6: [5], 7: [6], 8: [7], 9: [8]}
        EXPERT_SLOT = {10: [0], 11: [1, 2], 12: [3, 4], 13: [5, 6], 14: [7, 8], 15: [9]}
        PRE_SLOT = {3: [0], 5: [1], 7: [2], 9: [3], 11: [4], 13: [5], 14: [6]}

        def run(**parts):
            for kind, c, k in order():
                if kind in parts:
                    parts[kind](c, k)

        block = ctx.enter_context(nc.Block())

        @block.sync
        def _(sp):
            sp.dma_start(par[:, 0:FIRST_COLS], params[:, 0:FIRST_COLS]).then_inc(loaded_first, 16)
            for c in range(CHUNKS):
                b, t0 = tokens(c)
                sp.dma_start(x_in[:, b, TAPS - 1 + t0:TAPS - 1 + t0 + CHUNK],
                             x_t[:, c * CHUNK:(c + 1) * CHUNK]).then_inc(loaded_x, 16)
                if c == 0:
                    sp.dma_start(par[:, FIRST_COLS:], params[:, FIRST_COLS:]).then_inc(loaded_rest, 16)
            sp.dma_start(wg[:], w_gate).then_inc(loaded_experts, 16)
            sp.dma_start(wu[:], w_up).then_inc(loaded_experts, 16)
            sp.dma_start(wd[:], w_down).then_inc(loaded_experts, 16)
            for c in range(CHUNKS):
                sp.wait_ge(result_act, c + 1)
                sp.dma_start(out[c * CHUNK:(c + 1) * CHUNK, :].rearrange("(j t) d -> t j d", j=BLOCKS),
                             result[:, c % 2]).then_inc(stored[c % 2], 16)
            for s in stored:
                sp.wait_ge(s, 16 * CHUNKS // 2)

        @block.tensor
        def _(pe):
            mm, turn = nc.tensor.matmul, nc.tensor.transpose

            def setup():
                after(pe, setup_dve, 0, "diag")
                for h in range(HALVES):
                    for k in range(TAPS):
                        last = mm(block_of(ps_h[h][:, :], k), in_x[:, h, :], conv_diag[:, h, k, :], start=True, stop=True)
                    last.then_inc(setup_pe.sem, 1)

            def pre(c, k):
                q = c % 2
                b, t0 = tokens(c)
                if k == 0:
                    if c == 0:
                        after(pe, setup_act, 0, "conv1")
                        after(pe, setup_dve, 0, "zero")
                    pe.wait_ge(loaded_x, 64 if c else 64)
                    if c:
                        after(pe, pre_act, c - 1, "y1")
                    for h in range(HALVES):
                        if h:
                            after(pe, pre_act, c, "u0")
                        for tap in range(TAPS):
                            last = mm(ps_pre[:, :], conv_proj[:, h, tap, :], x_in[:, b, t0 + tap:t0 + tap + CHUNK],
                                      start=(tap == 0), stop=(tap == TAPS - 1))
                        last.then_inc(pre_pe.sem, 1)
                if k == 1:
                    for g in range(2):
                        after(pe, pre_act, c, ("u1", "gate0")[g])
                        for i in range(2):
                            t = TAPS - 1 + t0 + (2 * g + i) * P
                            last = mm(ps_pre[:, i * INNER:(i + 1) * INNER], x_in[:, b, t:t + P], in_res,
                                      start=True, stop=True)
                        last.then_inc(pre_pe.sem, 1)
                if k == 2:
                    after(pe, pre_act, c, "gate1")
                    for h in range(HALVES):
                        last = mm(ps_pre[0:RANK, :], x_proj[:, h, 0:RANK], u[:, h, :], start=(h == 0), stop=(h == 1))
                    last.then_inc(pre_pe.sem, 1)
                    after(pe, pre_act, c, "low")
                    if c == 0:
                        after(pe, setup_dve, 0, "select")
                    for h in range(HALVES):
                        last = mm(ps_pre[0:96, :], b_stack[:, h, :], u[:, h, :], start=(h == 0), stop=(h == 1))
                    last.then_inc(pre_pe.sem, 1)
                if k == 3:
                    after(pe, pre_act, c, "ball")
                    for j in range(BLOCKS):
                        for h in range(HALVES):
                            last = mm(ps_pre[:, j * STATE:(j + 1) * STATE], u[:, h, j * P:(j + 1) * P],
                                      x_proj[:, h, RANK + STATE:RANK + 2 * STATE], start=(h == 0), stop=(h == 1))
                    last.then_inc(pre_pe.sem, 1)
                if k == 4:
                    for h in range(HALVES):
                        after(pe, pre_act, c, ("crows", "relu0")[h])
                        mm(ps_pre[:, :], dt_proj[0:RANK, h * P:(h + 1) * P], dt_low[:, :],
                           start=True, stop=True).then_inc(pre_pe.sem, 1)
                if k == 5:
                    for g in range(2):
                        after(pe, pre_act, c, ("relu1", "y0")[g])
                        for i in range(2):
                            j = 2 * g + i
                            for h in range(HALVES):
                                last = mm(ps_pre[:, i * INNER + h * P:i * INNER + (h + 1) * P],
                                          u[:, h, j * P:(j + 1) * P], skip_diag[:, h, :], start=True, stop=True)
                        last.then_inc(pre_pe.sem, 1)

            def row(g):
                c, n = divmod(g, STATE)
                if n == 0:
                    after(pe, pre_dve, c, "part3")
                if g:
                    pe.wait_ge(row_act, g)
                mm(ps_b[:, :], select[:, n, :], b_parts[:, c % 2, :], start=True, stop=True).then_inc(row_pe, 1)

            def step(c, n):
                g = c * STATE + n
                if g == 0:
                    row(0)
                if g + 1 < STEPS:
                    row(g + 1)
                pe.wait_ge(state_dve, 2 * g + 2)
                for i in range(2):
                    if g:
                        pe.wait_ge(y_dve, 2 * (g - 1) + i + 1)
                    elif i == 0:
                        after(pe, setup_act, 0, "conv1")
                    for jj in range(2):
                        for h in range(HALVES):
                            last = turn(ps_h[i][:, jj * INNER + h * P:jj * INNER + (h + 1) * P],
                                        state[:, g % 2, h, (2 * i + jj) * P:(2 * i + jj + 1) * P], ident)
                    last.then_inc(turned_pe, 1)

            def tail(c, k):
                q = c % 2
                b, t0 = tokens(c)
                if k == 0:
                    after(pe, tail_dve, c, "yg")
                    if c:
                        after(pe, moe_dve, c - 1, "accs")
                    for h in range(HALVES):
                        for j in range(BLOCKS):
                            last = turn(block_of((ps_g, ps_u[0])[h][:, :], j), y[:, q, j, h * P:(h + 1) * P], ident)
                        last.then_inc(tail_pe.sem, 1)
                if k == 1:
                    after(pe, tail_act, c, "yg1")
                    for j in range(BLOCKS):
                        t = TAPS - 1 + t0 + j * P
                        mm(block_of(ps_u[1][:, :], j), x_in[:, b, t:t + P], ident, start=True, stop=False)
                        for h in range(HALVES):
                            last = mm(block_of(ps_u[1][:, :], j), yg_t[:, h, j * P:(j + 1) * P], out_proj[:, h, :],
                                      start=False, stop=(h == 1))
                    last.then_inc(tail_pe.sem, 1)
                if k == 2:
                    after(pe, tail_act, c, "x1")
                    for j in range(BLOCKS):
                        last = turn(block_of(ps_d[:, :], j), x1[:, j, :], ident)
                    last.then_inc(tail_pe.sem, 1)
                    after(pe, tail_act, c, "x1q")
                    for j in range(BLOCKS):
                        last = mm(block_of(ps_u[0][:, :], j), x1_q[:, j * P:(j + 1) * P], ffn_q[:, :], start=True, stop=True)
                    last.then_inc(tail_pe.sem, 1)
                if k == 4:
                    after(pe, tail_act, c, "x2")
                    for j in range(BLOCKS):
                        last = turn(block_of(ps_g[:, :], j), x2[:, j, :], ident)
                    last.then_inc(tail_pe.sem, 1)
                    after(pe, tail_act, c, "x2t")
                    mm(ps_u[0][:, :], par_of("l1_delta"), x2_t[:, :], start=True, stop=True).then_inc(tail_pe.sem, 1)
                    mm(ps_u[1][0:STATE, :], par_of("l1_b"), x2_t[:, :], start=True, stop=True).then_inc(tail_pe.sem, 1)
                if k == 5:
                    after(pe, tail_dve, c, "sp")
                    mm(ps_d[0:STATE, :], mean_w[:, :], l1_sp[:, :], start=True, stop=True).then_inc(tail_pe.sem, 1)
                    after(pe, tail_dve, c, "scan")
                    for j in range(BLOCKS):
                        mm(block_of(ps_g[:, :], j), x2_t[:, j * P:(j + 1) * P], l1_diag[:, :], start=True, stop=False)
                        last = mm(block_of(ps_g[:, :], j), l1_state[:, q, j * P:(j + 1) * P],
                                  par_of("l1_c")[0:STATE, :], start=False, stop=True)
                    last.then_inc(tail_pe.sem, 1)
                if k == 6:
                    after(pe, tail_act, c, "hn")
                    for j in range(BLOCKS):
                        last = turn(block_of(ps_u[0][:, :], j), hn[:, j, :], ident)
                    last.then_inc(tail_pe.sem, 1)
                if k == 7:
                    after(pe, tail_act, c, "hnt")
                    for j in range(BLOCKS):
                        last = mm(ps_d[:, j * EXPERTS:(j + 1) * EXPERTS], hn_t[:, j * P:(j + 1) * P],
                                  par_of("router"), start=True, stop=True)
                    last.then_inc(tail_pe.sem, 1)
                if k == 8:
                    after(pe, tail_dve, c, "picked")
                    for j in range(BLOCKS):
                        o = ps_u[1][:, j * EXPERTS:(j + 1) * EXPERTS]
                        mm(o, before[:, :], picked[:, j, :], start=True, stop=False)
                        for i in range(j):
                            mm(o, ones[:, :], picked[:, i, :], start=False, stop=False)
                        last = mm(o, ones[:, :], picked_before[:, :], start=False, stop=True)
                    last.then_inc(tail_pe.sem, 1)

            def expert(c, e):
                side = e == EXPERTS
                if e > EXPERTS:
                    return
                q = e % 2
                if not side:
                    for f in range(2):
                        if e == 0 and f == 0:
                            after(pe, setup_dve, 0, "side_u")
                            after(pe, tail_act, c, "hnt")
                            after(pe, tail_act, c, "hn")
                        elif f == 0:
                            after(pe, moe_act, c, f"g{e - 1}b")
                        else:
                            after(pe, moe_act, c, f"g{e}a")
                        mm(ps_g[:, :], wg[:, e, f * P:(f + 1) * P], hn_t[:, :], start=True, stop=True).then_inc(moe_pe.sem, 1)
                        if e:
                            after(pe, moe_dve, c, f"h{e - 1}{'ab'[f]}")
                        else:
                            after(pe, tail_dve, c, "late")
                        mm(ps_u[f][:, :], wu[:, e, f * P:(f + 1) * P], hn_t[:, :], start=True, stop=True).then_inc(moe_pe.sem, 1)
                    after(pe, moe_dve, c, f"acc{e - 1}" if e else "h0b")
                    after(pe, moe_dve, c, f"h{e}b")
                    for j in range(BLOCKS):
                        for f in range(2):
                            last = mm(block_of(ps_d[:, :], j), hidden[:, q, f, j * P:(j + 1) * P], wd[:, e, f, :],
                                      start=(f == 0), stop=(f == 1))
                    last.then_inc(moe_pe.sem, 1)
                else:
                    after(pe, moe_act, c, f"g{e - 1}b")
                    mm(ps_g[0:SIDE, :], side_g[:, :], hn_t[:, :], start=True, stop=True).then_inc(moe_pe.sem, 1)
                    after(pe, moe_dve, c, f"h{e - 1}a")
                    mm(ps_u[0][0:SIDE, :], side_u[:, :], hn_t[:, :], start=True, stop=True).then_inc(moe_pe.sem, 1)
                    after(pe, moe_dve, c, f"acc{e - 1}")
                    after(pe, moe_dve, c, "hs")
                    for j in range(BLOCKS):
                        last = mm(block_of(ps_d[:, :], j), hidden[0:SIDE, q, 0, j * P:(j + 1) * P],
                                  par_of("side_d")[0:SIDE, :], start=True, stop=True)
                    last.then_inc(moe_pe.sem, 1)

            setup()
            run(pre=pre, step=step, tail=tail, expert=expert)

        @block.scalar
        def _(act):
            def do(marks, out_, in_, func, **kw):
                nc.scalar.activation(out_, in_, func, **kw).then_inc(marks.sem, 1)

            def copy(marks, out_, in_, **kw):
                nc.scalar.copy(out_, in_, **kw).then_inc(marks.sem, 1)

            def setup():
                act.wait_ge(loaded_first, 16)
                do(setup_act, decay_rate[:, :, :], par_of("a_log").rearrange("p (h n) -> p h n", h=HALVES), ACT.Exp)
                act.wait_ge(loaded_rest, 16)
                do(setup_act, l1_rate[:, :], par_of("l1_a_log")[0:STATE, :], ACT.Exp)
                for h in range(HALVES):
                    after(act, setup_pe, 0, f"conv{h}")
                    copy(setup_act, conv_proj[:, h, :, :], ps_h[h][:, :].rearrange("p (k d) -> p k d", k=TAPS))

            def pre(c, k):
                q = c % 2
                if k == 0:
                    for h in range(HALVES):
                        after(act, pre_pe, c, f"conv{h}")
                        if c and h == 0:
                            after(act, pre_dve, c - 1, "du1")
                            after(act, pre_pe, c - 1, "skip1")
                        do(pre_act, u[:, h, :], ps_pre[:, :], ACT.Silu, bias=conv_b[:, h:h + 1])
                if k == 1:
                    for g in range(2):
                        after(act, pre_pe, c, f"res{g}")
                        if c >= 2 and g == 0:
                            after(act, tail_dve, c - 2, "yg")
                        do(pre_act, res_gate[:, q, 2 * g:2 * g + 2, :],
                           ps_pre[:, :].rearrange("p (j d) -> p j d", j=2), ACT.Silu)
                if k == 2:
                    after(act, pre_pe, c, "low")
                    copy(pre_act, dt_low[:, :], ps_pre[0:RANK, :])
                    after(act, pre_pe, c, "bstack")
                    if c:
                        after(act, pre_dve, c - 1, "part3")
                    copy(pre_act, b_all[:, :], ps_pre[0:96, :])
                if k == 3:
                    after(act, pre_pe, c, "crows")
                    if c >= 2:
                        act.wait_ge(y_dve, 2 * STATE * (c - 1))
                    copy(pre_act, c_rows[:, q, :, :], ps_pre[:, 0:BLOCKS * STATE].rearrange("p (j n) -> p j n", j=BLOCKS))
                if k == 4:
                    for h in range(HALVES):
                        after(act, pre_pe, c, f"dt{h}")
                        do(pre_act, sp_abs[:, h, :], ps_pre[:, :], ACT.Abs, bias=dt_b[:, h:h + 1])
                        if c and h == 0:
                            after(act, pre_dve, c - 1, "delta1")
                        do(pre_act, sp_relu[:, h, :], ps_pre[:, :], ACT.Relu, bias=dt_b[:, h:h + 1])
                    for h in range(HALVES):
                        after(act, pre_act, c, f"abs{h}")
                        do(pre_act, sp_exp[:, h, :], sp_abs[:, h, :], ACT.Exp, scale=-1.0)
                    for h in range(HALVES):
                        after(act, pre_act, c, f"exp{h}")
                        do(pre_act, sp_ln[:, h, :], sp_exp[:, h, :], ACT.Ln, bias=1.0)
                if k == 5:
                    for g in range(2):
                        after(act, pre_pe, c, f"skip{g}")
                        if c >= 2 and g == 0:
                            after(act, tail_pe, c - 2, "yg1")
                        copy(pre_act, y[:, q, 2 * g:2 * g + 2, :], ps_pre[:, :].rearrange("p (j d) -> p j d", j=2))

            def row(g):
                act.wait_ge(row_pe, g + 1)
                if g >= RING:
                    act.wait_ge(drive_pool, g - RING + 1)
                nc.scalar.copy(b_row[:, g % RING, :], ps_b[:, :]).then_inc(row_act, 1)

            def step(c, n):
                g = c * STATE + n
                row(g)
                if n == 0:
                    after(act, pre_dve, c, "delta1")
                if g == 0:
                    after(act, setup_dve, 0, "rate")
                if g >= RING:
                    act.wait_ge(state_dve, 2 * (g - RING) + 2)
                for h in range(HALVES):
                    nc.scalar.activation(decay[:, g % RING, h, :], delta[:, c % 2, h, :], ACT.Exp,
                                         scale=decay_rate[:, h, n:n + 1]).then_inc(decay_act, 1)

            def tail(c, k):
                if k == 0:
                    for h in range(HALVES):
                        after(act, tail_pe, c, f"yg{h}")
                        copy(tail_act, yg_t[:, h, :], (ps_g, ps_u[0])[h][:, :])
                if k == 1:
                    after(act, tail_dve, c, "sh1")
                    for j in range(BLOCKS):
                        last = nc.scalar.activation(x1[:, j, :], block_of(ps_u[1][:, :], j), ACT.Identity,
                                                    bias=shift[:, j:j + 1], scale=rstd[:, j:j + 1])
                    last.then_inc(tail_act.sem, 1)
                if k == 2:
                    after(act, tail_pe, c, "x1t")
                    copy(tail_act, x1_q[:, :], ps_d[:, :], saturate=False)
                    after(act, tail_pe, c, "ffn")
                    copy(tail_act, ffn_out[:, :, :], blocks_of(ps_u[0][:, :]))
                if k == 3:
                    after(act, tail_dve, c, "sh2")
                    for j in range(BLOCKS):
                        last = nc.scalar.activation(x2[:, j, :], r2[:, j, :], ACT.Identity,
                                                    bias=shift[:, j:j + 1], scale=rstd[:, j:j + 1])
                    last.then_inc(tail_act.sem, 1)
                if k == 4:
                    after(act, tail_pe, c, "x2t")
                    copy(tail_act, x2_t[:, :], ps_g[:, :])
                    after(act, tail_pe, c, "dlt")
                    do(tail_act, l1_abs[:, :], ps_u[0][:, :], ACT.Abs, bias=par_of("l1_delta_b"))
                    do(tail_act, l1_relu[:, :], ps_u[0][:, :], ACT.Relu, bias=par_of("l1_delta_b"))
                    after(act, tail_act, c, "abs")
                    do(tail_act, l1_exp[:, :], l1_abs[:, :], ACT.Exp, scale=-1.0)
                    after(act, tail_act, c, "exp")
                    do(tail_act, l1_ln[:, :], l1_exp[:, :], ACT.Ln, bias=1.0)
                if k == 5:
                    after(act, tail_pe, c, "mean")
                    copy(tail_act, l1_step[:, :], ps_d[0:STATE, :])
                    do(tail_act, l1_decay[:, :], ps_d[0:STATE, :], ACT.Exp, scale=l1_rate[:, :])
                if k == 6:
                    after(act, tail_dve, c, "sh3")
                    for j in range(BLOCKS):
                        last = nc.scalar.activation(x3[:, j, :], block_of(ps_g[:, :], j), ACT.Identity,
                                                    bias=shift[:, j:j + 1], scale=rstd[:, j:j + 1])
                    last.then_inc(tail_act.sem, 1)
                    after(act, tail_dve, c, "f3")
                    for j in range(BLOCKS):
                        last = nc.scalar.activation(hn[:, j, :], block_of(ps_g[:, :], j), ACT.Identity,
                                                    bias=shift3[:, j:j + 1], scale=scale3[:, j:j + 1])
                    last.then_inc(tail_act.sem, 1)
                    after(act, tail_pe, c, "hnt")
                    copy(tail_act, hn_t[:, :], ps_u[0][:, :])
                if k == 7:
                    after(act, tail_dve, c, "cen")
                    do(tail_act, exps[:, :, :], centred[:, :, :], ACT.Exp)
                if k == 8:
                    after(act, tail_dve, c, "wone")
                    if c:
                        act.wait_ge(result_act, c)
                    for j in range(BLOCKS):
                        last = nc.scalar.activation(acc[:, j, :], x3[:, j, :], ACT.Identity, scale=x_weight[:, j:j + 1])
                    last.then_inc(tail_act.sem, 1)

            def expert(c, e):
                q = e % 2
                if e < EXPERTS:
                    for f in range(2):
                        after(act, moe_pe, c, f"g{e}{'ab'[f]}")
                        if e:
                            after(act, moe_dve, c, f"h{e - 1}{'ab'[f]}")
                        do(moe_act, gelu[:, f, :], ps_g[:, :], ACT.Gelu)
                elif e == EXPERTS:
                    after(act, moe_pe, c, "gs")
                    after(act, moe_dve, c, f"h{e - 1}a")
                    do(moe_act, gelu[0:SIDE, 0, :], ps_g[0:SIDE, :], ACT.Gelu)
                else:
                    after(act, moe_dve, c, "sh")
                    if c >= 2:
                        act.wait_ge(stored[c % 2], 16 * (c // 2))
                    for j in range(BLOCKS):
                        last = nc.scalar.activation(result[:, c % 2, j, :], acc[:, j, :], ACT.Identity,
                                                    bias=shift[:, j:j + 1], scale=rstd[:, j:j + 1])
                    last.then_inc(result_act, 1)

            setup()
            run(pre=pre, step=step, tail=tail, expert=expert)

        @block.gpsimd
        def _(pool):
            nc.gpsimd.memset(minus_half[:, :], -0.5).then_inc(pool_const, 1)
            nc.gpsimd.memset(mean_w[:, :], 1.0 / P).then_inc(pool_const, 1)
            pool.wait_ge(pool_const, 2)

            def step(c, n):
                g = c * STATE + n
                if n == 0:
                    after(pool, pre_dve, c, "du1")
                pool.wait_ge(row_act, g + 1)
                if g >= RING:
                    pool.wait_ge(state_dve, 2 * (g - RING) + 2)
                nc.gpsimd.tensor_tensor(drive[:, g % RING, :, :], du[:, c % 2, :, :],
                                        b_row[:, g % RING:g % RING + 1, :].broadcast_to([P, HALVES, CHUNK]),
                                        ALU.mult).then_inc(drive_pool, 1)

            def rsqrt(marks, c, v, r, in_, eps, in_name, in_marks, out_):
                after(pool, in_marks, c, in_name)
                nc.gpsimd.tensor_scalar(var_eps[:, :], in_, 1.0, eps, ALU.mult, ALU.add).then_inc(marks.sem, 1)
                after(pool, marks, c, v)
                nc.gpsimd.tensor_tensor(out_, var_eps[:, :], minus_half[:, :], ALU.pow).then_inc(marks.sem, 1)

            def tail(c, k):
                if k == 1:
                    rsqrt(tail_pool, c, "v1", "rstd1", moments[:, :, 1], LN_EPS, "mo1", tail_dve, rstd[:, :])
                if k == 2:
                    after(pool, tail_act, c, "x1")
                    nc.gpsimd.tensor_tensor(x1_bias[:, :, :], x1[:, :, :],
                                            par_of("ffn_b")[:, None, :].broadcast_to([P, BLOCKS, P]),
                                            ALU.add).then_inc(tail_pool.sem, 1)
                if k == 3:
                    rsqrt(tail_pool, c, "v2", "rstd2", moments[:, :, 1], LN_EPS, "mo2", tail_dve, rstd[:, :])
                if k == 6:
                    rsqrt(tail_pool, c, "v3", "rstd3", moments[:, :, 1], LN_EPS, "mo3", tail_dve, rstd[:, :])
                    rsqrt(tail_pool, c, "v4", "rms", mean_sq[:, :], RMS_EPS, "msq", tail_dve, rms[:, :])

            def expert(c, e):
                if e == EXPERTS + 1:
                    rsqrt(moe_pool, c, "v", "rstd", moments[:, :, 1], LN_EPS, "mo", moe_dve, rstd[:, :])

            run(step=step, tail=tail, expert=expert)

        @block.vector
        def _(dve):
            v = nc.vector

            def do(marks, ins):
                ins.then_inc(marks.sem, 1)

            def own(marks, c, name):
                dve.wait_ge(marks.sem, marks.done(c, name))

            def setup():
                dve.wait_ge(loaded_first, 16)
                for h in range(HALVES):
                    for k in range(TAPS):
                        i = h * TAPS + k
                        last = v.tensor_scalar(conv_diag[:, h, k, :], ident, conv_w[:, i:i + 1], None, ALU.mult)
                do(setup_dve, last)
                for h in range(HALVES):
                    last = v.tensor_scalar(skip_diag[:, h, :], ident, skip[:, h:h + 1], None, ALU.mult)
                do(setup_dve, last)
                last = v.memset(b_stack[:, :, :], 0.0)
                do(setup_dve, last)
                own(setup_dve, 0, "b_stack")
                for i in range(3):
                    last = v.tensor_copy(b_stack[:, :, 32 * i:32 * i + STATE], x_proj[:, :, RANK:RANK + STATE])
                do(setup_dve, last)
                do(setup_dve, v.tensor_tensor(parts_of[:, :], ident[0:96, 0:STATE], ident[0:96, 32:32 + STATE], ALU.add))
                own(setup_dve, 0, "two")
                do(setup_dve, v.tensor_tensor(parts_of[:, :], parts_of[:, :], ident[0:96, 64:64 + STATE], ALU.add))
                own(setup_dve, 0, "three")
                do(setup_dve, v.tensor_copy(select[:, :, :], parts_of[:, :, None].broadcast_to([96, STATE, P])))
                dve.wait_ge(loaded_rest, 16)
                after(dve, setup_act, 0, "l1_exp")
                v.tensor_scalar(l1_rate[:, :], l1_rate[:, :], -1.0, None, ALU.mult)
                do(setup_dve, v.tensor_scalar(decay_rate[:, :, :], decay_rate[:, :, :], -1.0, None, ALU.mult))
                do(setup_dve, v.memset(ones[:, :], 1.0))
                w = par_of("ffn_w")
                do(setup_dve, v.tensor_scalar(ffn_t[:, :], w, 128.0, -128.0, ALU.min, ALU.max))
                own(setup_dve, 0, "clip")
                do(setup_dve, v.tensor_copy(ffn_small[:, :], ffn_t[:, :], saturate=False))
                do(setup_dve, v.tensor_scalar(ffn_t2[:, :], w, 448.0, -448.0, ALU.min, ALU.max))
                own(setup_dve, 0, "clip_half")
                do(setup_dve, v.tensor_scalar(ffn_half[:, :], ffn_t2[:, :], 0.5, None, ALU.mult, saturate=False))
                own(setup_dve, 0, "half_a")
                do(setup_dve, v.tensor_scalar(ffn_big[:, :], ffn_half[:, :], 2.0, None, ALU.mult))
                do(setup_dve, v.tensor_copy(ffn_t[:, :], ffn_small[:, :]))
                do(setup_dve, v.tensor_tensor(ffn_t3[:, :], ffn_t2[:, :], ffn_t2[:, :], ALU.mult))
                own(setup_dve, 0, "mask")
                do(setup_dve, v.tensor_tensor(ffn_big[:, :], ffn_big[:, :], ffn_t[:, :], ALU.subtract))
                own(setup_dve, 0, "diff")
                do(setup_dve, v.scalar_tensor_tensor(ffn_t3[:, :], ffn_t3[:, :], 4096.0, ffn_big[:, :], ALU.is_ge, ALU.mult))
                own(setup_dve, 0, "mix")
                do(setup_dve, v.tensor_tensor(ffn_q[:, :], ffn_t3[:, :], ffn_t[:, :], ALU.add))
                do(setup_dve, v.tensor_copy(before[:, :], par_of("before")))
                do(setup_dve, v.scalar_tensor_tensor(l1_diag[:, :], ident, par_of("l1_d"), ident, ALU.mult, ALU.add))
                dve.wait_ge(loaded_experts, 48)
                for e in range(EXPERTS):
                    last = v.tensor_scalar(wg[:, e, :], wg[:, e, :], par_of("norm_w")[:, e:e + 1], None, ALU.mult)
                do(setup_dve, last)
                for e in range(EXPERTS):
                    last = v.tensor_scalar(wu[:, e, :], wu[:, e, :], par_of("norm_w")[:, e:e + 1], None, ALU.mult)
                do(setup_dve, last)
                do(setup_dve, v.tensor_scalar(side_g[:, :], par_of("side_g"), par_of("f_norm"), None, ALU.mult))
                do(setup_dve, v.tensor_scalar(side_u[:, :], par_of("side_u"), par_of("f_norm"), None, ALU.mult))
                v.memset(picked_before[:, :], 0.0)
                v.memset(picked_sum[:, :], 0.0)
                do(setup_dve, v.memset(x_in[:, :, 0:TAPS - 1], 0.0))

            def pre(c, k):
                q = c % 2
                if k == 3:
                    after(dve, pre_act, c, "ball")
                    if c >= 2:
                        dve.wait_ge(row_pe, STATE * (c - 1))
                    do(pre_dve, v.tensor_copy(b_cut[:, :], b_all[:, :]))
                    v.tensor_copy(b_parts[0:32, q, :], b_all[0:32, :])
                    own(pre_dve, c, "cut1")
                    do(pre_dve, v.tensor_tensor(b_left[:, :], b_all[:, :], b_cut[:, :], ALU.subtract))
                    own(pre_dve, c, "left1")
                    do(pre_dve, v.tensor_copy(b_cut2[:, :], b_left[:, :]))
                    v.tensor_copy(b_parts[32:64, q, :], b_left[32:64, :])
                    own(pre_dve, c, "cut2")
                    do(pre_dve, v.tensor_tensor(b_all[64:96, :], b_left[64:96, :], b_cut2[64:96, :], ALU.subtract))
                    own(pre_dve, c, "left2")
                    do(pre_dve, v.tensor_copy(b_parts[64:96, q, :], b_all[64:96, :]))
                if k == 5:
                    after(dve, pre_act, c, "ln1")
                    if c >= 2:
                        dve.wait_ge(decay_act, 2 * STATE * (c - 1))
                    for h in range(HALVES):
                        do(pre_dve, v.tensor_scalar(delta[:, q, h, :], sp_exp[:, h, :], 1.0, -1.0, ALU.add, ALU.add))
                        own(pre_dve, c, f"t{h}")
                        do(pre_dve, v.tensor_tensor(delta[:, q, h, :], sp_ln[:, h, :], delta[:, q, h, :], ALU.subtract))
                        own(pre_dve, c, f"a{h}")
                        do(pre_dve, v.tensor_tensor(delta[:, q, h, :], delta[:, q, h, :], sp_exp[:, h, :], ALU.add))
                    for h in range(HALVES):
                        own(pre_dve, c, f"b{h}")
                        do(pre_dve, v.tensor_tensor(delta[:, q, h, :], delta[:, q, h, :], sp_relu[:, h, :], ALU.add))
                if k == 6:
                    if c >= 2:
                        dve.wait_ge(drive_pool, STATE * (c - 1))
                    for h in range(HALVES):
                        own(pre_dve, c, f"delta{h}")
                        do(pre_dve, v.tensor_tensor(du[:, q, h, :], delta[:, q, h, :], u[:, h, :], ALU.mult))

            def add_y(g):
                c, n = divmod(g, STATE)
                if n == 0:
                    after(dve, pre_act, c, "y1")
                else:
                    dve.wait_ge(y_dve, 2 * g)
                for i in range(2):
                    dve.wait_ge(turned_pe, 2 * g + i + 1)
                    for jj in range(2):
                        j = 2 * i + jj
                        last = v.scalar_tensor_tensor(y[:, c % 2, j, :], ps_h[i][:, jj * INNER:(jj + 1) * INNER],
                                                      c_rows[:, c % 2, j, n:n + 1], y[:, c % 2, j, :], ALU.mult, ALU.add)
                    last.then_inc(y_dve, 1)

            def step(c, n):
                g = c * STATE + n
                first = c % PER_BATCH == 0
                dve.wait_ge(drive_pool, g + 1)
                cc, nn = divmod(g - 2, STATE)
                if g >= 2 and cc % PER_BATCH == 0:
                    dve.wait_ge(carry_dve, (cc // PER_BATCH) * STATE + nn + 1)
                for h in range(HALVES):
                    dve.wait_ge(decay_act, 2 * g + h + 1)
                    if not first:
                        dve.wait_ge(carry_dve, (c // PER_BATCH) * STATE + n + 1)
                    v.tensor_tensor_scan(state[:, g % 2, h, :], decay[:, g % RING, h, :], drive[:, g % RING, h, :],
                                         0.0 if first else carry[:, h, n:n + 1], ALU.mult, ALU.add).then_inc(state_dve, 1)
                if g:
                    add_y(g - 1)
                if first:
                    dve.wait_ge(state_dve, 2 * g + 2)
                    v.tensor_copy(carry[:, :, n:n + 1], state[:, g % 2, :, CHUNK - 1:CHUNK]).then_inc(carry_dve, 1)

            def flush(c, k):
                add_y(STEPS - 1)

            def layer_norm_stats(marks, c, of, st, mo):
                for j in range(BLOCKS):
                    last = v.bn_stats(stats[:, j, :], of(j))
                do(marks, last)
                own(marks, c, st)
                for j in range(BLOCKS):
                    last = v.bn_aggr(moments[:, j, :], stats[:, j, :])
                do(marks, last)

            def layer_norm_shift(marks, pool_marks, c, r, sh):
                after(dve, pool_marks, c, r)
                do(marks, v.scalar_tensor_tensor(shift[:, :], moments[:, :, 0], -1.0, rstd[:, :], ALU.mult, ALU.mult))

            def each(ap):
                return ap[:, :, None].broadcast_to([P, BLOCKS, EXPERTS])

            def tail(c, k):
                q = c % 2
                if k == 0:
                    dve.wait_ge(y_dve, 2 * STATE * (c + 1))
                    do(tail_dve, v.tensor_tensor(y[:, q, :, :], y[:, q, :, :], res_gate[:, q, :, :], ALU.mult))
                if k == 1:
                    after(dve, tail_pe, c, "r1")
                    layer_norm_stats(tail_dve, c, lambda j: block_of(ps_u[1][:, :], j), "st1", "mo1")
                    layer_norm_shift(tail_dve, tail_pool, c, "rstd1", "sh1")
                if k == 3:
                    after(dve, tail_act, c, "ffn")
                    after(dve, tail_pool, c, "bias")
                    do(tail_dve, v.tensor_tensor(r2[:, :, :], ffn_out[:, :, :], x1_bias[:, :, :], ALU.add))
                    own(tail_dve, c, "r2")
                    layer_norm_stats(tail_dve, c, lambda j: r2[:, j, :], "st2", "mo2")
                    layer_norm_shift(tail_dve, tail_pool, c, "rstd2", "sh2")
                if k == 4:
                    after(dve, tail_act, c, "ln")
                    do(tail_dve, v.tensor_scalar(l1_t[:, :], l1_exp[:, :], 1.0, -1.0, ALU.add, ALU.add))
                    own(tail_dve, c, "t")
                    do(tail_dve, v.tensor_tensor(l1_t[:, :], l1_ln[:, :], l1_t[:, :], ALU.subtract))
                    own(tail_dve, c, "a")
                    do(tail_dve, v.tensor_tensor(l1_t[:, :], l1_t[:, :], l1_exp[:, :], ALU.add))
                    own(tail_dve, c, "b")
                    do(tail_dve, v.tensor_tensor(l1_sp[:, :], l1_t[:, :], l1_relu[:, :], ALU.add))
                if k == 5:
                    after(dve, tail_act, c, "decay")
                    do(tail_dve, v.tensor_tensor(l1_drive[:, :], l1_step[:, :], ps_u[1][0:STATE, :], ALU.mult))
                    own(tail_dve, c, "drive")
                    first = c % PER_BATCH == 0
                    do(tail_dve, v.tensor_tensor_scan(l1_state[:, q, :], l1_decay[:, :], l1_drive[:, :],
                                                      0.0 if first else l1_state[:, 1 - q, CHUNK - 1:CHUNK],
                                                      ALU.mult, ALU.add))
                if k == 6:
                    after(dve, tail_pe, c, "r3")
                    layer_norm_stats(tail_dve, c, lambda j: block_of(ps_g[:, :], j), "st3", "mo3")
                    after(dve, tail_pool, c, "rstd3")
                    do(tail_dve, v.tensor_tensor(mean_sq[:, :], moments[:, :, 1], rstd[:, :], ALU.mult))
                    own(tail_dve, c, "vr")
                    do(tail_dve, v.tensor_tensor(mean_sq[:, :], mean_sq[:, :], rstd[:, :], ALU.mult))
                    do(tail_dve, v.scalar_tensor_tensor(shift[:, :], moments[:, :, 0], -1.0, rstd[:, :], ALU.mult, ALU.mult))
                    after(dve, tail_pool, c, "rms")
                    own(tail_dve, c, "sh3")
                    do(tail_dve, v.scalar_tensor_tensor(rms_inv[:, :], mean_sq[:, :], RMS_EPS, rms[:, :], ALU.add, ALU.mult))
                    do(tail_dve, v.tensor_tensor(scale3[:, :], rstd[:, :], rms[:, :], ALU.mult))
                    do(tail_dve, v.tensor_tensor(shift3[:, :], shift[:, :], rms[:, :], ALU.mult))
                if k == 7:
                    after(dve, tail_pe, c, "logits")
                    do(tail_dve, v.tensor_tensor(logits[:, :, :], ps_d[:, 0:BLOCKS * EXPERTS].rearrange(
                        "p (j e) -> p j e", j=BLOCKS), each(rms_inv), ALU.mult))
                    own(tail_dve, c, "lg")
                    do(tail_dve, v.tensor_reduce(top[:, :], logits[:, :, :], AX.X, ALU.max))
                    own(tail_dve, c, "top")
                    do(tail_dve, v.tensor_tensor(centred[:, :, :], logits[:, :, :], each(top), ALU.subtract))
                    after(dve, tail_act, c, "exps")
                    do(tail_dve, v.tensor_reduce(total[:, :], exps[:, :, :], AX.X, ALU.add))
                    own(tail_dve, c, "tot")
                    do(tail_dve, v.reciprocal(total_inv[:, :], total[:, :]))
                    own(tail_dve, c, "tinv")
                    do(tail_dve, v.tensor_tensor(probs[:, :, :], exps[:, :, :], each(total_inv), ALU.mult))
                    own(tail_dve, c, "probs")
                    for j in range(BLOCKS):
                        last = v.max(sorted8[:, j, :], probs[:, j, :])
                    do(tail_dve, last)
                    own(tail_dve, c, "sort")
                    for j in range(BLOCKS):
                        last = v.max_index(where8[:, j, :], sorted8[:, j, :], probs[:, j, :])
                    do(tail_dve, last)
                    own(tail_dve, c, "where")
                    do(tail_dve, v.tensor_copy(where_f[:, :, :], where8[:, :, :]))
                    own(tail_dve, c, "wf")
                    index = par_of("index")[:, None, :].broadcast_to([P, BLOCKS, EXPERTS])
                    for pick, i in ((pick1, 0), (pick2, 1)):
                        do(tail_dve, v.tensor_tensor(pick[:, :, :], index,
                                                     where_f[:, :, i:i + 1].broadcast_to([P, BLOCKS, EXPERTS]), ALU.is_equal))
                    own(tail_dve, c, "p2")
                    do(tail_dve, v.tensor_tensor(picked[:, :, :], pick1[:, :, :], pick2[:, :, :], ALU.add))
                if k == 8:
                    after(dve, tail_pe, c, "counts")
                    own(tail_dve, c, "picked")
                    counts = ps_u[1][:, 0:BLOCKS * EXPERTS].rearrange("p (j e) -> p j e", j=BLOCKS)
                    do(tail_dve, v.scalar_tensor_tensor(late[:, :, :], counts, float(CAPACITY), picked[:, :, :],
                                                        ALU.is_ge, ALU.mult))
                    own(tail_dve, c, "late")
                    do(tail_dve, v.tensor_reduce(overflow[:, :], late[:, :, :], AX.X, ALU.max))
                    own(tail_dve, c, "over")
                    do(tail_dve, v.tensor_scalar(kept[:, :], overflow[:, :], -1.0, 1.0, ALU.mult, ALU.add))
                    do(tail_dve, v.tensor_tensor(weight0[:, :, :], probs[:, :, :], picked[:, :, :], ALU.mult))
                    own(tail_dve, c, "w0")
                    do(tail_dve, v.tensor_tensor(weight[:, :, :], weight0[:, :, :], each(kept), ALU.mult))
                    own(tail_dve, c, "w")
                    do(tail_dve, v.tensor_reduce(weight_sum[:, :], weight[:, :, :], AX.X, ALU.add))
                    own(tail_dve, c, "wsum")
                    do(tail_dve, v.tensor_scalar(x_weight[:, :], weight_sum[:, :], 2.0, None, ALU.add))
                    do(tail_dve, v.tensor_reduce(picked_new[:, :], picked[:, :, :].rearrange("p j e -> p e j"), AX.X, ALU.add))
                    own(tail_dve, c, "red")
                    do(tail_dve, v.tensor_tensor(picked_sum[:, :], picked_sum[:, :], picked_new[:, :], ALU.add))
                    own(tail_dve, c, "psum")
                    do(tail_dve, v.tensor_copy(picked_before[:, :], picked_sum[:, :]))

            def expert(c, e):
                q = e % 2

                def accumulate(name, weights):
                    after(dve, moe_pe, c, name)
                    for j in range(BLOCKS):
                        last = v.scalar_tensor_tensor(acc[:, j, :], block_of(ps_d[:, :], j), weights(j), acc[:, j, :],
                                                      ALU.mult, ALU.add)
                    do(moe_dve, last)

                if e < EXPERTS:
                    for f in range(2):
                        after(dve, moe_pe, c, f"u{e}{'ab'[f]}")
                        after(dve, moe_act, c, f"g{e}{'ab'[f]}")
                        do(moe_dve, v.tensor_tensor(hidden[:, q, f, :], gelu[:, f, :], ps_u[f][:, :], ALU.mult))
                    if e == 0:
                        after(dve, tail_act, c, "acc")
                    else:
                        own(moe_dve, c, f"acc{e - 1}" )
                    accumulate(f"d{e}", lambda j: weight[:, j, e:e + 1])
                elif e == EXPERTS:
                    after(dve, moe_pe, c, "us")
                    after(dve, moe_act, c, "gs")
                    do(moe_dve, v.tensor_tensor(hidden[0:SIDE, q, 0, :], gelu[0:SIDE, 0, :], ps_u[0][0:SIDE, :], ALU.mult))
                    own(moe_dve, c, f"acc{e - 1}")
                    accumulate("ds", lambda j: overflow[:, j:j + 1])
                else:
                    own(moe_dve, c, "accs")
                    layer_norm_stats(moe_dve, c, lambda j: acc[:, j, :], "st", "mo")
                    layer_norm_shift(moe_dve, moe_pool, c, "rstd", "sh")

            setup()
            run(pre=pre, step=step, tail=tail, expert=expert, flush=flush)


def kernel(**inputs):
    import numpy as np
    import concourse.bacc as bacc
    from concourse.bass_utils import run_bass_kernel_spmd

    a = {k: np.asarray(v) for k, v in inputs.items()}

    def halves(w):
        return w.reshape(HALVES, P, -1).transpose(1, 0, 2).reshape(P, -1)

    def padded(w):
        return np.concatenate([w, np.zeros((P - w.shape[0], w.shape[1]), w.dtype)])

    in_w = a["L0_attn_in_proj_w"]
    columns = {
        "ident": np.eye(P, dtype=np.float32),
        "conv_w": halves(a["L0_attn_conv_w"].reshape(INNER, TAPS)),
        "conv_b": halves(a["L0_attn_conv_b"]),
        "dt_b": halves(a["L0_attn_dt_proj_b"]),
        "a_log": halves(a["L0_attn_A_log"]),
        "skip": halves(a["L0_attn_Dp"]),
        "in_x": halves(in_w[:INNER]),
        "in_res": in_w[INNER:].T,
        "x_proj": halves(a["L0_attn_x_proj_w"].T),
        "dt_proj": padded(a["L0_attn_dt_proj_w"].T),
        "out_proj": halves(a["L0_attn_out_proj_w"].T),
        "ffn_w": a["L0_ffn_weight"].T,
        "ffn_b": np.broadcast_to(a["L0_ffn_bias"], (P, P)),
        "l1_b": a["L1_attn_B"].T,
        "l1_c": padded(a["L1_attn_C"].T),
        "l1_d": a["L1_attn_D"][:, None],
        "l1_delta": a["L1_attn_W_delta"].T,
        "l1_delta_b": a["L1_attn_b_delta"][:, None],
        "l1_a_log": padded(a["L1_attn_A_log"][:, None]),
        "router": a["L1_ffn_Wr"],
        "norm_w": a["L1_ffn_norm_w"].T,
        "f_norm": a["L1_ffn_f_norm"][:, None],
        "side_g": a["L1_ffn_fWg"],
        "side_u": a["L1_ffn_fWu"],
        "side_d": padded(a["L1_ffn_fWd"]),
        "before": np.triu(np.ones((P, P), np.float32), 1),
        "index": np.broadcast_to(np.arange(EXPERTS, dtype=np.float32), (P, EXPERTS)),
    }
    assert list(columns) == list(PARAMS) and all(columns[k].shape == (P, w) for k, w in PARAMS.items())
    arrays = {
        "x_t": np.ascontiguousarray(a["L0_attn_x"].reshape(TOKENS, P).T),
        "params": np.ascontiguousarray(np.concatenate(list(columns.values()), axis=1)),
        "w_gate": np.ascontiguousarray(a["L1_ffn_Wg"].transpose(1, 0, 2)),
        "w_up": np.ascontiguousarray(a["L1_ffn_Wu"].transpose(1, 0, 2)),
        "w_down": np.ascontiguousarray(a["L1_ffn_Wd"].reshape(EXPERTS, 2, P, P).transpose(2, 0, 1, 3)),
    }
    nc = bacc.Bacc("TRN2", target_bir_lowering=False, num_devices=1)
    ins = [nc.dram_tensor(k, w.shape, F32, kind="ExternalInput").ap() for k, w in arrays.items()]
    out = nc.dram_tensor("out", (TOKENS, P), F32, kind="ExternalOutput").ap()
    build(nc, *ins, out)
    got = run_bass_kernel_spmd(nc, [arrays], core_ids=[0]).results[0]["out"]
    return got.reshape(BATCH, LENGTH, P)
```

```python
from contextlib import ExitStack

import concourse.bass as bass
from concourse import mybir

F32 = mybir.dt.float32
F32R = mybir.dt.float32r
F16 = mybir.dt.float16
BF16 = mybir.dt.bfloat16
F8 = mybir.dt.float8e4
U32 = mybir.dt.uint32
ALU = mybir.AluOpType
ACT = mybir.ActivationFunctionType
AX = mybir.AxisListType

P = 128
BATCH, LENGTH = 2, 1024
TOKENS = BATCH * LENGTH
CHUNK = 512
BLOCKS = CHUNK // P
CHUNKS = TOKENS // CHUNK
PER_BATCH = LENGTH // CHUNK
HALVES = 2
INNER = HALVES * P
STATE = 16
RANK = 64
TAPS = 4
EXPERTS = 8
HIDDEN = 256
SIDE = 64
CAPACITY = 512
LN_EPS = 1e-5
RMS_EPS = 1e-6
RING = 3
STEPS = CHUNKS * STATE
LEAD = 2
GROUP = 3
NETS = EXPERTS + 1

PARAMS = {
    "ident": P, "conv_w": HALVES * TAPS, "conv_b": HALVES, "dt_b": HALVES, "a_log": HALVES * STATE,
    "skip": HALVES, "in_x": HALVES * P, "in_res": INNER, "x_proj": HALVES * 96, "dt_proj": INNER,
    "out_proj": HALVES * P, "ffn_w": P, "ffn_b": P, "l1_b": STATE, "l1_c": P, "l1_d": 1, "l1_delta": P,
    "l1_delta_b": 1, "l1_a_log": 1, "router": EXPERTS, "norm_w": EXPERTS, "f_norm": 1,
    "side_g": SIDE, "side_u": SIDE, "side_d": P, "before": P, "index": EXPERTS,
}
AT, _n = {}, 0
for _k, _w in PARAMS.items():
    AT[_k] = (_n, _w)
    _n += _w
PARAM_COLS = _n
FIRST_COLS = AT["out_proj"][0]


class Marks:

    def __init__(self, sem, names):
        self.sem, self.names = sem, names.split()
        assert len(set(self.names)) == len(self.names)

    def done(self, c, name):
        return c * len(self.names) + self.names.index(name) + 1


def build(nc, x_t, params, w_gate, w_up, w_down, b_dram, weight_dram, out):
    with ExitStack() as ctx:
        def sb(name, shape, dt=F32):
            return ctx.enter_context(nc.sbuf_tensor(name, shape, dt))

        def bank(name):
            return ctx.enter_context(nc.psum_tensor(name, [P, 512], F32))

        def sem(name):
            return ctx.enter_context(nc.semaphore(name))

        par = sb("par", [P, PARAM_COLS])

        def par_of(name):
            a, w = AT[name]
            return par[:, a:a + w]

        ident = par_of("ident")
        conv_w, conv_b, dt_b = par_of("conv_w"), par_of("conv_b"), par_of("dt_b")
        skip = par_of("skip")
        in_x = par_of("in_x").rearrange("p (h m) -> p h m", h=HALVES)
        in_res = par_of("in_res")
        x_proj = par_of("x_proj").rearrange("p (h m) -> p h m", h=HALVES)
        dt_proj = par_of("dt_proj")
        out_proj = par_of("out_proj").rearrange("p (h m) -> p h m", h=HALVES)
        x_in = sb("x_in", [P, BATCH, TAPS - 1 + LENGTH])
        w_in = {k: [sb(f"{k}{part}", [P, EXPERTS, HIDDEN], F32R) for part in range(2)] for k in ("wg", "wu")}
        wd = sb("wd", [P, EXPERTS, 2, P])
        conv_proj = sb("conv_proj", [P, HALVES, TAPS, P])
        skip_diag = sb("skip_diag", [P, HALVES, P])
        decay_rate = sb("decay_rate", [P, HALVES, STATE])
        l1_rate = sb("l1_rate", [STATE, 1])
        l1_diag = sb("l1_diag", [P, P])
        mean_w = sb("mean_w", [P, STATE])
        ffn_small = sb("ffn_small", [P, P], F8)
        ffn_half = sb("ffn_half", [P, P], F8)
        ffn_q = sb("ffn_q", [P, P], F16)
        before = sb("before", [P, P], BF16)
        ones = sb("ones", [P, P], BF16)
        minus_half = sb("minus_half", [P, BLOCKS])
        side_g = sb("side_g", [P, SIDE])
        side_u = sb("side_u", [P, SIDE])

        gelu = sb("gelu", [P, GROUP, 2, CHUNK])
        hidden = sb("hidden", [P, 2, 2, CHUNK])
        weight_row = sb("weight_row", [P, GROUP, CHUNK])
        acc_t = sb("acc_t", [P, CHUNK])
        x1 = sb("x1", [P, BLOCKS, P])
        acc = acc_t[:, :].rearrange("p (j d) -> p j d", j=BLOCKS)
        hn = x1
        conv_diag = weight_row[:, 0:2, :].rearrange("p h (k d) -> p h k d", k=TAPS)
        ffn_t, ffn_t2, ffn_t3, ffn_big = (acc_t[:, i * P:(i + 1) * P] for i in range(4))
        w_loaded = {"wg": gelu[:, 0:2, :, :].rearrange("p r f (e n) -> p (r f e) n", n=HIDDEN),
                    "wu": hidden[:, :, :, :].rearrange("p r f (e n) -> p (r f e) n", n=HIDDEN)}
        sp_relu = weight_row[:, 0:2, :]
        yg_t = hidden[:, 0, :, :]
        l1_ln = l1_abs = gelu[:, 0, 0, :]
        l1_exp = gelu[:, 0, 1, :]
        l1_relu = gelu[:, 1, 0, :]
        l1_sp = l1_t = gelu[:, 1, 1, :]
        l1_step, l1_decay = gelu[0:STATE, 2, 0, :], gelu[0:STATE, 2, 1, :]
        l1_drive = hidden[0:STATE, 1, 0, :]

        u = sb("u", [P, HALVES, CHUNK])
        res_gate = sb("res_gate", [P, 2, BLOCKS, INNER])
        low = sb("low", [RANK + STATE, 2, CHUNK])
        c_rows = sb("c_rows", [P, 2, BLOCKS, STATE])
        sp_abs = sb("sp_abs", [P, HALVES, CHUNK])
        sp_exp = sb("sp_exp", [P, HALVES, CHUNK])
        sp_ln = sp_abs
        delta = sb("delta", [P, 2, HALVES, CHUNK])
        du = sb("du", [P, 2, HALVES, CHUNK])
        y = sb("y", [P, 2, BLOCKS, INNER])
        b_row = sb("b_row", [P, 2, 2, CHUNK])
        decay = sb("decay", [P, RING, HALVES, CHUNK])
        drive = sb("drive", [P, RING, HALVES, CHUNK])
        state = sb("state", [P, 2, HALVES, CHUNK])
        carry = sb("carry", [P, HALVES, STATE])
        stats = sb("stats", [P, BLOCKS, 6])
        moments = sb("moments", [P, BLOCKS, 2])
        var_eps = sb("var_eps", [P, BLOCKS])
        rstd = sb("rstd", [P, BLOCKS])
        shift = sb("shift", [P, BLOCKS])
        x1_bias = sb("x1_bias", [P, BLOCKS, P])
        x1_q = sb("x1_q", [P, CHUNK], F8)
        ffn_out = sb("ffn_out", [P, BLOCKS, P], F16)
        r2 = x2 = x1_bias
        x2_t = sb("x2_t", [P, CHUNK])
        l1_state = sb("l1_state", [STATE, 2, CHUNK])
        mean_sq = sb("mean_sq", [P, BLOCKS])
        rms = sb("rms", [P, BLOCKS])
        rms_inv = sb("rms_inv", [P, BLOCKS])
        scale3 = sb("scale3", [P, BLOCKS])
        shift3 = sb("shift3", [P, BLOCKS])
        x3 = sb("x3", [P, BLOCKS, P])
        hn_t = sb("hn_t", [P, CHUNK])
        hn_parts = [sb(f"hn_part{part}", [P, CHUNK], F32R) for part in range(2)]
        logits = sb("logits", [P, BLOCKS, EXPERTS])
        top = sb("top", [P, BLOCKS])
        centred = sb("centred", [P, BLOCKS, EXPERTS])
        exps = sb("exps", [P, BLOCKS, EXPERTS])
        total = sb("total", [P, BLOCKS])
        total_inv = sb("total_inv", [P, BLOCKS])
        probs = sb("probs", [P, BLOCKS, EXPERTS])
        sorted8 = sb("sorted8", [P, BLOCKS, 8])
        where8 = sb("where8", [P, BLOCKS, 8], U32)
        where_f = sb("where_f", [P, BLOCKS, 8])
        pick1 = sb("pick1", [P, BLOCKS, EXPERTS])
        pick2 = sb("pick2", [P, BLOCKS, EXPERTS])
        picked = sb("picked", [P, BLOCKS, EXPERTS], BF16)
        picked_new = sb("picked_new", [P, EXPERTS])
        picked_sum = sb("picked_sum", [P, EXPERTS])
        picked_before = sb("picked_before", [P, EXPERTS], BF16)
        late = sb("late", [P, BLOCKS, EXPERTS])
        kept = sb("kept", [P, BLOCKS])
        weight0 = sb("weight0", [P, BLOCKS, EXPERTS])
        net_weight = sb("net_weight", [P, BLOCKS, NETS])
        weight, overflow = net_weight[:, :, 0:EXPERTS], net_weight[:, :, EXPERTS]
        weight_t = sb("weight_t", [NETS, CHUNK])
        weight_sum = sb("weight_sum", [P, BLOCKS])
        x_weight = sb("x_weight", [P, BLOCKS])
        stats4 = sb("stats4", [P, BLOCKS, 6])
        moments4 = sb("moments4", [P, BLOCKS, 2])
        var_eps4 = sb("var_eps4", [P, BLOCKS])
        rstd4 = sb("rstd4", [P, BLOCKS])
        shift4 = sb("shift4", [P, BLOCKS])
        result = sb("result", [P, BLOCKS, P])

        ps_pre = bank("ps_pre")
        ps_h = [bank("ps_h0"), bank("ps_h1")]
        ps_g = [bank("ps_g0"), bank("ps_g1")]
        ps_u = [bank("ps_u0"), bank("ps_u1")]
        ps_acc = bank("ps_acc")

        loaded_first = sem("loaded_first")
        loaded_x = [sem(f"loaded_x{c}") for c in range(CHUNKS)]
        loaded_rest = sem("loaded_rest")
        loaded_gate = sem("loaded_gate")
        loaded_up = sem("loaded_up")
        loaded_down = sem("loaded_down")
        stored = sem("stored")
        pool_const = sem("pool_const")
        setup_dve = Marks(sem("setup_dve"), "diag zero skip_diag rate ones clip small_a clip_half half_a "
                          "big small mask diff mix cast before l1_diag side_g side_u")
        setup_act = Marks(sem("setup_act"), "a_exp l1_exp conv0 conv1")
        setup_pe = Marks(sem("setup_pe"), "conv0 conv1")
        split_dve = sem("split_dve")
        pre_pe = Marks(sem("pre_pe"), "conv0 conv1 res0 res1 low crows dt0 dt1 skip0 skip1")
        pre_act = Marks(sem("pre_act"), "u0 u1 gate0 gate1 low crows abs0 relu0 abs1 relu1 exp0 exp1 ln0 ln1 y0 y1")
        pre_dve = Marks(sem("pre_dve"), "t0 a0 b0 t1 a1 b1 delta0 delta1 du0 du1")
        rows_out = sem("rows_out")
        rows_in = [sem(f"rows_in{i}") for i in range(2)]
        decay_act = sem("decay_act")
        drive_pool = sem("drive_pool")
        state_dve = sem("state_dve")
        carry_dve = sem("carry_dve")
        turned_pe = sem("turned_pe")
        y_dve = sem("y_dve")
        tail_pe = Marks(sem("tail_pe"), "yg0 yg1 r1 x1t ffn x2t dlt bx mean r3 hnt logits counts wt")
        tail_act = Marks(sem("tail_act"), "yg0 yg1 x1 x1q ffn x2 x2t abs relu exp ln step decay x3 hn hnt hi exps wt")
        tail_dve = Marks(sem("tail_dve"), "yg st1 mo1 sh1 r2 st2 mo2 sh2 t a b sp drive scan st3 mo3 vr msq sh3 inv s3 "
                         "f3 lo lg top cen tot tinv probs sort where wf p1 p2 picked late over kept w0 w wsum xw red psum pbef")
        tail_pool = Marks(sem("tail_pool"), "v1 rstd1 bias v2 rstd2 v3 rstd3 v4 rms")
        weights_out = sem("weights_out")
        weights_in = sem("weights_in")
        gate_pe = sem("gate_pe")
        gelu_act = sem("gelu_act")
        weighted_pool = sem("weighted_pool")
        up_pe = sem("up_pe")
        hidden_dve = sem("hidden_dve")
        down_pe = sem("down_pe")
        fin_pe = Marks(sem("fin_pe"), "acc")
        fin_act = Marks(sem("fin_act"), "acc_t result")
        fin_dve = Marks(sem("fin_dve"), "acc st mo sh")
        fin_pool = Marks(sem("fin_pool"), "v rstd")

        def after(eng, marks, c, name):
            eng.wait_ge(marks.sem, marks.done(c, name))

        def tokens(c):
            return c // PER_BATCH, c % PER_BATCH * CHUNK

        def block_of(ap, j):
            return ap[:, j * P:(j + 1) * P]

        def blocks_of(ap):
            return ap.rearrange("p (j d) -> p j d", j=BLOCKS)

        PRE_PARTS, TAIL_PARTS = 6, 9
        SLOTS = [("pre", k, k) for k in range(PRE_PARTS)]
        SLOTS += [("tail", k, 16 + t) for k, t in enumerate((0, 1, 2, 2, 3, 4, 5, 6, 6))]
        for i in range(NETS // GROUP):
            at = 16 + 6 + 3 * i
            SLOTS += [("rows", i, at - (i > 0))]
            SLOTS += [("gate", GROUP * i + e, at) for e in range(GROUP)]
            SLOTS += [("up", GROUP * i + e, at + e) for e in range(GROUP)]
            SLOTS += [("join", GROUP * i + e, at + e + 1) for e in range(GROUP)]
            SLOTS += [("down", GROUP * i + e, at + e + 2) for e in range(GROUP)]
        SLOTS += [("fin", 0, 33)]
        LAST = 16 * CHUNKS + 18

        def run(lead=0, **parts):
            for k in range(PRE_PARTS):
                if "pre" in parts:
                    parts["pre"](0, k)
            for g in range(lead):
                parts["step"](*divmod(g, STATE))
            for slot in range(LAST):
                if "step" in parts and slot + lead < STEPS:
                    parts["step"](*divmod(slot + lead, STATE))
                if slot == STEPS and "flush" in parts:
                    parts["flush"](CHUNKS - 1, 0)
                for kind, k, at in sorted(SLOTS, key=lambda x: -x[2]):
                    if at < STATE:
                        c = slot // STATE + 1 if slot % STATE == at else -1
                        if not 0 < c < CHUNKS:
                            continue
                    elif (slot - at) % STATE == 0 and 0 <= (slot - at) // STATE < CHUNKS:
                        c = (slot - at) // STATE
                    else:
                        continue
                    if kind in parts:
                        parts[kind](c, k)

        block = ctx.enter_context(nc.Block())

        @block.sync
        def _(sp):
            sp.dma_start(par[:, 0:FIRST_COLS], params[:, 0:FIRST_COLS]).then_inc(loaded_first, 16)
            for c in range(CHUNKS):
                b, t0 = tokens(c)
                sp.dma_start(x_in[:, b, TAPS - 1 + t0:TAPS - 1 + t0 + CHUNK],
                             x_t[:, c * CHUNK:(c + 1) * CHUNK]).then_inc(loaded_x[c], 16)
                if c == 0:
                    sp.dma_start(par[:, FIRST_COLS:], params[:, FIRST_COLS:]).then_inc(loaded_rest, 16)
            sp.dma_start(w_loaded["wg"], w_gate).then_inc(loaded_gate, 16)
            sp.dma_start(w_loaded["wu"], w_up).then_inc(loaded_up, 16)
            sp.dma_start(wd[:], w_down).then_inc(loaded_down, 16)

            def pair(m):
                c, n = divmod(2 * m, STATE)
                if m >= 2:
                    sp.wait_ge(drive_pool, 2 * (m - 2) + 2)
                if n == 0:
                    sp.wait_ge(rows_out, 16 * (c + 1))
                sp.dma_start(b_row[:, m % 2, :, :],
                             b_dram[c % 2, None, n:n + 2, :].broadcast_to([P, 2, CHUNK])).then_inc(rows_in[m % 2], 16)

            def pre(c, k):
                if k == 2:
                    after(sp, pre_act, c, "low")
                    if c >= 2:
                        for i in range(2):
                            sp.wait_ge(rows_in[i], 16 * STATE // 4 * (c - 1))
                    sp.dma_start(b_dram[c % 2], low[RANK:RANK + STATE, c % 2, :]).then_inc(rows_out, 16)

            def step(c, n):
                g = c * STATE + n
                if g == 0:
                    pair(0)
                if g % 2 == 0 and g + 2 < STEPS:
                    pair(g // 2 + 1)

            def tail(c, k):
                if k == 8:
                    after(sp, tail_act, c, "wt")
                    if c:
                        sp.wait_ge(weights_in, 16 * (NETS // GROUP) * c)
                    sp.dma_start(weight_dram[:, :], weight_t[:, :]).then_inc(weights_out, 16)

            def rows(c, i):
                if i == 0:
                    sp.wait_ge(weights_out, 16 * (c + 1))
                if c or i:
                    sp.wait_ge(weighted_pool, NETS * c + GROUP * i)
                elif i == 0:
                    after(sp, setup_pe, 0, "conv1")
                sp.dma_start(weight_row[:, :, :], weight_dram[None, GROUP * i:GROUP * (i + 1), :]
                             .broadcast_to([P, GROUP, CHUNK])).then_inc(weights_in, 16)

            def fin(c, k):
                after(sp, fin_act, c, "result")
                sp.dma_start(out[c * CHUNK:(c + 1) * CHUNK, :].rearrange("(j t) d -> t j d", j=BLOCKS),
                             result[:, :, :]).then_inc(stored, 16)

            run(pre=pre, step=step, tail=tail, rows=rows, fin=fin)
            sp.wait_ge(stored, 16 * CHUNKS)

        @block.tensor
        def _(pe):
            mm, turn = nc.tensor.matmul, nc.tensor.transpose

            def setup():
                after(pe, setup_dve, 0, "diag")
                for h in range(HALVES):
                    for k in range(TAPS):
                        last = mm(block_of(ps_h[h][:, :], k), in_x[:, h, :], conv_diag[:, h, k, :], start=True, stop=True)
                    last.then_inc(setup_pe.sem, 1)

            def pre(c, k):
                q = c % 2
                b, t0 = tokens(c)
                if k == 0:
                    if c == 0:
                        after(pe, setup_act, 0, "conv1")
                        after(pe, setup_dve, 0, "zero")
                    pe.wait_ge(loaded_x[c], 16)
                    if c:
                        after(pe, pre_act, c - 1, "y1")
                    for h in range(HALVES):
                        if h:
                            after(pe, pre_act, c, "u0")
                        for tap in range(TAPS):
                            last = mm(ps_pre[:, :], conv_proj[:, h, tap, :], x_in[:, b, t0 + tap:t0 + tap + CHUNK],
                                      start=(tap == 0), stop=(tap == TAPS - 1))
                        last.then_inc(pre_pe.sem, 1)
                if k == 1:
                    for g in range(2):
                        after(pe, pre_act, c, ("u1", "gate0")[g])
                        for i in range(2):
                            t = TAPS - 1 + t0 + (2 * g + i) * P
                            last = mm(ps_pre[:, i * INNER:(i + 1) * INNER], x_in[:, b, t:t + P], in_res,
                                      start=True, stop=True)
                        last.then_inc(pre_pe.sem, 1)
                if k == 2:
                    after(pe, pre_act, c, "gate1")
                    for h in range(HALVES):
                        last = mm(ps_pre[0:RANK + STATE, :], x_proj[:, h, 0:RANK + STATE], u[:, h, :],
                                  start=(h == 0), stop=(h == 1))
                    last.then_inc(pre_pe.sem, 1)
                if k == 3:
                    after(pe, pre_act, c, "low")
                    for j in range(BLOCKS):
                        for h in range(HALVES):
                            last = mm(ps_pre[:, j * STATE:(j + 1) * STATE], u[:, h, j * P:(j + 1) * P],
                                      x_proj[:, h, RANK + STATE:RANK + 2 * STATE], start=(h == 0), stop=(h == 1))
                    last.then_inc(pre_pe.sem, 1)
                if k == 4:
                    for h in range(HALVES):
                        after(pe, pre_act, c, ("crows", "relu0")[h])
                        mm(ps_pre[:, :], dt_proj[0:RANK, h * P:(h + 1) * P], low[0:RANK, q, :],
                           start=True, stop=True).then_inc(pre_pe.sem, 1)
                if k == 5:
                    if c == 0:
                        after(pe, setup_dve, 0, "skip_diag")
                    for g in range(2):
                        after(pe, pre_act, c, ("relu1", "y0")[g])
                        for i in range(2):
                            j = 2 * g + i
                            for h in range(HALVES):
                                last = mm(ps_pre[:, i * INNER + h * P:i * INNER + (h + 1) * P],
                                          u[:, h, j * P:(j + 1) * P], skip_diag[:, h, :], start=True, stop=True)
                        last.then_inc(pre_pe.sem, 1)

            def step(c, n):
                g = c * STATE + n
                pe.wait_ge(state_dve, 2 * g + 2)
                for i in range(2):
                    if g:
                        pe.wait_ge(y_dve, 2 * (g - 1) + i + 1)
                    elif i == 0:
                        after(pe, setup_act, 0, "conv1")
                    for jj in range(2):
                        for h in range(HALVES):
                            last = turn(ps_h[i][:, jj * INNER + h * P:jj * INNER + (h + 1) * P],
                                        state[:, g % 2, h, (2 * i + jj) * P:(2 * i + jj + 1) * P], ident)
                    last.then_inc(turned_pe, 1)

            def tail(c, k):
                q = c % 2
                b, t0 = tokens(c)
                if k == 0:
                    after(pe, tail_dve, c, "yg")
                    if c:
                        pe.wait_ge(hidden_dve, NETS * c)
                        pe.wait_ge(gelu_act, NETS * c)
                    for h in range(HALVES):
                        for j in range(BLOCKS):
                            last = turn(block_of((ps_g[0], ps_u[0])[h][:, :], j), y[:, q, j, h * P:(h + 1) * P], ident)
                        last.then_inc(tail_pe.sem, 1)
                if k == 1:
                    after(pe, tail_act, c, "yg1")
                    for j in range(BLOCKS):
                        t = TAPS - 1 + t0 + j * P
                        mm(block_of(ps_u[1][:, :], j), x_in[:, b, t:t + P], ident, start=True, stop=False)
                        for h in range(HALVES):
                            last = mm(block_of(ps_u[1][:, :], j), yg_t[:, h, j * P:(j + 1) * P], out_proj[:, h, :],
                                      start=False, stop=(h == 1))
                    last.then_inc(tail_pe.sem, 1)
                if k == 2:
                    after(pe, tail_act, c, "x1")
                    for j in range(BLOCKS):
                        last = turn(block_of(ps_g[1][:, :], j), x1[:, j, :], ident)
                    last.then_inc(tail_pe.sem, 1)
                    after(pe, tail_act, c, "x1q")
                    for j in range(BLOCKS):
                        last = mm(block_of(ps_u[0][:, :], j), x1_q[:, j * P:(j + 1) * P], ffn_q[:, :], start=True, stop=True)
                    last.then_inc(tail_pe.sem, 1)
                if k == 4:
                    after(pe, tail_act, c, "x2")
                    for j in range(BLOCKS):
                        last = turn(block_of(ps_g[0][:, :], j), x2[:, j, :], ident)
                    last.then_inc(tail_pe.sem, 1)
                    after(pe, tail_act, c, "x2t")
                    mm(ps_u[0][:, :], par_of("l1_delta"), x2_t[:, :], start=True, stop=True).then_inc(tail_pe.sem, 1)
                    mm(ps_u[1][0:STATE, :], par_of("l1_b"), x2_t[:, :], start=True, stop=True).then_inc(tail_pe.sem, 1)
                if k == 5:
                    after(pe, tail_dve, c, "sp")
                    mm(ps_g[1][0:STATE, :], mean_w[:, :], l1_sp[:, :], start=True, stop=True).then_inc(tail_pe.sem, 1)
                    after(pe, tail_dve, c, "scan")
                    for j in range(BLOCKS):
                        mm(block_of(ps_g[0][:, :], j), x2_t[:, j * P:(j + 1) * P], l1_diag[:, :], start=True, stop=False)
                        last = mm(block_of(ps_g[0][:, :], j), l1_state[:, q, j * P:(j + 1) * P],
                                  par_of("l1_c")[0:STATE, :], start=False, stop=True)
                    last.then_inc(tail_pe.sem, 1)
                if k == 6:
                    after(pe, tail_act, c, "hn")
                    for j in range(BLOCKS):
                        last = turn(block_of(ps_u[0][:, :], j), hn[:, j, :], ident)
                    last.then_inc(tail_pe.sem, 1)
                if k == 7:
                    after(pe, tail_act, c, "hnt")
                    for j in range(BLOCKS):
                        last = mm(ps_g[1][:, j * EXPERTS:(j + 1) * EXPERTS], hn_t[:, j * P:(j + 1) * P],
                                  par_of("router"), start=True, stop=True)
                    last.then_inc(tail_pe.sem, 1)
                if k == 8:
                    after(pe, tail_dve, c, "picked")
                    for j in range(BLOCKS):
                        o = ps_u[1][:, j * EXPERTS:(j + 1) * EXPERTS]
                        mm(o, before[:, :], picked[:, j, :], start=True, stop=False)
                        for i in range(j):
                            mm(o, ones[:, :], picked[:, i, :], start=False, stop=False)
                        last = mm(o, ones[:, :], picked_before[:, :], start=False, stop=True)
                    last.then_inc(tail_pe.sem, 1)

                    after(pe, tail_dve, c, "w")
                    for j in range(BLOCKS):
                        last = mm(ps_g[1][0:NETS, j * P:(j + 1) * P], net_weight[:, j, :], ident, start=True, stop=True)
                    last.then_inc(tail_pe.sem, 1)

            def layer_in(banks, kind, e, released):
                for f in range(2):
                    if released:
                        released(f)
                    for i, (wp, hp) in enumerate(((0, 0), (0, 1), (1, 0))):
                        last = mm(banks[f][:, :], w_in[kind][wp][:, e, f * P:(f + 1) * P], hn_parts[hp][:, :],
                                  start=(i == 0), stop=(i == 2))
                return last

            def gate(c, e):
                m = NETS * c + e
                if e == 0:
                    after(pe, tail_dve, c, "lo")
                    after(pe, tail_act, c, "wt")
                    if c == 0:
                        pe.wait_ge(split_dve, 4 * EXPERTS)
                        after(pe, setup_dve, 0, "side_u")
                        pe.wait_ge(loaded_down, 16)
                else:
                    pe.wait_ge(gelu_act, m)
                if e < EXPERTS:
                    layer_in(ps_g, "wg", e, None).then_inc(gate_pe, 1)
                else:
                    mm(ps_g[0][0:SIDE, :], side_g[:, :], hn_t[:, :], start=True, stop=True).then_inc(gate_pe, 1)

            def up(c, e):
                m = NETS * c + e
                if e:
                    pe.wait_ge(hidden_dve, m)
                else:
                    after(pe, tail_dve, c, "late")
                if e < EXPERTS:
                    layer_in(ps_u, "wu", e, None).then_inc(up_pe, 1)
                else:
                    mm(ps_u[0][0:SIDE, :], side_u[:, :], hn_t[:, :], start=True, stop=True).then_inc(up_pe, 1)

            def down(c, e):
                m = NETS * c + e
                pe.wait_ge(hidden_dve, m + 1)
                if c and e == 0:
                    after(pe, fin_dve, c - 1, "acc")
                if e < EXPERTS:
                    for f in range(2):
                        last = mm(ps_acc[:, :], wd[:, e, f, :], hidden[:, m % 2, f, :], start=(e == 0 and f == 0), stop=False)
                else:
                    last = mm(ps_acc[:, :], par_of("side_d")[0:SIDE, :], hidden[0:SIDE, m % 2, 0, :], start=False, stop=True)
                last.then_inc(down_pe, 1)

            def fin(c, k):
                after(pe, fin_act, c, "acc_t")
                for j in range(BLOCKS):
                    last = turn(block_of(ps_acc[:, :], j), acc_t[:, j * P:(j + 1) * P], ident)
                last.then_inc(fin_pe.sem, 1)

            setup()
            run(pre=pre, step=step, tail=tail, gate=gate, up=up, down=down, fin=fin)

        @block.scalar
        def _(act):
            def do(marks, out_, in_, func, **kw):
                nc.scalar.activation(out_, in_, func, **kw).then_inc(marks.sem, 1)

            def copy(marks, out_, in_, **kw):
                nc.scalar.copy(out_, in_, **kw).then_inc(marks.sem, 1)

            def setup():
                act.wait_ge(loaded_first, 16)
                do(setup_act, decay_rate[:, :, :], par_of("a_log").rearrange("p (h n) -> p h n", h=HALVES), ACT.Exp)
                act.wait_ge(loaded_rest, 16)
                do(setup_act, l1_rate[:, :], par_of("l1_a_log")[0:STATE, :], ACT.Exp)
                for h in range(HALVES):
                    after(act, setup_pe, 0, f"conv{h}")
                    copy(setup_act, conv_proj[:, h, :, :], ps_h[h][:, :].rearrange("p (k d) -> p k d", k=TAPS))

            def pre(c, k):
                q = c % 2
                if k == 0:
                    for h in range(HALVES):
                        after(act, pre_pe, c, f"conv{h}")
                        if c and h == 0:
                            after(act, pre_dve, c - 1, "du1")
                            after(act, pre_pe, c - 1, "skip1")
                        do(pre_act, u[:, h, :], ps_pre[:, :], ACT.Silu, bias=conv_b[:, h:h + 1])
                if k == 1:
                    for g in range(2):
                        after(act, pre_pe, c, f"res{g}")
                        if c >= 2 and g == 0:
                            after(act, tail_dve, c - 2, "yg")
                        do(pre_act, res_gate[:, q, 2 * g:2 * g + 2, :],
                           ps_pre[:, :].rearrange("p (j d) -> p j d", j=2), ACT.Silu)
                if k == 2:
                    after(act, pre_pe, c, "low")
                    if c >= 2:
                        act.wait_ge(rows_out, 16 * (c - 1))
                    copy(pre_act, low[:, q, :], ps_pre[0:RANK + STATE, :])
                if k == 3:
                    after(act, pre_pe, c, "crows")
                    if c >= 2:
                        act.wait_ge(y_dve, 2 * STATE * (c - 1))
                    copy(pre_act, c_rows[:, q, :, :], ps_pre[:, 0:BLOCKS * STATE].rearrange("p (j n) -> p j n", j=BLOCKS))
                if k == 4:
                    for h in range(HALVES):
                        after(act, pre_pe, c, f"dt{h}")
                        do(pre_act, sp_abs[:, h, :], ps_pre[:, :], ACT.Abs, bias=dt_b[:, h:h + 1])
                        if c and h == 0:
                            after(act, pre_dve, c - 1, "delta1")
                        do(pre_act, sp_relu[:, h, :], ps_pre[:, :], ACT.Relu, bias=dt_b[:, h:h + 1])
                    for h in range(HALVES):
                        after(act, pre_act, c, f"abs{h}")
                        do(pre_act, sp_exp[:, h, :], sp_abs[:, h, :], ACT.Exp, scale=-1.0)
                    for h in range(HALVES):
                        after(act, pre_act, c, f"exp{h}")
                        do(pre_act, sp_ln[:, h, :], sp_exp[:, h, :], ACT.Ln, bias=1.0)
                if k == 5:
                    for g in range(2):
                        after(act, pre_pe, c, f"skip{g}")
                        if c >= 2 and g == 0:
                            after(act, tail_pe, c - 2, "yg1")
                        copy(pre_act, y[:, q, 2 * g:2 * g + 2, :], ps_pre[:, :].rearrange("p (j d) -> p j d", j=2))

            def step(c, n):
                g = c * STATE + n
                if n == 0:
                    after(act, pre_dve, c, "delta1")
                if g == 0:
                    after(act, setup_dve, 0, "rate")
                if g >= RING:
                    act.wait_ge(state_dve, 2 * (g - RING) + 2)
                for h in range(HALVES):
                    nc.scalar.activation(decay[:, g % RING, h, :], delta[:, c % 2, h, :], ACT.Exp,
                                         scale=decay_rate[:, h, n:n + 1]).then_inc(decay_act, 1)

            def tail(c, k):
                if k == 0:
                    if c:
                        act.wait_ge(down_pe, NETS * c)
                    for h in range(HALVES):
                        after(act, tail_pe, c, f"yg{h}")
                        copy(tail_act, yg_t[:, h, :], (ps_g[0], ps_u[0])[h][:, :])
                if k == 1:
                    after(act, tail_dve, c, "sh1")
                    for j in range(BLOCKS):
                        last = nc.scalar.activation(x1[:, j, :], block_of(ps_u[1][:, :], j), ACT.Identity,
                                                    bias=shift[:, j:j + 1], scale=rstd[:, j:j + 1])
                    last.then_inc(tail_act.sem, 1)
                if k == 2:
                    after(act, tail_pe, c, "x1t")
                    copy(tail_act, x1_q[:, :], ps_g[1][:, :], saturate=False)
                    after(act, tail_pe, c, "ffn")
                    copy(tail_act, ffn_out[:, :, :], blocks_of(ps_u[0][:, :]))
                if k == 3:
                    after(act, tail_dve, c, "sh2")
                    for j in range(BLOCKS):
                        last = nc.scalar.activation(x2[:, j, :], r2[:, j, :], ACT.Identity,
                                                    bias=shift[:, j:j + 1], scale=rstd[:, j:j + 1])
                    last.then_inc(tail_act.sem, 1)
                if k == 4:
                    after(act, tail_pe, c, "x2t")
                    copy(tail_act, x2_t[:, :], ps_g[0][:, :])
                    after(act, tail_pe, c, "dlt")
                    do(tail_act, l1_abs[:, :], ps_u[0][:, :], ACT.Abs, bias=par_of("l1_delta_b"))
                    do(tail_act, l1_relu[:, :], ps_u[0][:, :], ACT.Relu, bias=par_of("l1_delta_b"))
                    after(act, tail_act, c, "abs")
                    do(tail_act, l1_exp[:, :], l1_abs[:, :], ACT.Exp, scale=-1.0)
                    after(act, tail_act, c, "exp")
                    do(tail_act, l1_ln[:, :], l1_exp[:, :], ACT.Ln, bias=1.0)
                if k == 5:
                    after(act, tail_pe, c, "mean")
                    copy(tail_act, l1_step[:, :], ps_g[1][0:STATE, :])
                    do(tail_act, l1_decay[:, :], ps_g[1][0:STATE, :], ACT.Exp, scale=l1_rate[:, :])
                if k == 6:
                    after(act, tail_dve, c, "sh3")
                    for j in range(BLOCKS):
                        last = nc.scalar.activation(x3[:, j, :], block_of(ps_g[0][:, :], j), ACT.Identity,
                                                    bias=shift[:, j:j + 1], scale=rstd[:, j:j + 1])
                    last.then_inc(tail_act.sem, 1)
                    after(act, tail_dve, c, "f3")
                    for j in range(BLOCKS):
                        last = nc.scalar.activation(hn[:, j, :], block_of(ps_g[0][:, :], j), ACT.Identity,
                                                    bias=shift3[:, j:j + 1], scale=scale3[:, j:j + 1])
                    last.then_inc(tail_act.sem, 1)
                    after(act, tail_pe, c, "hnt")
                    copy(tail_act, hn_t[:, :], ps_u[0][:, :])
                    copy(tail_act, hn_parts[0][:, :], ps_u[0][:, :])
                if k == 7:
                    after(act, tail_dve, c, "cen")
                    do(tail_act, exps[:, :, :], centred[:, :, :], ACT.Exp)
                if k == 8:
                    after(act, tail_pe, c, "wt")
                    if c:
                        act.wait_ge(weights_out, 16 * c)
                    copy(tail_act, weight_t[:, :], ps_g[1][0:NETS, :])

            def gate(c, e):
                m = NETS * c + e
                act.wait_ge(gate_pe, m + 1)
                if m >= GROUP:
                    act.wait_ge(hidden_dve, m - GROUP + 1)
                if e < EXPERTS:
                    for f in range(2):
                        last = nc.scalar.activation(gelu[:, m % GROUP, f, :], ps_g[f][:, :], ACT.Gelu)
                else:
                    last = nc.scalar.activation(gelu[0:SIDE, m % GROUP, 0, :], ps_g[0][0:SIDE, :], ACT.Gelu)
                last.then_inc(gelu_act, 1)

            def fin(c, k):
                act.wait_ge(down_pe, NETS * (c + 1))
                copy(fin_act, acc_t[:, :], ps_acc[:, :])
                after(act, fin_dve, c, "sh")
                if c:
                    act.wait_ge(stored, 16 * c)
                for j in range(BLOCKS):
                    last = nc.scalar.activation(result[:, j, :], acc[:, j, :], ACT.Identity,
                                                bias=shift4[:, j:j + 1], scale=rstd4[:, j:j + 1])
                last.then_inc(fin_act.sem, 1)

            setup()
            run(lead=LEAD, pre=pre, step=step, tail=tail, gate=gate, fin=fin)

        @block.gpsimd
        def _(pool):
            nc.gpsimd.memset(minus_half[:, :], -0.5).then_inc(pool_const, 1)
            nc.gpsimd.memset(mean_w[:, :], 1.0 / P).then_inc(pool_const, 1)
            pool.wait_ge(pool_const, 2)

            def step(c, n):
                g = c * STATE + n
                if n == 0:
                    after(pool, pre_dve, c, "du1")
                pool.wait_ge(rows_in[g // 2 % 2], 16 * (g // 4 + 1))
                if g >= RING:
                    pool.wait_ge(state_dve, 2 * (g - RING) + 2)
                nc.gpsimd.tensor_tensor(drive[:, g % RING, :, :], du[:, c % 2, :, :],
                                        b_row[:, g // 2 % 2, n % 2:n % 2 + 1, :].broadcast_to([P, HALVES, CHUNK]),
                                        ALU.mult).then_inc(drive_pool, 1)

            def rsqrt(marks, c, v, in_, eps, in_name, in_marks, out_, scratch):
                after(pool, in_marks, c, in_name)
                nc.gpsimd.tensor_scalar(scratch[:, :], in_, 1.0, eps, ALU.mult, ALU.add).then_inc(marks.sem, 1)
                after(pool, marks, c, v)
                nc.gpsimd.tensor_tensor(out_, scratch[:, :], minus_half[:, :], ALU.pow).then_inc(marks.sem, 1)

            def tail(c, k):
                if k == 1:
                    rsqrt(tail_pool, c, "v1", moments[:, :, 1], LN_EPS, "mo1", tail_dve, rstd[:, :], var_eps)
                if k == 2:
                    after(pool, tail_act, c, "x1")
                    nc.gpsimd.tensor_tensor(x1_bias[:, :, :], x1[:, :, :],
                                            par_of("ffn_b")[:, None, :].broadcast_to([P, BLOCKS, P]),
                                            ALU.add).then_inc(tail_pool.sem, 1)
                if k == 3:
                    rsqrt(tail_pool, c, "v2", moments[:, :, 1], LN_EPS, "mo2", tail_dve, rstd[:, :], var_eps)
                if k == 6:
                    rsqrt(tail_pool, c, "v3", moments[:, :, 1], LN_EPS, "mo3", tail_dve, rstd[:, :], var_eps)
                    rsqrt(tail_pool, c, "v4", mean_sq[:, :], RMS_EPS, "msq", tail_dve, rms[:, :], var_eps)

            def gate(c, e):
                m = NETS * c + e
                pool.wait_ge(gelu_act, m + 1)
                pool.wait_ge(weights_in, 16 * (m // GROUP + 1))
                part = gelu[:, m % GROUP, :, :] if e < EXPERTS else gelu[0:SIDE, m % GROUP, 0:1, :]
                row = weight_row[0:part.shape[0], m % GROUP:m % GROUP + 1, :]
                nc.gpsimd.tensor_tensor(part, part, row.broadcast_to(list(part.shape)), ALU.mult).then_inc(weighted_pool, 1)

            def fin(c, k):
                rsqrt(fin_pool, c, "v", moments4[:, :, 1], LN_EPS, "mo", fin_dve, rstd4[:, :], var_eps4)

            run(step=step, tail=tail, up=gate, fin=fin)

        @block.vector
        def _(dve):
            v = nc.vector

            def do(marks, ins):
                ins.then_inc(marks.sem, 1)

            def own(marks, c, name):
                dve.wait_ge(marks.sem, marks.done(c, name))

            def setup():
                dve.wait_ge(loaded_first, 16)
                for h in range(HALVES):
                    for k in range(TAPS):
                        i = h * TAPS + k
                        last = v.tensor_scalar(conv_diag[:, h, k, :], ident, conv_w[:, i:i + 1], None, ALU.mult)
                do(setup_dve, last)
                do(setup_dve, v.memset(x_in[:, :, 0:TAPS - 1], 0.0))
                for h in range(HALVES):
                    last = v.tensor_scalar(skip_diag[:, h, :], ident, skip[:, h:h + 1], None, ALU.mult)
                do(setup_dve, last)
                dve.wait_ge(loaded_rest, 16)
                after(dve, setup_act, 0, "l1_exp")
                v.tensor_scalar(l1_rate[:, :], l1_rate[:, :], -1.0, None, ALU.mult)
                do(setup_dve, v.tensor_scalar(decay_rate[:, :, :], decay_rate[:, :, :], -1.0, None, ALU.mult))
                do(setup_dve, v.memset(ones[:, :], 1.0))
                w = par_of("ffn_w")
                do(setup_dve, v.tensor_scalar(ffn_t[:, :], w, 128.0, -128.0, ALU.min, ALU.max))
                own(setup_dve, 0, "clip")
                do(setup_dve, v.tensor_copy(ffn_small[:, :], ffn_t[:, :], saturate=False))
                do(setup_dve, v.tensor_scalar(ffn_t2[:, :], w, 448.0, -448.0, ALU.min, ALU.max))
                own(setup_dve, 0, "clip_half")
                do(setup_dve, v.tensor_scalar(ffn_half[:, :], ffn_t2[:, :], 0.5, None, ALU.mult, saturate=False))
                own(setup_dve, 0, "half_a")
                do(setup_dve, v.tensor_scalar(ffn_big[:, :], ffn_half[:, :], 2.0, None, ALU.mult))
                do(setup_dve, v.tensor_copy(ffn_t[:, :], ffn_small[:, :]))
                do(setup_dve, v.tensor_tensor(ffn_t3[:, :], ffn_t2[:, :], ffn_t2[:, :], ALU.mult))
                own(setup_dve, 0, "mask")
                do(setup_dve, v.tensor_tensor(ffn_big[:, :], ffn_big[:, :], ffn_t[:, :], ALU.subtract))
                own(setup_dve, 0, "diff")
                do(setup_dve, v.scalar_tensor_tensor(ffn_t3[:, :], ffn_t3[:, :], 4096.0, ffn_big[:, :], ALU.is_ge, ALU.mult))
                own(setup_dve, 0, "mix")
                do(setup_dve, v.tensor_tensor(ffn_q[:, :], ffn_t3[:, :], ffn_t[:, :], ALU.add))
                do(setup_dve, v.tensor_copy(before[:, :], par_of("before")))
                do(setup_dve, v.scalar_tensor_tensor(l1_diag[:, :], ident, par_of("l1_d"), ident, ALU.mult, ALU.add))
                do(setup_dve, v.tensor_scalar(side_g[:, :], par_of("side_g"), par_of("f_norm"), None, ALU.mult))
                do(setup_dve, v.tensor_scalar(side_u[:, :], par_of("side_u"), par_of("f_norm"), None, ALU.mult))
                v.memset(picked_before[:, :], 0.0)
                v.memset(picked_sum[:, :], 0.0)

            def split(e):
                norm = par_of("norm_w")[:, e:e + 1]
                for i, (kind, loaded) in enumerate((("wg", loaded_gate), ("wu", loaded_up))):
                    dve.wait_ge(loaded, 16)
                    high, low_part = (x[:, e, :] for x in w_in[kind])
                    v.tensor_scalar(high, w_loaded[kind][:, e, :], norm, None, ALU.mult).then_inc(split_dve, 1)
                    dve.wait_ge(split_dve, 4 * e + 2 * i + 1)
                    v.scalar_tensor_tensor(low_part, w_loaded[kind][:, e, :], norm, high, ALU.mult,
                                           ALU.subtract).then_inc(split_dve, 1)

            def pre(c, k):
                q = c % 2
                if k == 4:
                    after(dve, pre_act, c, "ln1")
                    if c >= 2:
                        dve.wait_ge(decay_act, 2 * STATE * (c - 1))
                    for h in range(HALVES):
                        do(pre_dve, v.tensor_scalar(delta[:, q, h, :], sp_exp[:, h, :], 1.0, -1.0, ALU.add, ALU.add))
                        own(pre_dve, c, f"t{h}")
                        do(pre_dve, v.tensor_tensor(delta[:, q, h, :], sp_ln[:, h, :], delta[:, q, h, :], ALU.subtract))
                        own(pre_dve, c, f"a{h}")
                        do(pre_dve, v.tensor_tensor(delta[:, q, h, :], delta[:, q, h, :], sp_exp[:, h, :], ALU.add))
                    for h in range(HALVES):
                        own(pre_dve, c, f"b{h}")
                        do(pre_dve, v.tensor_tensor(delta[:, q, h, :], delta[:, q, h, :], sp_relu[:, h, :], ALU.add))
                if k == 5:
                    if c >= 2:
                        dve.wait_ge(drive_pool, STATE * (c - 1))
                    for h in range(HALVES):
                        own(pre_dve, c, f"delta{h}")
                        do(pre_dve, v.tensor_tensor(du[:, q, h, :], delta[:, q, h, :], u[:, h, :], ALU.mult))

            def add_y(g):
                c, n = divmod(g, STATE)
                if n == 0:
                    after(dve, pre_act, c, "y1")
                else:
                    dve.wait_ge(y_dve, 2 * g)
                for i in range(2):
                    dve.wait_ge(turned_pe, 2 * g + i + 1)
                    for jj in range(2):
                        j = 2 * i + jj
                        last = v.scalar_tensor_tensor(y[:, c % 2, j, :], ps_h[i][:, jj * INNER:(jj + 1) * INNER],
                                                      c_rows[:, c % 2, j, n:n + 1], y[:, c % 2, j, :], ALU.mult, ALU.add)
                    last.then_inc(y_dve, 1)

            def step(c, n):
                g = c * STATE + n
                first = c % PER_BATCH == 0
                dve.wait_ge(drive_pool, g + 1)
                cc, nn = divmod(g - 2, STATE)
                if g >= 2 and cc % PER_BATCH == 0:
                    dve.wait_ge(carry_dve, (cc // PER_BATCH) * STATE + nn + 1)
                for h in range(HALVES):
                    dve.wait_ge(decay_act, 2 * g + h + 1)
                    if not first:
                        dve.wait_ge(carry_dve, (c // PER_BATCH) * STATE + n + 1)
                    v.tensor_tensor_scan(state[:, g % 2, h, :], decay[:, g % RING, h, :], drive[:, g % RING, h, :],
                                         0.0 if first else carry[:, h, n:n + 1], ALU.mult, ALU.add).then_inc(state_dve, 1)
                if g:
                    add_y(g - 1)
                if c == 0 and n % 2 == 0:
                    split(n // 2)
                if first:
                    dve.wait_ge(state_dve, 2 * g + 2)
                    v.tensor_copy(carry[:, :, n:n + 1], state[:, g % 2, :, CHUNK - 1:CHUNK]).then_inc(carry_dve, 1)

            def flush(c, k):
                add_y(STEPS - 1)

            def layer_norm_stats(marks, c, of, st, mo):
                for j in range(BLOCKS):
                    last = v.bn_stats(stats[:, j, :], of(j))
                do(marks, last)
                own(marks, c, st)
                for j in range(BLOCKS):
                    last = v.bn_aggr(moments[:, j, :], stats[:, j, :])
                do(marks, last)

            def layer_norm_shift(marks, pool_marks, c, r, sh):
                after(dve, pool_marks, c, r)
                do(marks, v.scalar_tensor_tensor(shift[:, :], moments[:, :, 0], -1.0, rstd[:, :], ALU.mult, ALU.mult))

            def each(ap):
                return ap[:, :, None].broadcast_to([P, BLOCKS, EXPERTS])

            def tail(c, k):
                q = c % 2
                if k == 0:
                    dve.wait_ge(y_dve, 2 * STATE * (c + 1))
                    do(tail_dve, v.tensor_tensor(y[:, q, :, :], y[:, q, :, :], res_gate[:, q, :, :], ALU.mult))
                if k == 1:
                    after(dve, tail_pe, c, "r1")
                    layer_norm_stats(tail_dve, c, lambda j: block_of(ps_u[1][:, :], j), "st1", "mo1")
                    layer_norm_shift(tail_dve, tail_pool, c, "rstd1", "sh1")
                if k == 3:
                    after(dve, tail_act, c, "ffn")
                    after(dve, tail_pool, c, "bias")
                    do(tail_dve, v.tensor_tensor(r2[:, :, :], ffn_out[:, :, :], x1_bias[:, :, :], ALU.add))
                    own(tail_dve, c, "r2")
                    layer_norm_stats(tail_dve, c, lambda j: r2[:, j, :], "st2", "mo2")
                    layer_norm_shift(tail_dve, tail_pool, c, "rstd2", "sh2")
                if k == 4:
                    after(dve, tail_act, c, "ln")
                    do(tail_dve, v.tensor_scalar(l1_t[:, :], l1_exp[:, :], 1.0, -1.0, ALU.add, ALU.add))
                    own(tail_dve, c, "t")
                    do(tail_dve, v.tensor_tensor(l1_t[:, :], l1_ln[:, :], l1_t[:, :], ALU.subtract))
                    own(tail_dve, c, "a")
                    do(tail_dve, v.tensor_tensor(l1_t[:, :], l1_t[:, :], l1_exp[:, :], ALU.add))
                    own(tail_dve, c, "b")
                    do(tail_dve, v.tensor_tensor(l1_sp[:, :], l1_t[:, :], l1_relu[:, :], ALU.add))
                if k == 5:
                    after(dve, tail_act, c, "decay")
                    do(tail_dve, v.tensor_tensor(l1_drive[:, :], l1_step[:, :], ps_u[1][0:STATE, :], ALU.mult))
                    own(tail_dve, c, "drive")
                    first = c % PER_BATCH == 0
                    do(tail_dve, v.tensor_tensor_scan(l1_state[:, q, :], l1_decay[:, :], l1_drive[:, :],
                                                      0.0 if first else l1_state[:, 1 - q, CHUNK - 1:CHUNK],
                                                      ALU.mult, ALU.add))
                if k == 6:
                    after(dve, tail_pe, c, "r3")
                    layer_norm_stats(tail_dve, c, lambda j: block_of(ps_g[0][:, :], j), "st3", "mo3")
                    after(dve, tail_pool, c, "rstd3")
                    do(tail_dve, v.tensor_tensor(mean_sq[:, :], moments[:, :, 1], rstd[:, :], ALU.mult))
                    own(tail_dve, c, "vr")
                    do(tail_dve, v.tensor_tensor(mean_sq[:, :], mean_sq[:, :], rstd[:, :], ALU.mult))
                    do(tail_dve, v.scalar_tensor_tensor(shift[:, :], moments[:, :, 0], -1.0, rstd[:, :], ALU.mult, ALU.mult))
                    after(dve, tail_pool, c, "rms")
                    own(tail_dve, c, "sh3")
                    do(tail_dve, v.scalar_tensor_tensor(rms_inv[:, :], mean_sq[:, :], RMS_EPS, rms[:, :], ALU.add, ALU.mult))
                    do(tail_dve, v.tensor_tensor(scale3[:, :], rstd[:, :], rms[:, :], ALU.mult))
                    do(tail_dve, v.tensor_tensor(shift3[:, :], shift[:, :], rms[:, :], ALU.mult))
                    after(dve, tail_act, c, "hi")
                    do(tail_dve, v.tensor_tensor(hn_parts[1][:, :], ps_u[0][:, :], hn_parts[0][:, :], ALU.subtract))
                if k == 7:
                    after(dve, tail_pe, c, "logits")
                    do(tail_dve, v.tensor_tensor(logits[:, :, :], ps_g[1][:, 0:BLOCKS * EXPERTS].rearrange(
                        "p (j e) -> p j e", j=BLOCKS), each(rms_inv), ALU.mult))
                    own(tail_dve, c, "lg")
                    do(tail_dve, v.tensor_reduce(top[:, :], logits[:, :, :], AX.X, ALU.max))
                    own(tail_dve, c, "top")
                    do(tail_dve, v.tensor_tensor(centred[:, :, :], logits[:, :, :], each(top), ALU.subtract))
                    after(dve, tail_act, c, "exps")
                    do(tail_dve, v.tensor_reduce(total[:, :], exps[:, :, :], AX.X, ALU.add))
                    own(tail_dve, c, "tot")
                    do(tail_dve, v.reciprocal(total_inv[:, :], total[:, :]))
                    own(tail_dve, c, "tinv")
                    do(tail_dve, v.tensor_tensor(probs[:, :, :], exps[:, :, :], each(total_inv), ALU.mult))
                    own(tail_dve, c, "probs")
                    for j in range(BLOCKS):
                        last = v.max(sorted8[:, j, :], probs[:, j, :])
                    do(tail_dve, last)
                    own(tail_dve, c, "sort")
                    for j in range(BLOCKS):
                        last = v.max_index(where8[:, j, :], sorted8[:, j, :], probs[:, j, :])
                    do(tail_dve, last)
                    own(tail_dve, c, "where")
                    do(tail_dve, v.tensor_copy(where_f[:, :, :], where8[:, :, :]))
                    own(tail_dve, c, "wf")
                    index = par_of("index")[:, None, :].broadcast_to([P, BLOCKS, EXPERTS])
                    for pick, i in ((pick1, 0), (pick2, 1)):
                        do(tail_dve, v.tensor_tensor(pick[:, :, :], index,
                                                     where_f[:, :, i:i + 1].broadcast_to([P, BLOCKS, EXPERTS]), ALU.is_equal))
                    own(tail_dve, c, "p2")
                    do(tail_dve, v.tensor_tensor(picked[:, :, :], pick1[:, :, :], pick2[:, :, :], ALU.add))
                if k == 8:
                    after(dve, tail_pe, c, "counts")
                    own(tail_dve, c, "picked")
                    counts = ps_u[1][:, 0:BLOCKS * EXPERTS].rearrange("p (j e) -> p j e", j=BLOCKS)
                    do(tail_dve, v.scalar_tensor_tensor(late[:, :, :], counts, float(CAPACITY), picked[:, :, :],
                                                        ALU.is_ge, ALU.mult))
                    own(tail_dve, c, "late")
                    do(tail_dve, v.tensor_reduce(overflow, late[:, :, :], AX.X, ALU.max))
                    own(tail_dve, c, "over")
                    do(tail_dve, v.tensor_scalar(kept[:, :], overflow, -1.0, 1.0, ALU.mult, ALU.add))
                    do(tail_dve, v.tensor_tensor(weight0[:, :, :], probs[:, :, :], picked[:, :, :], ALU.mult))
                    own(tail_dve, c, "w0")
                    do(tail_dve, v.tensor_tensor(weight, weight0[:, :, :], each(kept), ALU.mult))
                    own(tail_dve, c, "w")
                    do(tail_dve, v.tensor_reduce(weight_sum[:, :], weight, AX.X, ALU.add))
                    own(tail_dve, c, "wsum")
                    do(tail_dve, v.tensor_scalar(x_weight[:, :], weight_sum[:, :], 2.0, None, ALU.add))
                    do(tail_dve, v.tensor_reduce(picked_new[:, :], picked[:, :, :].rearrange("p j e -> p e j"), AX.X, ALU.add))
                    own(tail_dve, c, "red")
                    do(tail_dve, v.tensor_tensor(picked_sum[:, :], picked_sum[:, :], picked_new[:, :], ALU.add))
                    own(tail_dve, c, "psum")
                    do(tail_dve, v.tensor_copy(picked_before[:, :], picked_sum[:, :]))

            def join(c, e):
                m = NETS * c + e
                dve.wait_ge(up_pe, m + 1)
                dve.wait_ge(weighted_pool, m + 1)
                if m >= 2:
                    dve.wait_ge(down_pe, m - 1)
                for f in range(2 if e < EXPERTS else 1):
                    w = P if e < EXPERTS else SIDE
                    last = v.tensor_tensor(hidden[0:w, m % 2, f, :], gelu[0:w, m % GROUP, f, :], ps_u[f][0:w, :], ALU.mult)
                last.then_inc(hidden_dve, 1)

            def fin(c, k):
                after(dve, fin_pe, c, "acc")
                for j in range(BLOCKS):
                    last = v.scalar_tensor_tensor(acc[:, j, :], x3[:, j, :], x_weight[:, j:j + 1],
                                                  block_of(ps_acc[:, :], j), ALU.mult, ALU.add)
                do(fin_dve, last)
                own(fin_dve, c, "acc")
                for j in range(BLOCKS):
                    last = v.bn_stats(stats4[:, j, :], acc[:, j, :])
                do(fin_dve, last)
                own(fin_dve, c, "st")
                for j in range(BLOCKS):
                    last = v.bn_aggr(moments4[:, j, :], stats4[:, j, :])
                do(fin_dve, last)
                after(dve, fin_pool, c, "rstd")
                do(fin_dve, v.scalar_tensor_tensor(shift4[:, :], moments4[:, :, 0], -1.0, rstd4[:, :], ALU.mult, ALU.mult))

            setup()
            run(pre=pre, step=step, tail=tail, join=join, fin=fin, flush=flush)


def kernel(**inputs):
    import numpy as np
    import concourse.bacc as bacc
    from concourse.bass_utils import run_bass_kernel_spmd

    a = {k: np.asarray(v) for k, v in inputs.items()}

    def halves(w):
        return w.reshape(HALVES, P, -1).transpose(1, 0, 2).reshape(P, -1)

    def padded(w):
        return np.concatenate([w, np.zeros((P - w.shape[0], w.shape[1]), w.dtype)])

    in_w = a["L0_attn_in_proj_w"]
    columns = {
        "ident": np.eye(P, dtype=np.float32),
        "conv_w": halves(a["L0_attn_conv_w"].reshape(INNER, TAPS)),
        "conv_b": halves(a["L0_attn_conv_b"]),
        "dt_b": halves(a["L0_attn_dt_proj_b"]),
        "a_log": halves(a["L0_attn_A_log"]),
        "skip": halves(a["L0_attn_Dp"]),
        "in_x": halves(in_w[:INNER]),
        "in_res": in_w[INNER:].T,
        "x_proj": halves(a["L0_attn_x_proj_w"].T),
        "dt_proj": padded(a["L0_attn_dt_proj_w"].T),
        "out_proj": halves(a["L0_attn_out_proj_w"].T),
        "ffn_w": a["L0_ffn_weight"].T,
        "ffn_b": np.broadcast_to(a["L0_ffn_bias"], (P, P)),
        "l1_b": a["L1_attn_B"].T,
        "l1_c": padded(a["L1_attn_C"].T),
        "l1_d": a["L1_attn_D"][:, None],
        "l1_delta": a["L1_attn_W_delta"].T,
        "l1_delta_b": a["L1_attn_b_delta"][:, None],
        "l1_a_log": padded(a["L1_attn_A_log"][:, None]),
        "router": a["L1_ffn_Wr"],
        "norm_w": a["L1_ffn_norm_w"].T,
        "f_norm": a["L1_ffn_f_norm"][:, None],
        "side_g": a["L1_ffn_fWg"],
        "side_u": a["L1_ffn_fWu"],
        "side_d": padded(a["L1_ffn_fWd"]),
        "before": np.triu(np.ones((P, P), np.float32), 1),
        "index": np.broadcast_to(np.arange(EXPERTS, dtype=np.float32), (P, EXPERTS)),
    }
    assert list(columns) == list(PARAMS) and all(columns[k].shape == (P, w) for k, w in PARAMS.items())
    arrays = {
        "x_t": np.ascontiguousarray(a["L0_attn_x"].reshape(TOKENS, P).T),
        "params": np.ascontiguousarray(np.concatenate(list(columns.values()), axis=1)),
        "w_gate": np.ascontiguousarray(a["L1_ffn_Wg"].transpose(1, 0, 2)),
        "w_up": np.ascontiguousarray(a["L1_ffn_Wu"].transpose(1, 0, 2)),
        "w_down": np.ascontiguousarray(a["L1_ffn_Wd"].reshape(EXPERTS, 2, P, P).transpose(2, 0, 1, 3)),
    }
    nc = bacc.Bacc("TRN2", target_bir_lowering=False, num_devices=1)
    ins = [nc.dram_tensor(k, w.shape, F32, kind="ExternalInput").ap() for k, w in arrays.items()]
    ins += [nc.dram_tensor("b_dram", (2, STATE, CHUNK), F32, kind="Internal").ap(),
            nc.dram_tensor("weight_dram", (NETS, CHUNK), F32, kind="Internal").ap()]
    out = nc.dram_tensor("out", (TOKENS, P), F32, kind="ExternalOutput").ap()
    build(nc, *ins, out)
    got = run_bass_kernel_spmd(nc, [arrays], core_ids=[0]).results[0]["out"]
    return got.reshape(BATCH, LENGTH, P)
```

```python
from contextlib import ExitStack

import concourse.bass as bass
from concourse import mybir

F32 = mybir.dt.float32
F32R = mybir.dt.float32r
F16 = mybir.dt.float16
BF16 = mybir.dt.bfloat16
F8 = mybir.dt.float8e4
U32 = mybir.dt.uint32
ALU = mybir.AluOpType
ACT = mybir.ActivationFunctionType
AX = mybir.AxisListType

P = 128
BATCH, LENGTH = 2, 1024
TOKENS = BATCH * LENGTH
CHUNK = 512
BLOCKS = CHUNK // P
CHUNKS = TOKENS // CHUNK
PER_BATCH = LENGTH // CHUNK
HALVES = 2
INNER = HALVES * P
STATE = 16
RANK = 64
TAPS = 4
EXPERTS = 8
HIDDEN = 256
SIDE = 64
CAPACITY = 512
LN_EPS = 1e-5
RMS_EPS = 1e-6
RING = 5
STEPS = CHUNKS * STATE
LEAD = 2
GROUP = 3
NETS = EXPERTS + 1
EXP_LN = "natural_log_exp_and_others"

PARAMS = {
    "ident": P, "conv_w": HALVES * TAPS, "conv_b": HALVES, "dt_b": HALVES, "a_log": HALVES * STATE,
    "skip": HALVES, "in_x": HALVES * P, "in_res": INNER, "x_proj": HALVES * 96, "dt_proj": INNER,
    "out_proj": HALVES * P, "ffn_w": P, "ffn_b": P, "l1_b": STATE, "l1_c": P, "l1_d": 1, "l1_delta": P,
    "l1_delta_b": 1, "l1_a_log": 1, "router": EXPERTS, "norm_w": EXPERTS, "f_norm": 1,
    "side_g": SIDE, "side_u": SIDE, "side_d": P, "before": P, "index": EXPERTS,
}
AT, _n = {}, 0
for _k, _w in PARAMS.items():
    AT[_k] = (_n, _w)
    _n += _w
PARAM_COLS = _n
FIRST_COLS = AT["out_proj"][0]


STEP = tuple(range(STATE))
PLACES = {
    "sync": {
        "pre": (-15.5, -15, -14.75, -12.25, -11.25, -11.25, -11.25, -11),
        "step": tuple(n - 0.75 for n in STEP),
        "fin": (35.5,),
        "pre 1": (-15.5, -15, -14.5, -14, -13.25, -13.25, -13.25, -13.25),
    },
    "tensor": {
        "pre": (-15.5, -14.75, -14.5, -14.5, -14, -14, -13.5, -13.25),
        "skip": (0.85,),
        "finish": (3.5, 5.5, 7.5, 9.5, 11.5, 14.5, 15.5, 16.6),
        "tail": (17.5, 18.5, 19.1, 19.25, 20.25, 20.35, 20.5, 21.5, 22.25, 22.75, 23, 23, 23.5, 23.85, 24.25, 24.75),
        "gate": (24, 24, 24.5, 26.5, 28, 28.75, 29.25, 29.5, 30.25),
        "up": (24.5, 25.25, 25.75, 27.25, 28.25, 28.75, 29.75, 30.25, 31.25),
        "down": (25.25, 25.75, 26.75, 28.25, 29.25, 29.75, 30.75, 31.25, 32),
        "pre 1": (-15.5, -15, -14.5, -14.25, -14, -14, -13.25, -13.25),
        "tail 3": (17.5, 18.5, 19.1, 19.25, 20.35, 20.5, 20.75, 21.5, 22.25, 22.75, 23, 23, 23.5, 23.85, 24.25, 24.75),
        "gate 3": (24, 24, 24.75, 26.75, 27.75, 28.5, 28.5, 29.25, 30.25),
        "up 3": (24.5, 25.25, 25.5, 26.5, 28, 28.5, 29.5, 30, 30.75),
        "down 3": (25.25, 25.75, 26.5, 28, 29, 29.5, 30.5, 31, 31.5),
    },
    "scalar": {
        "pre": (-15.5, -15, -14.5, -14.5, -13.75, -13.5, -13.25, -13.25),
        "step": tuple(n - 1.5 for n in STEP),
        "tail": (17.5, 18, 18.75, 19.1, 19.5, 20, 20.1, 21.25, 22.25, 22.25, 22.25, 22.5, 23.5, 23.85, 24.25, 24.75),
        "gate": (24, 24.5, 24.75, 26.5, 28, 28.75, 29.25, 29.5, 30.25),
        "fin": (32.5, 33),
        "split": (-13.26, 0.2, 2.1, 4, 5.9, 7.8, 9.7, 11.6),
        "pre 1": (-15.5, -15, -14.25, -14.25, -13.75, -13.5, -13.25, -13.25),
        "tail 3": (17.5, 18, 18.75, 19.1, 20.1, 20.5, 20.5, 21.25, 22.25, 22.25, 22.25, 22.5, 23.5, 23.85, 24.25, 24.75),
        "gate 3": (24, 24.5, 25, 26.75, 27.75, 28.5, 28.5, 29.25, 30.25),
    },
    "gpsimd": {
        "du": (-2.5,),
        "step": tuple(n - 1.5 for n in STEP),
        "tail": (17, 18, 19.35, 19.5, 20.5, 20.5, 20.6, 21.5, 22.25, 22.75, 23, 23, 23.5, 23.85, 24.25, 24.75),
        "pair": (2.8, 4.8, 6.55, 8.8, 10.3, 12.3, 14.3, 15.8),
        "tail 3": (18, 19, 19.35, 19.5, 20.5, 20.6, 21, 21.5, 22.25, 22.75, 23, 23, 23.5, 23.85, 24.25, 24.75),
    },
    "vector": {
        "delta": (-11.5,),
        "step": STEP,
        "finish": (1.75, 2.75, 3.5, 4.5, 5.5, 6.5, 7.5, 8.5, 8.5, 9.5, 11.5, 12.5, 13.5, 14.5, 15.5, 16.2),
        "tail": (17.5, 18.5, 18.75, 19.1, 20, 20.1, 20.5, 21.5, 22.25, 22.75, 23, 23, 23.5, 23.85, 24.25, 24.75),
        "join": (25, 25.75, 26.25, 27.75, 28.5, 29, 30, 31, 31.75),
        "accum": (26, 26.75, 27.25, 28.75, 29.75, 30.25, 31.25, 31.75, 33),
        "fin": (33, 33.5),
        "split": (1.2, 3.1, 5, 6.9, 8.8, 10.7, 12.6, 14.5),
        "delta 1": (-11.25,),
        "tail 3": (17.5, 18.5, 18.75, 19.1, 20.1, 20.5, 20.5, 21.5, 22.25, 22.75, 23, 23, 23.5, 23.85, 24.25, 24.75),
        "join 3": (24.5, 25.25, 25.5, 27.5, 28.25, 28.75, 29.75, 30.75, 31.25),
        "accum 3": (26, 26.75, 27, 28.5, 29.5, 30, 31, 31.5, 32.5),
    },
}


class Marks:

    def __init__(self, sem, names):
        self.sem, self.names = sem, names.split()
        assert len(set(self.names)) == len(self.names)

    def done(self, c, name):
        return c * len(self.names) + self.names.index(name) + 1


def build(nc, x_t, params, w_gate, w_up, w_down, bc_dram, out):
    with ExitStack() as ctx:
        def sb(name, shape, dt=F32):
            return ctx.enter_context(nc.sbuf_tensor(name, shape, dt))

        def bank(name):
            return ctx.enter_context(nc.psum_tensor(name, [P, 512], F32))

        def sem(name):
            return ctx.enter_context(nc.semaphore(name))

        par = sb("par", [P, PARAM_COLS])

        def par_of(name):
            a, w = AT[name]
            return par[:, a:a + w]

        ident = par_of("ident")
        conv_w, conv_b, dt_b = par_of("conv_w"), par_of("conv_b"), par_of("dt_b")
        skip = par_of("skip")
        in_x = par_of("in_x").rearrange("p (h m) -> p h m", h=HALVES)
        in_res = par_of("in_res")
        x_proj = par_of("x_proj").rearrange("p (h m) -> p h m", h=HALVES)
        dt_proj = par_of("dt_proj")
        out_proj = par_of("out_proj").rearrange("p (h m) -> p h m", h=HALVES)
        x_in = sb("x_in", [P, BATCH, TAPS - 1 + LENGTH])
        w_in = {k: [sb(f"{k}{part}", [P, EXPERTS, HIDDEN], F32R) for part in range(2)] for k in ("wg", "wu")}
        wd = sb("wd", [P, EXPERTS, 2, P])
        conv_proj = sb("conv_proj", [P, HALVES, TAPS, P])
        skip_diag = sb("skip_diag", [P, HALVES, P])
        decay_rate = sb("decay_rate", [P, HALVES, STATE])
        l1_rate = sb("l1_rate", [STATE, 1])
        l1_diag = sb("l1_diag", [P, P])
        mean_w = sb("mean_w", [P, STATE])
        ffn_small = sb("ffn_small", [P, P], F8)
        ffn_half = sb("ffn_half", [P, P], F8)
        ffn_q = sb("ffn_q", [P, P], F16)
        before = sb("before", [P, P], BF16)
        ones = sb("ones", [P, P], BF16)
        eps = sb("eps", [P, 2])
        side_g = sb("side_g", [P, SIDE])
        side_u = sb("side_u", [P, SIDE])

        gelu = sb("gelu", [P, GROUP, 2, CHUNK])
        hidden = sb("hidden", [P, 2, 2, CHUNK])
        sp_relu = sb("sp_relu", [P, HALVES, CHUNK])
        acc = sb("acc", [P, BLOCKS, P])
        x1 = sb("x1", [P, BLOCKS, P])
        hn = x1
        conv_diag = sp_relu[:, :, :].rearrange("p h (k d) -> p h k d", k=TAPS)
        ffn_t, ffn_t2, ffn_t3, ffn_big = (acc[:, i, :] for i in range(4))
        w_loaded = {"wg": gelu[:, 0:2, :, :].rearrange("p r f (e n) -> p (r f e) n", n=HIDDEN),
                    "wu": hidden[:, :, :, :].rearrange("p r f (e n) -> p (r f e) n", n=HIDDEN)}
        l1_ln = l1_abs = gelu[:, 0, 0, :]
        l1_exp = gelu[:, 0, 1, :]
        l1_relu = gelu[:, 1, 0, :]
        l1_sp = l1_t = gelu[:, 1, 1, :]
        l1_step, l1_decay = gelu[0:STATE, 2, 0, :], gelu[0:STATE, 2, 1, :]
        l1_drive = hidden[0:STATE, 1, 0, :]

        u = sb("u", [P, HALVES, CHUNK])
        res_gate = sb("res_gate", [P, 2, HALVES, CHUNK])
        low = sb("low", [RANK + 2 * STATE, 2, CHUNK])
        sp_abs = sb("sp_abs", [P, HALVES, CHUNK])
        sp_exp = sb("sp_exp", [P, HALVES, CHUNK])
        sp_ln = sp_abs
        delta = sb("delta", [P, 2, HALVES, CHUNK])
        du = sb("du", [P, HALVES, CHUNK])
        b_row = sb("b_row", [P, 2, 2, CHUNK])
        c_row = sb("c_row", [P, 2, 2, CHUNK])
        decay = sb("decay", [P, RING, HALVES, CHUNK])
        drive = sb("drive", [P, RING, HALVES, CHUNK])
        state, product = drive, decay
        carry = sb("carry", [P, HALVES, STATE])
        stats = sb("stats", [P, BLOCKS, 6])
        moments = sb("moments", [P, BLOCKS, 2])
        var_log = sb("var_log", [P, BLOCKS])
        rstd = sb("rstd", [P, BLOCKS])
        shift = sb("shift", [P, BLOCKS])
        x1_bias = sb("x1_bias", [P, BLOCKS, P])
        x1_q = sb("x1_q", [P, CHUNK], F8)
        ffn_out = sb("ffn_out", [P, BLOCKS, P], F16)
        r2 = x2 = x1_bias
        x2_t = sb("x2_t", [P, CHUNK])
        l1_state = sb("l1_state", [STATE, 2, CHUNK])
        mean_sq = sb("mean_sq", [P, BLOCKS])
        rms = sb("rms", [P, BLOCKS])
        rms_inv = sb("rms_inv", [P, BLOCKS])
        scale3 = sb("scale3", [P, BLOCKS])
        shift3 = sb("shift3", [P, BLOCKS])
        x3 = sb("x3", [P, BLOCKS, P])
        hn_t = sb("hn_t", [P, CHUNK])
        hn_parts = [sb(f"hn_part{part}", [P, CHUNK], F32R) for part in range(2)]
        logits = sb("logits", [P, BLOCKS, EXPERTS])
        top = sb("top", [P, BLOCKS])
        centred = sb("centred", [P, BLOCKS, EXPERTS])
        exps = sb("exps", [P, BLOCKS, EXPERTS])
        total = sb("total", [P, BLOCKS])
        total_inv = sb("total_inv", [P, BLOCKS])
        probs = sb("probs", [P, BLOCKS, EXPERTS])
        sorted8 = sb("sorted8", [P, BLOCKS, 8])
        where8 = sb("where8", [P, BLOCKS, 8], U32)
        where_f = sb("where_f", [P, BLOCKS, 8])
        pick1 = sb("pick1", [P, BLOCKS, EXPERTS])
        pick2 = sb("pick2", [P, BLOCKS, EXPERTS])
        picked = sb("picked", [P, BLOCKS, EXPERTS], BF16)
        picked_new = sb("picked_new", [P, EXPERTS])
        picked_sum = sb("picked_sum", [P, EXPERTS])
        picked_before = sb("picked_before", [P, EXPERTS], BF16)
        late = sb("late", [P, BLOCKS, EXPERTS])
        kept = sb("kept", [P, BLOCKS])
        weight0 = sb("weight0", [P, BLOCKS, EXPERTS])
        net_weight = sb("net_weight", [P, BLOCKS, NETS])
        weight, overflow = net_weight[:, :, 0:EXPERTS], net_weight[:, :, EXPERTS]
        weight_sum = sb("weight_sum", [P, BLOCKS])
        x_weight = sb("x_weight", [P, BLOCKS])
        stats4 = sb("stats4", [P, BLOCKS, 6])
        moments4 = sb("moments4", [P, BLOCKS, 2])
        var_log4 = sb("var_log4", [P, BLOCKS])
        rstd4 = sb("rstd4", [P, BLOCKS])
        shift4 = sb("shift4", [P, BLOCKS])
        result = sb("result", [P, BLOCKS, P])

        ps_pre = bank("ps_pre")
        ps_y = [bank("ps_y0"), bank("ps_y1")]
        ps_g = [bank("ps_g0"), bank("ps_g1")]
        ps_u = [bank("ps_u0"), bank("ps_u1")]
        ps_acc = bank("ps_acc")

        def pre_bank(c, k):
            return (*ps_g, *ps_u, ps_acc, ps_pre, ps_g[0])[k] if c == 0 else (ps_pre, ps_acc)[k % 2]

        LAST = CHUNKS - 1

        def out_bank(c, e):
            return ps_pre if c == LAST and e % 2 else ps_acc

        loaded_first = sem("loaded_first")
        loaded_x = [sem(f"loaded_x{c}") for c in range(CHUNKS)]
        loaded_rest = sem("loaded_rest")
        loaded_gate = sem("loaded_gate")
        loaded_up = sem("loaded_up")
        loaded_down = sem("loaded_down")
        stored = sem("stored")
        pool_const = sem("pool_const")
        setup_dve = Marks(sem("setup_dve"), "diag zero skip_diag rate ones clip small_a clip_half half_a "
                          "big small mask diff mix cast before l1_diag side_g side_u")
        setup_act = Marks(sem("setup_act"), "a_exp l1_exp conv0 conv1")
        setup_pe = Marks(sem("setup_pe"), "conv0 conv1")
        split_act = sem("split_act")
        split_dve = sem("split_dve")
        pre_pe = Marks(sem("pre_pe"), "conv0 conv1 res0 res1 low dt0 dt1")
        skip_pe = sem("skip_pe")
        pre_act = Marks(sem("pre_act"), "u0 u1 gate0 gate1 low abs0 relu0 abs1 relu1 exp0 exp1 ln0 ln1")
        pre_dve = Marks(sem("pre_dve"), "t0 t1 a0 a1 b0 b1 delta0 delta1")
        du_pool = sem("du_pool")
        rows_out = sem("rows_out")
        b_in = [sem(f"b_in{i}") for i in range(2)]
        c_in = [sem(f"c_in{i}") for i in range(2)]
        decay_act = sem("decay_act")
        drive_pool = sem("drive_pool")
        state_dve = sem("state_dve")
        carry_dve = sem("carry_dve")
        product_dve = sem("product_dve")
        pair_pool = sem("pair_pool")
        y_pe = sem("y_pe")
        tail_pe = Marks(sem("tail_pe"), "r1 x1t ffn x2t dlt bx mean r3 hnt logits counts")
        tail_act = Marks(sem("tail_act"), "l1 rstd1 x1 x1q ffn l2 rstd2 x2 x2t abs exp relu ln step decay "
                         "l3 rstd3 l4 rms hn hnt hi x3 exps acc")
        tail_dve = Marks(sem("tail_dve"), "yg0 yg1 st1 mo1 sh1 r2 st2 mo2 sh2 t a b sp drive scan st3 mo3 vr msq sh3 inv s3 "
                         "f3 lo lg top cen tot tinv probs sort where wf p1 p2 picked late over kept w0 w wsum xw red psum pbef")
        tail_pool = Marks(sem("tail_pool"), "bias")
        gate_pe = sem("gate_pe")
        gelu_act = sem("gelu_act")
        up_pe = sem("up_pe")
        hidden_dve = sem("hidden_dve")
        down_pe = sem("down_pe")
        acc_dve = sem("acc_dve")
        fin_act = Marks(sem("fin_act"), "l rstd result")
        fin_dve = Marks(sem("fin_dve"), "st mo sh")

        def after(eng, marks, c, name):
            eng.wait_ge(marks.sem, marks.done(c, name))

        def tokens(c):
            return c // PER_BATCH, c % PER_BATCH * CHUNK

        def block_of(ap, j):
            return ap[:, j * P:(j + 1) * P]

        def blocks_of(ap):
            return ap.rearrange("p (j d) -> p j d", j=BLOCKS)

        def run(engine, **parts):
            places = PLACES[engine]
            order = sorted((STATE * c + at, c, i, k) for i, kind in enumerate(parts)
                           for c in range(1 if kind == "split" else CHUNKS)
                           for k, at in enumerate(places.get(f"{kind} {c}", places[kind])))
            for i in range(len(parts)):
                mine = [(c, k) for _, c, j, k in order if j == i]
                assert mine == sorted(mine)
            kinds = list(parts.values())
            for _, c, i, k in order:
                kinds[i](c, k)

        block = ctx.enter_context(nc.Block())

        @block.sync
        def _(sp):
            sp.dma_start(par[:, 0:FIRST_COLS], params[:, 0:FIRST_COLS]).then_inc(loaded_first, 16)
            for c in range(CHUNKS):
                b, t0 = tokens(c)
                sp.dma_start(x_in[:, b, TAPS - 1 + t0:TAPS - 1 + t0 + CHUNK],
                             x_t[:, c * CHUNK:(c + 1) * CHUNK]).then_inc(loaded_x[c], 16)
                if c == 0:
                    sp.dma_start(par[:, FIRST_COLS:], params[:, FIRST_COLS:]).then_inc(loaded_rest, 16)
            sp.dma_start(w_loaded["wg"], w_gate).then_inc(loaded_gate, 16)
            sp.dma_start(w_loaded["wu"], w_up).then_inc(loaded_up, 16)
            sp.dma_start(wd[:], w_down).then_inc(loaded_down, 16)

            def pair(m, ring, arrived, row, used):
                c, n = divmod(2 * m, STATE)
                if m >= 2:
                    sp.wait_ge(used, 2 * (m - 2) + 2)
                if n == 0:
                    sp.wait_ge(rows_out, 16 * (c + 1))
                sp.dma_start(ring[:, m % 2, :, :],
                             bc_dram[c % 2, None, row + n:row + n + 2, :].broadcast_to([P, 2, CHUNK])).then_inc(arrived[m % 2], 16)

            def pre(c, k):
                if k == 4:
                    after(sp, pre_act, c, "low")
                    if c >= 2:
                        for i in range(2):
                            sp.wait_ge(b_in[i], 16 * STATE // 4 * (c - 1))
                            sp.wait_ge(c_in[i], 16 * STATE // 4 * (c - 1))
                    sp.dma_start(bc_dram[c % 2], low[RANK:RANK + 2 * STATE, c % 2, :]).then_inc(rows_out, 16)

            def step(c, n):
                g = c * STATE + n
                if g == 0:
                    pair(0, b_row, b_in, 0, drive_pool)
                    pair(0, c_row, c_in, STATE, product_dve)
                    pair(1, b_row, b_in, 0, drive_pool)
                if g % 2 == 0:
                    if g + 2 < STEPS:
                        pair(g // 2 + 1, c_row, c_in, STATE, product_dve)
                    if g + 4 < STEPS:
                        pair(g // 2 + 2, b_row, b_in, 0, drive_pool)

            def fin(c, k):
                after(sp, fin_act, c, "result")
                sp.dma_start(out[c * CHUNK:(c + 1) * CHUNK, :].rearrange("(j t) d -> t j d", j=BLOCKS),
                             result[:, :, :]).then_inc(stored, 16)

            run("sync", pre=pre, step=step, fin=fin)
            sp.wait_ge(stored, 16 * CHUNKS)

        @block.tensor
        def _(pe):
            mm, turn = nc.tensor.matmul, nc.tensor.transpose

            def setup():
                after(pe, setup_dve, 0, "diag")
                for h in range(HALVES):
                    for k in range(TAPS):
                        last = mm(block_of(ps_y[h][:, :], k), in_x[:, h, :], conv_diag[:, h, k, :], start=True, stop=True)
                    last.then_inc(setup_pe.sem, 1)

            def pre(c, k):
                if k == 7:
                    return
                q = c % 2
                b, t0 = tokens(c)
                bank_ = pre_bank(c, k)
                if k < 2:
                    if c == 0 and k == 0:
                        after(pe, setup_act, 0, "conv1")
                        after(pe, setup_dve, 0, "zero")
                    if c and k == 0:
                        after(pe, pre_act, c - 1, "relu1")
                    if c > 2 and k == 1:
                        pe.wait_ge(acc_dve, NETS * (c - 2))
                    pe.wait_ge(loaded_x[c], 16)
                    for tap in range(TAPS):
                        last = mm(bank_[:, :], conv_proj[:, k, tap, :], x_in[:, b, t0 + tap:t0 + tap + CHUNK],
                                  start=(tap == 0), stop=(tap == TAPS - 1))
                elif k < 4:
                    if c:
                        after(pe, pre_act, c, ("u0", "u1")[k - 2])
                    last = mm(bank_[:, :], block_of(in_res, k - 2), x_in[:, b, TAPS - 1 + t0:TAPS - 1 + t0 + CHUNK],
                              start=True, stop=True)
                elif k == 4:
                    after(pe, pre_act, c, "gate0" if c else "u1")
                    for h in range(HALVES):
                        last = mm(bank_[0:RANK + 2 * STATE, :], x_proj[:, h, :], u[:, h, :],
                                  start=(h == 0), stop=(h == 1))
                else:
                    h = k - 5
                    after(pe, pre_act, c, "low")
                    last = mm(bank_[:, :], dt_proj[0:RANK, h * P:(h + 1) * P], low[0:RANK, q, :], start=True, stop=True)
                last.then_inc(pre_pe.sem, 1)

            def skip_in(c, k):
                if c == 0:
                    after(pe, setup_dve, 0, "skip_diag")
                    after(pe, pre_act, 0, "u1")
                else:
                    after(pe, tail_dve, c - 1, "yg1")
                for h in range(HALVES):
                    last = mm(ps_y[h][:, :], skip_diag[:, h, :], u[:, h, :], start=True, stop=False)
                last.then_inc(skip_pe, 1)

            def finish(c, n):
                g = c * STATE + 2 * n + 1
                if c:
                    pe.wait_ge(pair_pool, (g - STATE) // 2 + 1)
                for step in (g,) if c else (g - 1, g):
                    if c == 0:
                        pe.wait_ge(product_dve, step + 1)
                    for h in range(HALVES):
                        last = mm(ps_y[h][:, :], ident, product[:, step % RING, h, :], start=False,
                                  stop=(step % STATE == STATE - 1))
                last.then_inc(y_pe, 1)

            def tail(c, k):
                q = c % 2
                b, t0 = tokens(c)
                if k == 0:
                    if c:
                        pe.wait_ge(hidden_dve, 2 * NETS * c)
                        pe.wait_ge(gelu_act, 2 * NETS * c)
                    for j in range(BLOCKS):
                        t = TAPS - 1 + t0 + j * P
                        mm(block_of(ps_u[1][:, :], j), x_in[:, b, t:t + P], ident, start=(j == 0), stop=False)
                    after(pe, tail_dve, c, "yg1")
                    for j in range(BLOCKS):
                        for h in range(HALVES):
                            last = mm(block_of(ps_u[1][:, :], j), res_gate[:, q, h, j * P:(j + 1) * P], out_proj[:, h, :],
                                      start=False, stop=(j == BLOCKS - 1 and h == 1))
                    last.then_inc(tail_pe.sem, 1)
                if k == 2:
                    after(pe, tail_act, c, "x1")
                    for j in range(BLOCKS):
                        last = turn(block_of(ps_g[1][:, :], j), x1[:, j, :], ident)
                    last.then_inc(tail_pe.sem, 1)
                if k == 3:
                    after(pe, tail_act, c, "x1q")
                    for j in range(BLOCKS):
                        last = mm(block_of(ps_u[0][:, :], j), x1_q[:, j * P:(j + 1) * P], ffn_q[:, :], start=True, stop=True)
                    last.then_inc(tail_pe.sem, 1)
                if k == 5:
                    after(pe, tail_act, c, "x2")
                    for j in range(BLOCKS):
                        last = turn(block_of(ps_g[0][:, :], j), x2[:, j, :], ident)
                    last.then_inc(tail_pe.sem, 1)
                if k == 6:
                    after(pe, tail_act, c, "x2t")
                    mm(ps_u[0][:, :], par_of("l1_delta"), x2_t[:, :], start=True, stop=True).then_inc(tail_pe.sem, 1)
                    mm(ps_u[1][0:STATE, :], par_of("l1_b"), x2_t[:, :], start=True, stop=True).then_inc(tail_pe.sem, 1)
                if k == 7:
                    after(pe, tail_dve, c, "sp")
                    mm(ps_g[1][0:STATE, :], mean_w[:, :], l1_sp[:, :], start=True, stop=True).then_inc(tail_pe.sem, 1)
                    for j in range(BLOCKS):
                        mm(block_of(ps_g[0][:, :], j), x2_t[:, j * P:(j + 1) * P], l1_diag[:, :], start=(j == 0), stop=False)
                if k == 8:
                    after(pe, tail_dve, c, "scan")
                    for j in range(BLOCKS):
                        last = mm(block_of(ps_g[0][:, :], j), l1_state[:, q, j * P:(j + 1) * P],
                                  par_of("l1_c")[0:STATE, :], start=False, stop=(j == BLOCKS - 1))
                    last.then_inc(tail_pe.sem, 1)
                if k == 11:
                    after(pe, tail_act, c, "hn")
                    for j in range(BLOCKS):
                        last = turn(block_of(ps_u[0][:, :], j), hn[:, j, :], ident)
                    last.then_inc(tail_pe.sem, 1)
                if k == 12:
                    after(pe, tail_act, c, "hnt")
                    for j in range(BLOCKS):
                        last = mm(ps_g[1][:, j * EXPERTS:(j + 1) * EXPERTS], hn_t[:, j * P:(j + 1) * P],
                                  par_of("router"), start=True, stop=True)
                    last.then_inc(tail_pe.sem, 1)
                if k == 14:
                    after(pe, tail_dve, c, "picked")
                    if c:
                        pe.wait_ge(acc_dve, NETS * c)
                    if c + 2 < CHUNKS:
                        after(pe, pre_act, c + 2, "relu0")
                    for j in range(BLOCKS):
                        o = ps_acc[:, j * EXPERTS:(j + 1) * EXPERTS]
                        mm(o, before[:, :], picked[:, j, :], start=True, stop=False)
                        for i in range(j):
                            mm(o, ones[:, :], picked[:, i, :], start=False, stop=False)
                        last = mm(o, ones[:, :], picked_before[:, :], start=False, stop=True)
                    last.then_inc(tail_pe.sem, 1)

            def layer_in(banks, kind, e, f):
                for i, (wp, hp) in enumerate(((0, 0), (0, 1), (1, 0))):
                    last = mm(banks[f][:, :], w_in[kind][wp][:, e, f * P:(f + 1) * P], hn_parts[hp][:, :],
                              start=(i == 0), stop=(i == 2))
                return last

            def gate(c, e):
                m = NETS * c + e
                if e == 0:
                    after(pe, tail_dve, c, "lg")
                    after(pe, tail_act, c, "x3")
                    if c == 0:
                        pe.wait_ge(split_dve, 2 * EXPERTS)
                        after(pe, setup_dve, 0, "side_u")
                        pe.wait_ge(loaded_down, 16)
                if e == EXPERTS:
                    pe.wait_ge(gelu_act, 2 * m)
                    mm(ps_g[0][0:SIDE, :], side_g[:, :], hn_t[:, :], start=True, stop=True).then_inc(gate_pe, 2)
                    return
                for f in range(2):
                    if e:
                        pe.wait_ge(gelu_act, 2 * (m - 1) + f + 1)
                    layer_in(ps_g, "wg", e, f).then_inc(gate_pe, 1)

            def up(c, e):
                m = NETS * c + e
                if e == EXPERTS:
                    pe.wait_ge(hidden_dve, 2 * m)
                    mm(ps_u[0][0:SIDE, :], side_u[:, :], hn_t[:, :], start=True, stop=True).then_inc(up_pe, 2)
                    return
                for f in range(2):
                    if e:
                        pe.wait_ge(hidden_dve, 2 * (m - 1) + f + 1)
                    layer_in(ps_u, "wu", e, f).then_inc(up_pe, 1)

            def down(c, e):
                m = NETS * c + e
                pe.wait_ge(hidden_dve, 2 * m + 2)
                if e == 0:
                    after(pe, tail_dve, c, "late")
                elif c < LAST or e > 1:
                    pe.wait_ge(acc_dve, m - (c == LAST))
                for j in range(BLOCKS):
                    for f in range(2 if e < EXPERTS else 1):
                        if e < EXPERTS:
                            last = mm(block_of(out_bank(c, e)[:, :], j), hidden[:, m % 2, f, j * P:(j + 1) * P], wd[:, e, f, :],
                                      start=(f == 0), stop=(f == 1))
                        else:
                            last = mm(block_of(out_bank(c, e)[:, :], j), hidden[0:SIDE, m % 2, 0, j * P:(j + 1) * P],
                                      par_of("side_d")[0:SIDE, :], start=True, stop=True)
                last.then_inc(down_pe, 1)

            setup()
            run("tensor", pre=pre, skip=skip_in, finish=finish, tail=tail, gate=gate, up=up, down=down)

        @block.scalar
        def _(act):
            def do(marks, out_, in_, func, **kw):
                nc.scalar.activation(out_, in_, func, **kw).then_inc(marks.sem, 1)

            def copy(marks, out_, in_, **kw):
                nc.scalar.copy(out_, in_, **kw).then_inc(marks.sem, 1)

            def setup():
                act.wait_ge(loaded_first, 16)
                act.wait_ge(pool_const, 3)
                do(setup_act, decay_rate[:, :, :], par_of("a_log").rearrange("p (h n) -> p h n", h=HALVES), ACT.Exp)
                act.wait_ge(loaded_rest, 16)
                do(setup_act, l1_rate[:, :], par_of("l1_a_log")[0:STATE, :], ACT.Exp)
                for h in range(HALVES):
                    after(act, setup_pe, 0, f"conv{h}")
                    copy(setup_act, conv_proj[:, h, :, :], ps_y[h][:, :].rearrange("p (k d) -> p k d", k=TAPS))

            def pre(c, k):
                q = c % 2
                if k < 2:
                    after(act, pre_pe, c, f"conv{k}")
                    if c and k == 0:
                        act.wait_ge(du_pool, c)
                        act.wait_ge(skip_pe, c)
                    do(pre_act, u[:, k, :], pre_bank(c, k)[:, :], ACT.Silu, bias=conv_b[:, k:k + 1])
                elif k < 4:
                    after(act, pre_pe, c, f"res{k - 2}")
                    if c >= 2 and k == 2:
                        after(act, tail_pe, c - 2, "r1")
                    do(pre_act, res_gate[:, q, k - 2, :], pre_bank(c, k)[:, :], ACT.Silu)
                    if k == 3:
                        nc.scalar.preload_act_table_set(EXP_LN)
                elif k == 4:
                    after(act, pre_pe, c, "low")
                    if c >= 2:
                        act.wait_ge(rows_out, 16 * (c - 1))
                    copy(pre_act, low[:, q, :], pre_bank(c, k)[0:RANK + 2 * STATE, :])
                elif k < 7:
                    h = k - 5
                    after(act, pre_pe, c, f"dt{h}")
                    if c and h == 0:
                        after(act, pre_dve, c - 1, "delta1")
                    do(pre_act, sp_abs[:, h, :], pre_bank(c, k)[:, :], ACT.Abs, bias=dt_b[:, h:h + 1])
                    do(pre_act, sp_relu[:, h, :], pre_bank(c, k)[:, :], ACT.Relu, bias=dt_b[:, h:h + 1])
                else:
                    for h in range(HALVES):
                        after(act, pre_act, c, f"abs{h}")
                        do(pre_act, sp_exp[:, h, :], sp_abs[:, h, :], ACT.Exp, scale=-1.0)
                    for h in range(HALVES):
                        after(act, pre_act, c, f"exp{h}")
                        do(pre_act, sp_ln[:, h, :], sp_exp[:, h, :], ACT.Ln, bias=1.0)

            def split(c, e):
                for kind, loaded in (("wg", loaded_gate), ("wu", loaded_up)):
                    act.wait_ge(loaded, 16)
                    nc.scalar.mul(w_in[kind][0][:, e, :], w_loaded[kind][:, e, :],
                                  par_of("norm_w")[:, e:e + 1]).then_inc(split_act, 1)

            def step(c, n):
                g = c * STATE + n
                if n == 0:
                    after(act, pre_dve, c, "delta1")
                if g == 0:
                    after(act, setup_dve, 0, "rate")
                old = g - RING
                if old >= STATE and old % 2 == 0:
                    act.wait_ge(pair_pool, (old - STATE) // 2 + 1)
                elif old >= 0:
                    act.wait_ge(y_pe, old // 2 + 1)
                for h in range(HALVES):
                    nc.scalar.activation(decay[:, g % RING, h, :], delta[:, c % 2, h, :], ACT.Exp,
                                         scale=decay_rate[:, h, n:n + 1]).then_inc(decay_act, 1)

            def rsqrt(marks, c, log, log_name, in_, eps_, out_):
                do(marks, log, in_, ACT.Ln, bias=eps_)
                after(act, marks, c, log_name)
                do(marks, out_, log, ACT.Exp, scale=-0.5)

            def normalise(marks, out_, of, scales, shifts):
                for j in range(BLOCKS):
                    last = nc.scalar.activation(out_[:, j, :], of(j), ACT.Identity,
                                                bias=shifts[:, j:j + 1], scale=scales[:, j:j + 1])
                last.then_inc(marks.sem, 1)

            def tail(c, k):
                if k == 1:
                    after(act, tail_dve, c, "mo1")
                    rsqrt(tail_act, c, var_log[:, :], "l1", moments[:, :, 1], eps[:, 0:1], rstd[:, :])
                if k == 2:
                    after(act, tail_dve, c, "sh1")
                    normalise(tail_act, x1, lambda j: block_of(ps_u[1][:, :], j), rstd, shift)
                if k == 3:
                    after(act, tail_pe, c, "x1t")
                    copy(tail_act, x1_q[:, :], ps_g[1][:, :], saturate=False)
                if k == 4:
                    after(act, tail_pe, c, "ffn")
                    copy(tail_act, ffn_out[:, :, :], blocks_of(ps_u[0][:, :]))
                    after(act, tail_dve, c, "mo2")
                    rsqrt(tail_act, c, var_log[:, :], "l2", moments[:, :, 1], eps[:, 0:1], rstd[:, :])
                if k == 5:
                    after(act, tail_dve, c, "sh2")
                    normalise(tail_act, x2, lambda j: r2[:, j, :], rstd, shift)
                if k == 6:
                    after(act, tail_pe, c, "x2t")
                    copy(tail_act, x2_t[:, :], ps_g[0][:, :])
                if k == 7:
                    after(act, tail_pe, c, "dlt")
                    do(tail_act, l1_abs, ps_u[0][:, :], ACT.Abs, bias=par_of("l1_delta_b"))
                    after(act, tail_act, c, "abs")
                    do(tail_act, l1_exp, l1_abs, ACT.Exp, scale=-1.0)
                    do(tail_act, l1_relu, ps_u[0][:, :], ACT.Relu, bias=par_of("l1_delta_b"))
                    after(act, tail_act, c, "exp")
                    do(tail_act, l1_ln, l1_exp, ACT.Ln, bias=1.0)
                if k == 8:
                    after(act, tail_pe, c, "mean")
                    copy(tail_act, l1_step, ps_g[1][0:STATE, :])
                    do(tail_act, l1_decay, ps_g[1][0:STATE, :], ACT.Exp, scale=l1_rate[:, :])
                if k == 9:
                    after(act, tail_dve, c, "mo3")
                    rsqrt(tail_act, c, var_log[:, :], "l3", moments[:, :, 1], eps[:, 0:1], rstd[:, :])
                if k == 10:
                    after(act, tail_dve, c, "msq")
                    rsqrt(tail_act, c, var_log[:, :], "l4", mean_sq[:, :], eps[:, 1:2], rms[:, :])
                if k == 11:
                    after(act, tail_dve, c, "f3")
                    normalise(tail_act, hn, lambda j: block_of(ps_g[0][:, :], j), scale3, shift3)
                if k == 12:
                    after(act, tail_pe, c, "hnt")
                    copy(tail_act, hn_t[:, :], ps_u[0][:, :])
                    copy(tail_act, hn_parts[0][:, :], ps_u[0][:, :])
                    normalise(tail_act, x3, lambda j: block_of(ps_g[0][:, :], j), rstd, shift)
                if k == 13:
                    after(act, tail_dve, c, "cen")
                    do(tail_act, exps[:, :, :], centred[:, :, :], ACT.Exp)
                if k == 15:
                    after(act, tail_dve, c, "xw")
                    if c:
                        after(act, fin_act, c - 1, "result")
                    for j in range(BLOCKS):
                        last = nc.scalar.mul(acc[:, j, :], x3[:, j, :], x_weight[:, j:j + 1])
                    last.then_inc(tail_act.sem, 1)

            def gate(c, e):
                m = NETS * c + e
                rows = P if e < EXPERTS else SIDE
                for f in range(2 if e < EXPERTS else 1):
                    inc = 1 if e < EXPERTS else 2
                    act.wait_ge(gate_pe, 2 * m + f + inc)
                    if m >= GROUP:
                        act.wait_ge(hidden_dve, 2 * (m - GROUP) + 2)
                    nc.scalar.activation(gelu[0:rows, m % GROUP, f, :], ps_g[f][0:rows, :], ACT.Gelu).then_inc(gelu_act, inc)
                if e % GROUP == GROUP - 1 and (c < LAST or e == EXPERTS):
                    nc.scalar.preload_act_table_set(EXP_LN)

            def fin(c, k):
                if k == 0:
                    after(act, fin_dve, c, "mo")
                    rsqrt(fin_act, c, var_log4[:, :], "l", moments4[:, :, 1], eps[:, 0:1], rstd4[:, :])
                if k == 1:
                    after(act, fin_dve, c, "sh")
                    if c:
                        act.wait_ge(stored, 16 * c)
                    normalise(fin_act, result, lambda j: acc[:, j, :], rstd4, shift4)

            setup()
            run("scalar", pre=pre, split=split, step=step, tail=tail, gate=gate, fin=fin)

        @block.gpsimd
        def _(pool):
            nc.gpsimd.memset(eps[:, 0:1], LN_EPS).then_inc(pool_const, 1)
            nc.gpsimd.memset(mean_w[:, :], 1.0 / P).then_inc(pool_const, 1)
            nc.gpsimd.memset(eps[:, 1:2], RMS_EPS).then_inc(pool_const, 1)

            def make_du(c, k):
                after(pool, pre_dve, c, "delta1")
                if c:
                    pool.wait_ge(drive_pool, STATE * c)
                nc.gpsimd.tensor_tensor(du[:, :, :], delta[:, c % 2, :, :], u[:, :, :], ALU.mult).then_inc(du_pool, 1)

            def step(c, n):
                g = c * STATE + n
                if n == 0:
                    pool.wait_ge(du_pool, c + 1)
                pool.wait_ge(b_in[g // 2 % 2], 16 * (g // 4 + 1))
                if g >= RING:
                    pool.wait_ge(product_dve, g - RING + 1)
                    cc, nn = divmod(g - RING, STATE)
                    if cc % PER_BATCH == 0:
                        pool.wait_ge(carry_dve, (cc // PER_BATCH) * STATE + nn + 1)
                nc.gpsimd.tensor_tensor(drive[:, g % RING, :, :], du[:, :, :],
                                        b_row[:, g // 2 % 2, n % 2:n % 2 + 1, :].broadcast_to([P, HALVES, CHUNK]),
                                        ALU.mult).then_inc(drive_pool, 1)

            def pair_up(c, n):
                g = c * STATE + 2 * n + 1
                if c == 0:
                    return
                pool.wait_ge(product_dve, g + 1)
                nc.gpsimd.tensor_tensor(product[:, g % RING, :, :], product[:, g % RING, :, :],
                                        product[:, (g - 1) % RING, :, :], ALU.add).then_inc(pair_pool, 1)

            def tail(c, k):
                if k == 2:
                    after(pool, tail_act, c, "x1")
                    nc.gpsimd.tensor_tensor(x1_bias[:, :, :], x1[:, :, :],
                                            par_of("ffn_b")[:, None, :].broadcast_to([P, BLOCKS, P]),
                                            ALU.add).then_inc(tail_pool.sem, 1)

            run("gpsimd", du=make_du, step=step, pair=pair_up, tail=tail)

        @block.vector
        def _(dve):
            v = nc.vector

            def do(marks, ins):
                ins.then_inc(marks.sem, 1)

            def own(marks, c, name):
                dve.wait_ge(marks.sem, marks.done(c, name))

            def setup():
                dve.wait_ge(loaded_first, 16)
                for h in range(HALVES):
                    for k in range(TAPS):
                        i = h * TAPS + k
                        last = v.tensor_scalar(conv_diag[:, h, k, :], ident, conv_w[:, i:i + 1], None, ALU.mult)
                do(setup_dve, last)
                do(setup_dve, v.memset(x_in[:, :, 0:TAPS - 1], 0.0))
                for h in range(HALVES):
                    last = v.tensor_scalar(skip_diag[:, h, :], ident, skip[:, h:h + 1], None, ALU.mult)
                do(setup_dve, last)
                dve.wait_ge(loaded_rest, 16)
                after(dve, setup_act, 0, "l1_exp")
                v.tensor_scalar(l1_rate[:, :], l1_rate[:, :], -1.0, None, ALU.mult)
                do(setup_dve, v.tensor_scalar(decay_rate[:, :, :], decay_rate[:, :, :], -1.0, None, ALU.mult))
                do(setup_dve, v.memset(ones[:, :], 1.0))
                w = par_of("ffn_w")
                do(setup_dve, v.tensor_scalar(ffn_t[:, :], w, 128.0, -128.0, ALU.min, ALU.max))
                own(setup_dve, 0, "clip")
                do(setup_dve, v.tensor_copy(ffn_small[:, :], ffn_t[:, :], saturate=False))
                do(setup_dve, v.tensor_scalar(ffn_t2[:, :], w, 448.0, -448.0, ALU.min, ALU.max))
                own(setup_dve, 0, "clip_half")
                do(setup_dve, v.tensor_scalar(ffn_half[:, :], ffn_t2[:, :], 0.5, None, ALU.mult, saturate=False))
                own(setup_dve, 0, "half_a")
                do(setup_dve, v.tensor_scalar(ffn_big[:, :], ffn_half[:, :], 2.0, None, ALU.mult))
                do(setup_dve, v.tensor_copy(ffn_t[:, :], ffn_small[:, :]))
                do(setup_dve, v.tensor_tensor(ffn_t3[:, :], ffn_t2[:, :], ffn_t2[:, :], ALU.mult))
                own(setup_dve, 0, "mask")
                do(setup_dve, v.tensor_tensor(ffn_big[:, :], ffn_big[:, :], ffn_t[:, :], ALU.subtract))
                own(setup_dve, 0, "diff")
                do(setup_dve, v.scalar_tensor_tensor(ffn_t3[:, :], ffn_t3[:, :], 4096.0, ffn_big[:, :], ALU.is_ge, ALU.mult))
                own(setup_dve, 0, "mix")
                do(setup_dve, v.tensor_tensor(ffn_q[:, :], ffn_t3[:, :], ffn_t[:, :], ALU.add))
                do(setup_dve, v.tensor_copy(before[:, :], par_of("before")))
                do(setup_dve, v.scalar_tensor_tensor(l1_diag[:, :], ident, par_of("l1_d"), ident, ALU.mult, ALU.add))
                do(setup_dve, v.tensor_scalar(side_g[:, :], par_of("side_g"), par_of("f_norm"), None, ALU.mult))
                do(setup_dve, v.tensor_scalar(side_u[:, :], par_of("side_u"), par_of("f_norm"), None, ALU.mult))
                v.memset(picked_before[:, :], 0.0)
                v.memset(picked_sum[:, :], 0.0)

            def split(c, e):
                norm = par_of("norm_w")[:, e:e + 1]
                for i, (kind, loaded) in enumerate((("wg", loaded_gate), ("wu", loaded_up))):
                    high, low_part = (x[:, e, :] for x in w_in[kind])
                    dve.wait_ge(loaded, 16)
                    dve.wait_ge(split_act, 2 * e + i + 1)
                    v.scalar_tensor_tensor(low_part, w_loaded[kind][:, e, :], norm, high, ALU.mult,
                                           ALU.subtract).then_inc(split_dve, 1)

            def make_delta(c, k):
                q = c % 2
                if c >= 2:
                    dve.wait_ge(decay_act, 2 * STATE * (c - 1))
                for h in range(HALVES):
                    after(dve, pre_act, c, f"exp{h}")
                    do(pre_dve, v.tensor_scalar(delta[:, q, h, :], sp_exp[:, h, :], 1.0, -1.0, ALU.add, ALU.add))
                for h in range(HALVES):
                    own(pre_dve, c, f"t{h}")
                    do(pre_dve, v.tensor_tensor(delta[:, q, h, :], sp_exp[:, h, :], delta[:, q, h, :], ALU.subtract))
                for h in range(HALVES):
                    own(pre_dve, c, f"a{h}")
                    do(pre_dve, v.tensor_tensor(delta[:, q, h, :], delta[:, q, h, :], sp_relu[:, h, :], ALU.add))
                for h in range(HALVES):
                    own(pre_dve, c, f"b{h}")
                    after(dve, pre_act, c, f"ln{h}")
                    do(pre_dve, v.tensor_tensor(delta[:, q, h, :], delta[:, q, h, :], sp_ln[:, h, :], ALU.add))

            def step(c, n):
                g = c * STATE + n
                first = c % PER_BATCH == 0
                dve.wait_ge(drive_pool, g + 1)
                if not first:
                    dve.wait_ge(carry_dve, (c // PER_BATCH) * STATE + n + 1)
                for h in range(HALVES):
                    dve.wait_ge(decay_act, 2 * g + h + 1)
                    v.tensor_tensor_scan(state[:, g % RING, h, :], decay[:, g % RING, h, :], drive[:, g % RING, h, :],
                                         0.0 if first else carry[:, h, n:n + 1], ALU.mult, ALU.add).then_inc(state_dve, 1)

            def finish(c, n):
                g = c * STATE + n
                dve.wait_ge(state_dve, 2 * g + 2)
                dve.wait_ge(c_in[g // 2 % 2], 16 * (g // 4 + 1))
                v.tensor_tensor(product[:, g % RING, :, :], state[:, g % RING, :, :],
                                c_row[:, g // 2 % 2, n % 2:n % 2 + 1, :].broadcast_to([P, HALVES, CHUNK]),
                                ALU.mult).then_inc(product_dve, 1)
                if c % PER_BATCH == 0:
                    v.tensor_copy(carry[:, :, n:n + 1], state[:, g % RING, :, CHUNK - 1:CHUNK]).then_inc(carry_dve, 1)

            def layer_norm_stats(marks, c, of, st, mo):
                for j in range(BLOCKS):
                    last = v.bn_stats(stats[:, j, :], of(j))
                do(marks, last)
                own(marks, c, st)
                for j in range(BLOCKS):
                    last = v.bn_aggr(moments[:, j, :], stats[:, j, :])
                do(marks, last)

            def layer_norm_shift(marks, act_marks, c, r, means, scales, shifts):
                after(dve, act_marks, c, r)
                do(marks, v.scalar_tensor_tensor(shifts[:, :], means, -1.0, scales[:, :], ALU.mult, ALU.mult))

            def each(ap):
                return ap[:, :, None].broadcast_to([P, BLOCKS, EXPERTS])

            def tail(c, k):
                q = c % 2
                if k == 0:
                    dve.wait_ge(y_pe, STATE // 2 * (c + 1))
                    for h in range(HALVES):
                        do(tail_dve, v.tensor_tensor(res_gate[:, q, h, :], res_gate[:, q, h, :], ps_y[h][:, :], ALU.mult))
                if k == 1:
                    after(dve, tail_pe, c, "r1")
                    layer_norm_stats(tail_dve, c, lambda j: block_of(ps_u[1][:, :], j), "st1", "mo1")
                if k == 2:
                    layer_norm_shift(tail_dve, tail_act, c, "rstd1", moments[:, :, 0], rstd, shift)
                if k == 4:
                    after(dve, tail_act, c, "ffn")
                    after(dve, tail_pool, c, "bias")
                    do(tail_dve, v.tensor_tensor(r2[:, :, :], ffn_out[:, :, :], x1_bias[:, :, :], ALU.add))
                    own(tail_dve, c, "r2")
                    layer_norm_stats(tail_dve, c, lambda j: r2[:, j, :], "st2", "mo2")
                if k == 5:
                    layer_norm_shift(tail_dve, tail_act, c, "rstd2", moments[:, :, 0], rstd, shift)
                if k == 7:
                    after(dve, tail_act, c, "exp")
                    do(tail_dve, v.tensor_scalar(l1_t[:, :], l1_exp[:, :], 1.0, -1.0, ALU.add, ALU.add))
                    own(tail_dve, c, "t")
                    do(tail_dve, v.tensor_tensor(l1_t[:, :], l1_exp[:, :], l1_t[:, :], ALU.subtract))
                    own(tail_dve, c, "a")
                    after(dve, tail_act, c, "relu")
                    do(tail_dve, v.tensor_tensor(l1_t[:, :], l1_t[:, :], l1_relu[:, :], ALU.add))
                    own(tail_dve, c, "b")
                    after(dve, tail_act, c, "ln")
                    do(tail_dve, v.tensor_tensor(l1_sp[:, :], l1_t[:, :], l1_ln[:, :], ALU.add))
                if k == 8:
                    after(dve, tail_act, c, "decay")
                    do(tail_dve, v.tensor_tensor(l1_drive[:, :], l1_step[:, :], ps_u[1][0:STATE, :], ALU.mult))
                    own(tail_dve, c, "drive")
                    first = c % PER_BATCH == 0
                    do(tail_dve, v.tensor_tensor_scan(l1_state[:, q, :], l1_decay[:, :], l1_drive[:, :],
                                                      0.0 if first else l1_state[:, 1 - q, CHUNK - 1:CHUNK],
                                                      ALU.mult, ALU.add))
                if k == 9:
                    after(dve, tail_pe, c, "r3")
                    layer_norm_stats(tail_dve, c, lambda j: block_of(ps_g[0][:, :], j), "st3", "mo3")
                if k == 10:
                    after(dve, tail_act, c, "rstd3")
                    do(tail_dve, v.tensor_tensor(mean_sq[:, :], moments[:, :, 1], rstd[:, :], ALU.mult))
                    own(tail_dve, c, "vr")
                    do(tail_dve, v.tensor_tensor(mean_sq[:, :], mean_sq[:, :], rstd[:, :], ALU.mult))
                    do(tail_dve, v.scalar_tensor_tensor(shift[:, :], moments[:, :, 0], -1.0, rstd[:, :], ALU.mult, ALU.mult))
                if k == 11:
                    after(dve, tail_act, c, "rms")
                    own(tail_dve, c, "sh3")
                    do(tail_dve, v.scalar_tensor_tensor(rms_inv[:, :], mean_sq[:, :], RMS_EPS, rms[:, :], ALU.add, ALU.mult))
                    do(tail_dve, v.tensor_tensor(scale3[:, :], rstd[:, :], rms[:, :], ALU.mult))
                    do(tail_dve, v.tensor_tensor(shift3[:, :], shift[:, :], rms[:, :], ALU.mult))
                if k == 12:
                    after(dve, tail_act, c, "hi")
                    do(tail_dve, v.tensor_tensor(hn_parts[1][:, :], ps_u[0][:, :], hn_parts[0][:, :], ALU.subtract))
                if k == 13:
                    after(dve, tail_pe, c, "logits")
                    do(tail_dve, v.tensor_tensor(logits[:, :, :], ps_g[1][:, 0:BLOCKS * EXPERTS].rearrange(
                        "p (j e) -> p j e", j=BLOCKS), each(rms_inv), ALU.mult))
                    own(tail_dve, c, "lg")
                    do(tail_dve, v.tensor_reduce(top[:, :], logits[:, :, :], AX.X, ALU.max))
                    own(tail_dve, c, "top")
                    do(tail_dve, v.tensor_tensor(centred[:, :, :], logits[:, :, :], each(top), ALU.subtract))
                if k == 14:
                    after(dve, tail_act, c, "exps")
                    do(tail_dve, v.tensor_reduce(total[:, :], exps[:, :, :], AX.X, ALU.add))
                    own(tail_dve, c, "tot")
                    do(tail_dve, v.reciprocal(total_inv[:, :], total[:, :]))
                    own(tail_dve, c, "tinv")
                    do(tail_dve, v.tensor_tensor(probs[:, :, :], exps[:, :, :], each(total_inv), ALU.mult))
                    own(tail_dve, c, "probs")
                    for j in range(BLOCKS):
                        last = v.max(sorted8[:, j, :], probs[:, j, :])
                    do(tail_dve, last)
                    own(tail_dve, c, "sort")
                    for j in range(BLOCKS):
                        last = v.max_index(where8[:, j, :], sorted8[:, j, :], probs[:, j, :])
                    do(tail_dve, last)
                    own(tail_dve, c, "where")
                    do(tail_dve, v.tensor_copy(where_f[:, :, :], where8[:, :, :]))
                    own(tail_dve, c, "wf")
                    index = par_of("index")[:, None, :].broadcast_to([P, BLOCKS, EXPERTS])
                    for pick, i in ((pick1, 0), (pick2, 1)):
                        do(tail_dve, v.tensor_tensor(pick[:, :, :], index,
                                                     where_f[:, :, i:i + 1].broadcast_to([P, BLOCKS, EXPERTS]), ALU.is_equal))
                    own(tail_dve, c, "p2")
                    do(tail_dve, v.tensor_tensor(picked[:, :, :], pick1[:, :, :], pick2[:, :, :], ALU.add))
                if k == 15:
                    after(dve, tail_pe, c, "counts")
                    own(tail_dve, c, "picked")
                    counts = ps_acc[:, 0:BLOCKS * EXPERTS].rearrange("p (j e) -> p j e", j=BLOCKS)
                    do(tail_dve, v.scalar_tensor_tensor(late[:, :, :], counts, float(CAPACITY), picked[:, :, :],
                                                        ALU.is_ge, ALU.mult))
                    own(tail_dve, c, "late")
                    do(tail_dve, v.tensor_reduce(overflow, late[:, :, :], AX.X, ALU.max))
                    own(tail_dve, c, "over")
                    do(tail_dve, v.tensor_scalar(kept[:, :], overflow, -1.0, 1.0, ALU.mult, ALU.add))
                    do(tail_dve, v.tensor_tensor(weight0[:, :, :], probs[:, :, :], picked[:, :, :], ALU.mult))
                    own(tail_dve, c, "w0")
                    do(tail_dve, v.tensor_tensor(weight, weight0[:, :, :], each(kept), ALU.mult))
                    own(tail_dve, c, "w")
                    do(tail_dve, v.tensor_reduce(weight_sum[:, :], weight, AX.X, ALU.add))
                    own(tail_dve, c, "wsum")
                    do(tail_dve, v.tensor_scalar(x_weight[:, :], weight_sum[:, :], 2.0, None, ALU.add))
                    do(tail_dve, v.tensor_reduce(picked_new[:, :], picked[:, :, :].rearrange("p j e -> p e j"), AX.X, ALU.add))
                    own(tail_dve, c, "red")
                    do(tail_dve, v.tensor_tensor(picked_sum[:, :], picked_sum[:, :], picked_new[:, :], ALU.add))
                    own(tail_dve, c, "psum")
                    do(tail_dve, v.tensor_copy(picked_before[:, :], picked_sum[:, :]))

            def join(c, e):
                m = NETS * c + e
                rows = P if e < EXPERTS else SIDE
                inc = 1 if e < EXPERTS else 2
                if m >= 2:
                    dve.wait_ge(down_pe, m - 1)
                for f in range(2 if e < EXPERTS else 1):
                    dve.wait_ge(gelu_act, 2 * m + f + inc)
                    dve.wait_ge(up_pe, 2 * m + f + inc)
                    v.tensor_tensor(hidden[0:rows, m % 2, f, :], gelu[0:rows, m % GROUP, f, :], ps_u[f][0:rows, :],
                                    ALU.mult).then_inc(hidden_dve, inc)

            def accum(c, e):
                m = NETS * c + e
                dve.wait_ge(down_pe, m + 1)
                if e:
                    dve.wait_ge(acc_dve, m)
                else:
                    after(dve, tail_act, c, "acc")
                for j in range(BLOCKS):
                    last = v.scalar_tensor_tensor(acc[:, j, :], block_of(out_bank(c, e)[:, :], j), net_weight[:, j, e:e + 1],
                                                  acc[:, j, :], ALU.mult, ALU.add)
                last.then_inc(acc_dve, 1)

            def fin(c, k):
                if k == 0:
                    dve.wait_ge(acc_dve, NETS * (c + 1))
                    for j in range(BLOCKS):
                        last = v.bn_stats(stats4[:, j, :], acc[:, j, :])
                    do(fin_dve, last)
                    own(fin_dve, c, "st")
                    for j in range(BLOCKS):
                        last = v.bn_aggr(moments4[:, j, :], stats4[:, j, :])
                    do(fin_dve, last)
                if k == 1:
                    layer_norm_shift(fin_dve, fin_act, c, "rstd", moments4[:, :, 0], rstd4, shift4)

            setup()
            run("vector", delta=make_delta, split=split, step=step, finish=finish, tail=tail, join=join, accum=accum, fin=fin)


def kernel(**inputs):
    import numpy as np
    import concourse.bacc as bacc
    from concourse.bass_utils import run_bass_kernel_spmd

    a = {k: np.asarray(v) for k, v in inputs.items()}

    def halves(w):
        return w.reshape(HALVES, P, -1).transpose(1, 0, 2).reshape(P, -1)

    def padded(w):
        return np.concatenate([w, np.zeros((P - w.shape[0], w.shape[1]), w.dtype)])

    in_w = a["L0_attn_in_proj_w"]
    columns = {
        "ident": np.eye(P, dtype=np.float32),
        "conv_w": halves(a["L0_attn_conv_w"].reshape(INNER, TAPS)),
        "conv_b": halves(a["L0_attn_conv_b"]),
        "dt_b": halves(a["L0_attn_dt_proj_b"]),
        "a_log": halves(a["L0_attn_A_log"]),
        "skip": halves(a["L0_attn_Dp"]),
        "in_x": halves(in_w[:INNER]),
        "in_res": in_w[INNER:].T,
        "x_proj": halves(a["L0_attn_x_proj_w"].T),
        "dt_proj": padded(a["L0_attn_dt_proj_w"].T),
        "out_proj": halves(a["L0_attn_out_proj_w"].T),
        "ffn_w": a["L0_ffn_weight"].T,
        "ffn_b": np.broadcast_to(a["L0_ffn_bias"], (P, P)),
        "l1_b": a["L1_attn_B"].T,
        "l1_c": padded(a["L1_attn_C"].T),
        "l1_d": a["L1_attn_D"][:, None],
        "l1_delta": a["L1_attn_W_delta"].T,
        "l1_delta_b": a["L1_attn_b_delta"][:, None],
        "l1_a_log": padded(a["L1_attn_A_log"][:, None]),
        "router": a["L1_ffn_Wr"],
        "norm_w": a["L1_ffn_norm_w"].T,
        "f_norm": a["L1_ffn_f_norm"][:, None],
        "side_g": a["L1_ffn_fWg"],
        "side_u": a["L1_ffn_fWu"],
        "side_d": padded(a["L1_ffn_fWd"]),
        "before": np.triu(np.ones((P, P), np.float32), 1),
        "index": np.broadcast_to(np.arange(EXPERTS, dtype=np.float32), (P, EXPERTS)),
    }
    assert list(columns) == list(PARAMS) and all(columns[k].shape == (P, w) for k, w in PARAMS.items())
    arrays = {
        "x_t": np.ascontiguousarray(a["L0_attn_x"].reshape(TOKENS, P).T),
        "params": np.ascontiguousarray(np.concatenate(list(columns.values()), axis=1)),
        "w_gate": np.ascontiguousarray(a["L1_ffn_Wg"].transpose(1, 0, 2)),
        "w_up": np.ascontiguousarray(a["L1_ffn_Wu"].transpose(1, 0, 2)),
        "w_down": np.ascontiguousarray(a["L1_ffn_Wd"].reshape(EXPERTS, 2, P, P).transpose(2, 0, 1, 3)),
    }
    nc = bacc.Bacc("TRN2", target_bir_lowering=False, num_devices=1)
    ins = [nc.dram_tensor(k, w.shape, F32, kind="ExternalInput").ap() for k, w in arrays.items()]
    ins.append(nc.dram_tensor("bc_dram", (2, 2 * STATE, CHUNK), F32, kind="Internal").ap())
    out = nc.dram_tensor("out", (TOKENS, P), F32, kind="ExternalOutput").ap()
    build(nc, *ins, out)
    got = run_bass_kernel_spmd(nc, [arrays], core_ids=[0]).results[0]["out"]
    return got.reshape(BATCH, LENGTH, P)
```
